# Optimizing a Trainium2 kernel written in Bass

```python
import numpy as np
import jax
import jax.numpy as jnp

def _softmax(x, axis=-1):
    return jax.nn.softmax(x, axis=axis)

def _gelu(x):
    return jax.nn.gelu(x, approximate=True)

def _silu(x):
    return jax.nn.silu(x)

def _sigmoid(x):
    return jax.nn.sigmoid(x)

def _layernorm(x, axis=-1, eps=1e-05):
    m = jnp.mean(x, axis=axis, keepdims=True)
    v = jnp.var(x, axis=axis, keepdims=True)
    return (x - m) / jnp.sqrt(v + eps)

def _scatter_add(tgt, idx, src, axis=0):
    return tgt.at[idx].add(src)

def _segment_sum(src, seg, n):
    return jax.ops.segment_sum(src, seg, n)
kernel_name = 'mk_perceiver_d2_seqx_r4_37ab73'

def setup_inputs(seed: int=0):
    np.random.seed(seed)
    _w = jnp.asarray

    def _rec_inputs():
        import jax
        import jax.numpy as jnp
        _rk = jax.random.key(seed)
        x = -0.0002928 + 1 * jax.random.normal(jax.random.fold_in(_rk, 1), (16, 64, 256), jnp.float32)
        _lenS = 64 - jax.random.randint(jax.random.fold_in(_rk, 7), (16,), 0, max(1, 64 // 4) + 1, jnp.int32)
        _lenS2 = 1024 - jax.random.randint(jax.random.fold_in(_rk, 8), (16,), 0, max(1, 1024 // 4) + 1, jnp.int32)
        _ctx_1024P = jax.random.normal(jax.random.fold_in(_rk, 11), (16, 16, 256), jnp.float32)
        _ctx_1024c = jax.random.dirichlet(jax.random.fold_in(_rk, 511), 0.3 * jnp.ones((16,), jnp.float32), (16, 1024))
        _ctx_1024t = jnp.einsum('bsk,bkd->bsd', _ctx_1024c, _ctx_1024P)
        _ctx_1024t = _ctx_1024t * jax.lax.rsqrt(jnp.mean(jnp.square(_ctx_1024t)) + 1e-12) * 0.953939
        ctx_1024 = -1.39393e-06 + 0.999914 * (_ctx_1024t + 0.3 * jax.random.normal(jax.random.fold_in(_rk, 611), (16, 1024, 256), jnp.float32))
        _validS = jnp.arange(64)[None, :] < _lenS[:, None]
        _validS2 = jnp.arange(1024)[None, :] < _lenS2[:, None]
        _causal = jnp.tril(jnp.ones((64, 64), dtype=bool))
        mask_1x1xSxS2_bk0 = jnp.logical_not(jnp.broadcast_to(_validS2[0:1, None, None, :], (1, 1, 64, 1024)))
        return (x, ctx_1024, mask_1x1xSxS2_bk0)
    x, ctx_1024, mask_1x1xSxS2_bk0 = _rec_inputs()

    def _L0_xattn_setup():
        import jax, jax.numpy as jnp
        import numpy as np
        B, S, D, H = (2, 512, 256, 16)
        HD = D // H
        key = jax.random.key(seed)
        ks = jax.random.split(key, 12)
        scale = 1.0 / np.sqrt(D)
        inp = {'query': jax.random.normal(ks[0], (B, S, D), jnp.float32), 'key': jax.random.normal(ks[1], (B, S, D), jnp.float32), 'value': jax.random.normal(ks[2], (B, S, D), jnp.float32), 'mask': jnp.tril(jnp.ones((1, 1, S, S), dtype=bool)), 'Wq': jax.random.normal(ks[3], (D, D), jnp.float32) * scale, 'bq': jax.random.normal(ks[4], (D,), jnp.float32) * scale, 'Wk': jax.random.normal(ks[5], (D, D), jnp.float32) * scale, 'bk': jax.random.normal(ks[6], (D,), jnp.float32) * scale, 'Wv': jax.random.normal(ks[7], (D, D), jnp.float32) * scale, 'bv': jax.random.normal(ks[8], (D,), jnp.float32) * scale, 'Wo': jax.random.normal(ks[9], (D, D), jnp.float32) * scale, 'bo': jax.random.normal(ks[10], (D,), jnp.float32) * scale}
        return inp
    _L0_xattn_all = _L0_xattn_setup()
    _L0_xattn_in = {k: v for k, v in _L0_xattn_all.items() if k in ('Wq', 'bq', 'Wk', 'bk', 'Wv', 'bv', 'Wo', 'bo')}
    del _L0_xattn_all

    def _L0_attn_setup():
        import jax, jax.numpy as jnp
        import numpy as np
        D_MODEL, N_HEADS, D_HEAD = (256, 16, 64)
        QKV = N_HEADS * D_HEAD
        EPS = 1e-05

        def _layernorm(x, gamma, beta):
            mu = jnp.mean(x, axis=-1, keepdims=True)
            var = jnp.mean((x - mu) ** 2, axis=-1, keepdims=True)
            return (x - mu) * jax.lax.rsqrt(var + EPS) * gamma + beta
        key = jax.random.key(seed)
        ks = jax.random.split(key, 5)
        B, T = (1, 512)
        s_in = 1.0 / np.sqrt(D_MODEL)
        s_qkv = 1.0 / np.sqrt(QKV)
        return {'x': jax.random.normal(ks[0], (B, T, D_MODEL), dtype=jnp.float32), 'Wq': jax.random.normal(ks[1], (QKV, D_MODEL), dtype=jnp.float32) * s_in, 'Wk': jax.random.normal(ks[2], (QKV, D_MODEL), dtype=jnp.float32) * s_in, 'Wv': jax.random.normal(ks[3], (QKV, D_MODEL), dtype=jnp.float32) * s_in, 'Wo': jax.random.normal(ks[4], (D_MODEL, QKV), dtype=jnp.float32) * s_qkv, 'q_gamma': jnp.ones((D_HEAD,), dtype=jnp.float32), 'q_beta': jnp.zeros((D_HEAD,), dtype=jnp.float32), 'k_gamma': jnp.ones((D_HEAD,), dtype=jnp.float32), 'k_beta': jnp.zeros((D_HEAD,), dtype=jnp.float32)}
    _L0_attn_all = _L0_attn_setup()
    _L0_attn_in = {k: v for k, v in _L0_attn_all.items() if k in ('Wq', 'Wk', 'Wv', 'Wo', 'q_gamma', 'q_beta', 'k_gamma', 'k_beta')}
    del _L0_attn_all

    def _L0_ffn_setup():
        import jax, jax.numpy as jnp
        import numpy as np
        MAX_VAL = 100.0
        key = jax.random.key(seed)
        k1, k2, k3 = jax.random.split(key, 3)
        B, S, D_IN, D_OUT = (4, 2048, 256, 256)
        x = jax.random.normal(k1, (B, S, D_IN), dtype=jnp.float32)
        weights = jax.random.normal(k2, (D_OUT, D_IN), dtype=jnp.float32)
        scale = jnp.ones((D_OUT,), dtype=jnp.float32)
        bias = jax.random.normal(k3, (D_OUT,), dtype=jnp.float32)
        return {'x': x, 'weights': weights, 'scale': scale, 'bias': bias}
    _L0_ffn_all = _L0_ffn_setup()
    _L0_ffn_in = {k: v for k, v in _L0_ffn_all.items() if k in ('weights', 'scale', 'bias')}
    del _L0_ffn_all

    def _L1_xattn_setup():
        import jax, jax.numpy as jnp
        import numpy as np
        EMBED_DIM = 256
        NUM_HEADS = 16
        HEAD_DIM = EMBED_DIM // NUM_HEADS
        key = jax.random.key(seed)
        ks = jax.random.split(key, 11)
        s = 1.0 / np.sqrt(EMBED_DIM)
        inp = {'query': jax.random.normal(ks[0], (4, 512, EMBED_DIM), jnp.float32), 'key': jax.random.normal(ks[1], (4, 512, EMBED_DIM), jnp.float32), 'value': jax.random.normal(ks[2], (4, 512, EMBED_DIM), jnp.float32), 'Wq': jax.random.uniform(ks[3], (EMBED_DIM, EMBED_DIM), jnp.float32, -s, s), 'bq': jax.random.uniform(ks[4], (EMBED_DIM,), jnp.float32, -s, s), 'Wk': jax.random.uniform(ks[5], (EMBED_DIM, EMBED_DIM), jnp.float32, -s, s), 'bk': jax.random.uniform(ks[6], (EMBED_DIM,), jnp.float32, -s, s), 'Wv': jax.random.uniform(ks[7], (EMBED_DIM, EMBED_DIM), jnp.float32, -s, s), 'bv': jax.random.uniform(ks[8], (EMBED_DIM,), jnp.float32, -s, s), 'Wo': jax.random.uniform(ks[9], (EMBED_DIM, EMBED_DIM), jnp.float32, -s, s), 'bo': jax.random.uniform(ks[10], (EMBED_DIM,), jnp.float32, -s, s)}
        return inp
    _L1_xattn_all = _L1_xattn_setup()
    _L1_xattn_in = {k: v for k, v in _L1_xattn_all.items() if k in ('Wq', 'bq', 'Wk', 'bk', 'Wv', 'bv', 'Wo', 'bo')}
    del _L1_xattn_all

    def _L1_attn_setup():
        import jax, jax.numpy as jnp
        import numpy as np
        B, T, D = (4, 512, 256)
        H, Kd = (4, 64)
        Vd = 128
        KEY_DIM, VAL_DIM = (H * Kd, H * Vd)
        CONV = 4
        EPS = 1e-06
        LN_EPS = 1e-05

        def _layernorm(x, g, b):
            m = jnp.mean(x, -1, keepdims=True)
            v = jnp.mean((x - m) ** 2, -1, keepdims=True)
            return (x - m) * jax.lax.rsqrt(v + LN_EPS) * g + b

        def _rmsnorm(x, w):
            return x * jax.lax.rsqrt(jnp.mean(x * x, -1, keepdims=True) + EPS) * w

        def _l2norm(x):
            return x * jax.lax.rsqrt(jnp.sum(x * x, -1, keepdims=True) + EPS)

        def _causal_conv_silu(x, w):
            t = x.shape[1]
            xp = jnp.pad(x, ((0, 0), (CONV - 1, 0), (0, 0)))
            y = xp[:, 0:t, :] * w[:, 0]
            for i in range(1, CONV):
                y = y + xp[:, i:i + t, :] * w[:, i]
            return jax.nn.silu(y)

        def _gated_delta_rule(q, k, v, g, beta):
            qT = jnp.moveaxis(q, 1, 0)
            kT = jnp.moveaxis(k, 1, 0)
            vT = jnp.moveaxis(v, 1, 0)
            gT = jnp.moveaxis(g, 1, 0)
            bT = jnp.moveaxis(beta, 1, 0)
            S0 = jnp.zeros((q.shape[0], H, Kd, Vd), q.dtype)

            def step(S, inp):
                q_t, k_t, v_t, g_t, b_t = inp
                S = S * jnp.exp(g_t)[..., None, None]
                kv = jnp.einsum('bhk,bhkv->bhv', k_t, S)
                delta = (v_t - kv) * b_t[..., None]
                S = S + k_t[..., :, None] * delta[..., None, :]
                o = jnp.einsum('bhk,bhkv->bhv', q_t, S)
                return (S, o)
            _, o = jax.lax.scan(step, S0, (qT, kT, vT, gT, bT))
            return jnp.moveaxis(o, 0, 1)

        def _forward(x, ln1_g, ln1_b, ln2_g, ln2_b, rms_in_w, Wq, Wk, Wv, conv_q_w, conv_k_w, conv_v_w, Wa, dt_bias, A_log, Wb, Wg, o_norm_w, Wo, W2, b2):
            b, t, _ = x.shape
            h = _layernorm(x, ln1_g, ln1_b)
            h = _rmsnorm(h, rms_in_w)
            q = _causal_conv_silu(h @ Wq, conv_q_w).reshape(b, t, H, Kd)
            k = _causal_conv_silu(h @ Wk, conv_k_w).reshape(b, t, H, Kd)
            v = _causal_conv_silu(h @ Wv, conv_v_w).reshape(b, t, H, Vd)
            q = _l2norm(q) * Kd ** (-0.5)
            k = _l2norm(k)
            g = -jnp.exp(A_log) * jax.nn.softplus(h @ Wa + dt_bias)
            beta = jax.nn.sigmoid(h @ Wb)
            o = _gated_delta_rule(q, k, v, g, beta)
            gate = (h @ Wg).reshape(b, t, H, Vd)
            o = _rmsnorm(o, o_norm_w) * jax.nn.silu(gate)
            enc = o.reshape(b, t, VAL_DIM) @ Wo
            x = x + enc
            h2 = _layernorm(x, ln2_g, ln2_b)
            x_out = jax.nn.gelu(h2 @ W2 + b2, approximate=False) + x
            return x_out
        key = jax.random.key(seed)
        ks = jax.random.split(key, 16)
        r = lambda k, shp, s=0.02: jax.random.normal(k, shp, dtype=jnp.float32) * s
        return {'x': jax.random.normal(ks[0], (B, T, D), dtype=jnp.float32), 'ln1_g': jnp.ones((D,), jnp.float32), 'ln1_b': jnp.zeros((D,), jnp.float32), 'ln2_g': jnp.ones((D,), jnp.float32), 'ln2_b': jnp.zeros((D,), jnp.float32), 'rms_in_w': jnp.ones((D,), jnp.float32), 'Wq': r(ks[1], (D, KEY_DIM)), 'Wk': r(ks[2], (D, KEY_DIM)), 'Wv': r(ks[3], (D, VAL_DIM)), 'conv_q_w': r(ks[4], (KEY_DIM, CONV), 0.3), 'conv_k_w': r(ks[5], (KEY_DIM, CONV), 0.3), 'conv_v_w': r(ks[6], (VAL_DIM, CONV), 0.3), 'Wa': r(ks[7], (D, H)), 'dt_bias': r(ks[8], (H,), 0.5), 'A_log': jnp.log(jax.random.uniform(ks[9], (H,), minval=1.0, maxval=16.0)), 'Wb': r(ks[10], (D, H)), 'Wg': r(ks[11], (D, VAL_DIM)), 'o_norm_w': jnp.ones((Vd,), jnp.float32), 'Wo': r(ks[12], (VAL_DIM, D)), 'W2': r(ks[13], (D, D)), 'b2': jnp.zeros((D,), jnp.float32)}
    _L1_attn_all = _L1_attn_setup()
    _L1_attn_in = {k: v for k, v in _L1_attn_all.items() if k in ('ln1_g', 'ln1_b', 'ln2_g', 'ln2_b', 'rms_in_w', 'Wq', 'Wk', 'Wv', 'conv_q_w', 'conv_k_w', 'conv_v_w', 'Wa', 'dt_bias', 'A_log', 'Wb', 'Wg', 'o_norm_w', 'Wo', 'W2', 'b2')}
    del _L1_attn_all

    def _L1_ffn_setup():
        import jax, jax.numpy as jnp
        import numpy as np
        B, S, D, F, E = (4, 512, 256, 1024, 8)
        key = jax.random.key(seed)
        ks = jax.random.split(key, 7)
        s1 = 1.0 / np.sqrt(D)
        s2 = 1.0 / np.sqrt(F)
        x = jax.random.normal(ks[0], (B, S, D), dtype=jnp.float32)
        W1 = jax.random.uniform(ks[1], (E, D, F), jnp.float32, -s1, s1)
        b1 = jax.random.uniform(ks[2], (E, F), jnp.float32, -s1, s1)
        W2 = jax.random.uniform(ks[3], (E, F, D), jnp.float32, -s2, s2)
        b2 = jax.random.uniform(ks[4], (E, D), jnp.float32, -s2, s2)
        Wr = jax.random.uniform(ks[5], (D, E), jnp.float32, -s1, s1)
        br = jax.random.uniform(ks[6], (E,), jnp.float32, -s1, s1)
        return {'x': x, 'W1': W1, 'b1': b1, 'W2': W2, 'b2': b2, 'Wr': Wr, 'br': br}
    _L1_ffn_all = _L1_ffn_setup()
    _L1_ffn_in = {k: v for k, v in _L1_ffn_all.items() if k in ('W1', 'b1', 'W2', 'b2', 'Wr', 'br')}
    del _L1_ffn_all
    return {'x': x, 'ctx_1024': ctx_1024, 'mask_1x1xSxS2_bk0': mask_1x1xSxS2_bk0, 'L0_xattn_Wq': _L0_xattn_in['Wq'], 'L0_xattn_bq': _L0_xattn_in['bq'], 'L0_xattn_Wk': _L0_xattn_in['Wk'], 'L0_xattn_bk': _L0_xattn_in['bk'], 'L0_xattn_Wv': _L0_xattn_in['Wv'], 'L0_xattn_bv': _L0_xattn_in['bv'], 'L0_xattn_Wo': _L0_xattn_in['Wo'], 'L0_xattn_bo': _L0_xattn_in['bo'], 'L0_attn_Wq': _L0_attn_in['Wq'], 'L0_attn_Wk': _L0_attn_in['Wk'], 'L0_attn_Wv': _L0_attn_in['Wv'], 'L0_attn_Wo': _L0_attn_in['Wo'], 'L0_attn_q_gamma': _L0_attn_in['q_gamma'], 'L0_attn_q_beta': _L0_attn_in['q_beta'], 'L0_attn_k_gamma': _L0_attn_in['k_gamma'], 'L0_attn_k_beta': _L0_attn_in['k_beta'], 'L0_ffn_weights': _L0_ffn_in['weights'], 'L0_ffn_scale': _L0_ffn_in['scale'], 'L0_ffn_bias': _L0_ffn_in['bias'], 'L1_xattn_Wq': _L1_xattn_in['Wq'], 'L1_xattn_bq': _L1_xattn_in['bq'], 'L1_xattn_Wk': _L1_xattn_in['Wk'], 'L1_xattn_bk': _L1_xattn_in['bk'], 'L1_xattn_Wv': _L1_xattn_in['Wv'], 'L1_xattn_bv': _L1_xattn_in['bv'], 'L1_xattn_Wo': _L1_xattn_in['Wo'], 'L1_xattn_bo': _L1_xattn_in['bo'], 'L1_attn_ln1_g': _L1_attn_in['ln1_g'], 'L1_attn_ln1_b': _L1_attn_in['ln1_b'], 'L1_attn_ln2_g': _L1_attn_in['ln2_g'], 'L1_attn_ln2_b': _L1_attn_in['ln2_b'], 'L1_attn_rms_in_w': _L1_attn_in['rms_in_w'], 'L1_attn_Wq': _L1_attn_in['Wq'], 'L1_attn_Wk': _L1_attn_in['Wk'], 'L1_attn_Wv': _L1_attn_in['Wv'], 'L1_attn_conv_q_w': _L1_attn_in['conv_q_w'], 'L1_attn_conv_k_w': _L1_attn_in['conv_k_w'], 'L1_attn_conv_v_w': _L1_attn_in['conv_v_w'], 'L1_attn_Wa': _L1_attn_in['Wa'], 'L1_attn_dt_bias': _L1_attn_in['dt_bias'], 'L1_attn_A_log': _L1_attn_in['A_log'], 'L1_attn_Wb': _L1_attn_in['Wb'], 'L1_attn_Wg': _L1_attn_in['Wg'], 'L1_attn_o_norm_w': _L1_attn_in['o_norm_w'], 'L1_attn_Wo': _L1_attn_in['Wo'], 'L1_attn_W2': _L1_attn_in['W2'], 'L1_attn_b2': _L1_attn_in['b2'], 'L1_ffn_W1': _L1_ffn_in['W1'], 'L1_ffn_b1': _L1_ffn_in['b1'], 'L1_ffn_W2': _L1_ffn_in['W2'], 'L1_ffn_b2': _L1_ffn_in['b2'], 'L1_ffn_Wr': _L1_ffn_in['Wr'], 'L1_ffn_br': _L1_ffn_in['br']}

def reference(x, ctx_1024, mask_1x1xSxS2_bk0, L0_xattn_Wq, L0_xattn_bq, L0_xattn_Wk, L0_xattn_bk, L0_xattn_Wv, L0_xattn_bv, L0_xattn_Wo, L0_xattn_bo, L0_attn_Wq, L0_attn_Wk, L0_attn_Wv, L0_attn_Wo, L0_attn_q_gamma, L0_attn_q_beta, L0_attn_k_gamma, L0_attn_k_beta, L0_ffn_weights, L0_ffn_scale, L0_ffn_bias, L1_xattn_Wq, L1_xattn_bq, L1_xattn_Wk, L1_xattn_bk, L1_xattn_Wv, L1_xattn_bv, L1_xattn_Wo, L1_xattn_bo, L1_attn_ln1_g, L1_attn_ln1_b, L1_attn_ln2_g, L1_attn_ln2_b, L1_attn_rms_in_w, L1_attn_Wq, L1_attn_Wk, L1_attn_Wv, L1_attn_conv_q_w, L1_attn_conv_k_w, L1_attn_conv_v_w, L1_attn_Wa, L1_attn_dt_bias, L1_attn_A_log, L1_attn_Wb, L1_attn_Wg, L1_attn_o_norm_w, L1_attn_Wo, L1_attn_W2, L1_attn_b2, L1_ffn_W1, L1_ffn_b1, L1_ffn_W2, L1_ffn_b2, L1_ffn_Wr, L1_ffn_br):
    import jax
    import jax.numpy as jnp

    def _L0_xattn_ref(query, key, value, mask, Wq, bq, Wk, bk, Wv, bv, Wo, bo):
        import jax, jax.numpy as jnp
        import numpy as np
        B, S, D, H = (2, 512, 256, 16)
        HD = D // H
        b = query.shape[0]
        q = (query @ Wq + bq).reshape(b, -1, H, HD).transpose(0, 2, 1, 3)
        k = (key @ Wk + bk).reshape(b, -1, H, HD).transpose(0, 2, 1, 3)
        v = (value @ Wv + bv).reshape(b, -1, H, HD).transpose(0, 2, 1, 3)
        scores = jnp.einsum('bhqd,bhkd->bhqk', q, k) / jnp.sqrt(jnp.float32(HD))
        scores = jnp.where(mask, scores, jnp.float32(-1000000000.0))
        attn = jax.nn.softmax(scores, axis=-1)
        ctx = jnp.einsum('bhqk,bhkd->bhqd', attn, v)
        concat = ctx.transpose(0, 2, 1, 3).reshape(b, -1, D)
        return concat @ Wo + bo

    def _L0_attn_ref(x, Wq, Wk, Wv, Wo, q_gamma, q_beta, k_gamma, k_beta):
        import jax, jax.numpy as jnp
        import numpy as np
        D_MODEL, N_HEADS, D_HEAD = (256, 16, 64)
        QKV = N_HEADS * D_HEAD
        EPS = 1e-05

        def _layernorm(x, gamma, beta):
            mu = jnp.mean(x, axis=-1, keepdims=True)
            var = jnp.mean((x - mu) ** 2, axis=-1, keepdims=True)
            return (x - mu) * jax.lax.rsqrt(var + EPS) * gamma + beta
        B, T, _ = x.shape

        def split_heads(y):
            return y.reshape(B, T, N_HEADS, D_HEAD).transpose(0, 2, 1, 3)
        q = split_heads(x @ Wq.T)
        k = split_heads(x @ Wk.T)
        v = split_heads(x @ Wv.T)
        q = _layernorm(q, q_gamma, q_beta)
        k = _layernorm(k, k_gamma, k_beta)
        kv = k[..., :, None] * v[..., None, :]
        S = jnp.cumsum(kv, axis=2)
        o = jnp.einsum('bhtd,bhtde->bhte', q, S)
        o = o.transpose(0, 2, 1, 3).reshape(B, T, QKV)
        return o @ Wo.T

    def _L0_ffn_ref(x, weights, scale, bias):
        import jax, jax.numpy as jnp
        import numpy as np
        MAX_VAL = 100.0
        w = (weights >= 0.0).astype(x.dtype) * 2.0 - 1.0
        y = jnp.einsum('bsi,oi->bso', x, w)
        y = y * scale + bias
        y = jnp.clip(y, -MAX_VAL, MAX_VAL)
        return y

    def _L1_xattn_ref(query, key, value, Wq, bq, Wk, bk, Wv, bv, Wo, bo):
        import jax, jax.numpy as jnp
        import numpy as np
        EMBED_DIM = 256
        NUM_HEADS = 16
        HEAD_DIM = EMBED_DIM // NUM_HEADS
        B, T, E = query.shape
        S = key.shape[1]
        H, D = (NUM_HEADS, HEAD_DIM)
        q = (query @ Wq.T + bq).reshape(B, T, H, D).transpose(0, 2, 1, 3)
        k = (key @ Wk.T + bk).reshape(B, S, H, D).transpose(0, 2, 1, 3)
        v = (value @ Wv.T + bv).reshape(B, S, H, D).transpose(0, 2, 1, 3)
        scores = jnp.einsum('bhtd,bhsd->bhts', q, k) / np.sqrt(D)
        causal = jnp.triu(jnp.full((T, S), -jnp.inf, jnp.float32), k=1)
        scores = scores + causal[None, None]
        attn = jax.nn.softmax(scores, axis=-1)
        out = jnp.einsum('bhts,bhsd->bhtd', attn, v)
        out = out.transpose(0, 2, 1, 3).reshape(B, T, E)
        out = out @ Wo.T + bo
        return out

    def _L1_attn_ref(x, ln1_g, ln1_b, ln2_g, ln2_b, rms_in_w, Wq, Wk, Wv, conv_q_w, conv_k_w, conv_v_w, Wa, dt_bias, A_log, Wb, Wg, o_norm_w, Wo, W2, b2):
        import jax, jax.numpy as jnp
        import numpy as np
        B, T, D = (4, 512, 256)
        H, Kd = (4, 64)
        Vd = 128
        KEY_DIM, VAL_DIM = (H * Kd, H * Vd)
        CONV = 4
        EPS = 1e-06
        LN_EPS = 1e-05

        def _layernorm(x, g, b):
            m = jnp.mean(x, -1, keepdims=True)
            v = jnp.mean((x - m) ** 2, -1, keepdims=True)
            return (x - m) * jax.lax.rsqrt(v + LN_EPS) * g + b

        def _rmsnorm(x, w):
            return x * jax.lax.rsqrt(jnp.mean(x * x, -1, keepdims=True) + EPS) * w

        def _l2norm(x):
            return x * jax.lax.rsqrt(jnp.sum(x * x, -1, keepdims=True) + EPS)

        def _causal_conv_silu(x, w):
            t = x.shape[1]
            xp = jnp.pad(x, ((0, 0), (CONV - 1, 0), (0, 0)))
            y = xp[:, 0:t, :] * w[:, 0]
            for i in range(1, CONV):
                y = y + xp[:, i:i + t, :] * w[:, i]
            return jax.nn.silu(y)

        def _gated_delta_rule(q, k, v, g, beta):
            qT = jnp.moveaxis(q, 1, 0)
            kT = jnp.moveaxis(k, 1, 0)
            vT = jnp.moveaxis(v, 1, 0)
            gT = jnp.moveaxis(g, 1, 0)
            bT = jnp.moveaxis(beta, 1, 0)
            S0 = jnp.zeros((q.shape[0], H, Kd, Vd), q.dtype)

            def step(S, inp):
                q_t, k_t, v_t, g_t, b_t = inp
                S = S * jnp.exp(g_t)[..., None, None]
                kv = jnp.einsum('bhk,bhkv->bhv', k_t, S)
                delta = (v_t - kv) * b_t[..., None]
                S = S + k_t[..., :, None] * delta[..., None, :]
                o = jnp.einsum('bhk,bhkv->bhv', q_t, S)
                return (S, o)
            _, o = jax.lax.scan(step, S0, (qT, kT, vT, gT, bT))
            return jnp.moveaxis(o, 0, 1)

        def _forward(x, ln1_g, ln1_b, ln2_g, ln2_b, rms_in_w, Wq, Wk, Wv, conv_q_w, conv_k_w, conv_v_w, Wa, dt_bias, A_log, Wb, Wg, o_norm_w, Wo, W2, b2):
            b, t, _ = x.shape
            h = _layernorm(x, ln1_g, ln1_b)
            h = _rmsnorm(h, rms_in_w)
            q = _causal_conv_silu(h @ Wq, conv_q_w).reshape(b, t, H, Kd)
            k = _causal_conv_silu(h @ Wk, conv_k_w).reshape(b, t, H, Kd)
            v = _causal_conv_silu(h @ Wv, conv_v_w).reshape(b, t, H, Vd)
            q = _l2norm(q) * Kd ** (-0.5)
            k = _l2norm(k)
            g = -jnp.exp(A_log) * jax.nn.softplus(h @ Wa + dt_bias)
            beta = jax.nn.sigmoid(h @ Wb)
            o = _gated_delta_rule(q, k, v, g, beta)
            gate = (h @ Wg).reshape(b, t, H, Vd)
            o = _rmsnorm(o, o_norm_w) * jax.nn.silu(gate)
            enc = o.reshape(b, t, VAL_DIM) @ Wo
            x = x + enc
            h2 = _layernorm(x, ln2_g, ln2_b)
            x_out = jax.nn.gelu(h2 @ W2 + b2, approximate=False) + x
            return x_out
        return _forward(x, ln1_g, ln1_b, ln2_g, ln2_b, rms_in_w, Wq, Wk, Wv, conv_q_w, conv_k_w, conv_v_w, Wa, dt_bias, A_log, Wb, Wg, o_norm_w, Wo, W2, b2)

    def _L1_ffn_ref(x, W1, b1, W2, b2, Wr, br):
        import jax, jax.numpy as jnp
        import numpy as np
        B, S, D, F, E = (4, 512, 256, 1024, 8)
        b, s, d = x.shape
        e = Wr.shape[1]
        logits = x @ Wr + br
        idx = jnp.argmax(logits, axis=-1)
        probs = jax.nn.softmax(logits, axis=-1)
        gates = jnp.take_along_axis(probs, idx[..., None], axis=-1)[..., 0]
        xf = x.reshape(-1, d)
        idxf = idx.reshape(-1)
        gf = gates.reshape(-1)
        out = jnp.zeros_like(xf)
        for ei in range(e):
            h = jax.nn.gelu(xf @ W1[ei] + b1[ei], approximate=False)
            y = h @ W2[ei] + b2[ei]
            mask = (idxf == ei).astype(xf.dtype)
            out = out + y * (gf * mask)[:, None]
        return out.reshape(b, s, d)
    x = x + _L0_xattn_ref(_layernorm(x, axis=-1), ctx_1024, ctx_1024, mask_1x1xSxS2_bk0, L0_xattn_Wq, L0_xattn_bq, L0_xattn_Wk, L0_xattn_bk, L0_xattn_Wv, L0_xattn_bv, L0_xattn_Wo, L0_xattn_bo)
    x = x + _L0_attn_ref(_layernorm(x, axis=-1), L0_attn_Wq, L0_attn_Wk, L0_attn_Wv, L0_attn_Wo, L0_attn_q_gamma, L0_attn_q_beta, L0_attn_k_gamma, L0_attn_k_beta)
    x = x + _L0_ffn_ref(_layernorm(x, axis=-1), L0_ffn_weights, L0_ffn_scale, L0_ffn_bias)
    x = x + _L1_xattn_ref(_layernorm(x, axis=-1), ctx_1024, ctx_1024, L1_xattn_Wq, L1_xattn_bq, L1_xattn_Wk, L1_xattn_bk, L1_xattn_Wv, L1_xattn_bv, L1_xattn_Wo, L1_xattn_bo)
    x = x + _L1_attn_ref(_layernorm(x, axis=-1), L1_attn_ln1_g, L1_attn_ln1_b, L1_attn_ln2_g, L1_attn_ln2_b, L1_attn_rms_in_w, L1_attn_Wq, L1_attn_Wk, L1_attn_Wv, L1_attn_conv_q_w, L1_attn_conv_k_w, L1_attn_conv_v_w, L1_attn_Wa, L1_attn_dt_bias, L1_attn_A_log, L1_attn_Wb, L1_attn_Wg, L1_attn_o_norm_w, L1_attn_Wo, L1_attn_W2, L1_attn_b2)
    x = x + _L1_ffn_ref(_layernorm(x, axis=-1), L1_ffn_W1, L1_ffn_b1, L1_ffn_W2, L1_ffn_b2, L1_ffn_Wr, L1_ffn_br)
    return x

_drawn_inputs = setup_inputs


def setup_inputs(seed=0):
    import zlib

    import numpy as np

    out = dict(_drawn_inputs(seed))
    spreads = {'L0_attn_q_gamma': (1.0, 0.2),
     'L0_attn_q_beta': (0.0, 0.1),
     'L0_attn_k_gamma': (1.0, 0.2),
     'L0_attn_k_beta': (0.0, 0.1),
     'L0_ffn_scale': (1.0, 0.2),
     'L1_attn_ln1_g': (1.0, 0.6),
     'L1_attn_ln1_b': (0.0, 0.8),
     'L1_attn_ln2_g': (1.0, 0.6),
     'L1_attn_ln2_b': (0.0, 2.0),
     'L1_attn_rms_in_w': (1.0, 0.6),
     'L1_attn_o_norm_w': (1.0, 0.6),
     'L1_attn_b2': (0.0, 2.0)}
    factors = {'L0_xattn_bk': 64.0,
     'L0_ffn_bias': 4.968,
     'L1_xattn_Wq': 8.0,
     'L1_xattn_bq': 8.0,
     'L1_xattn_Wk': 8.0,
     'L1_xattn_bk': 64.0,
     'L1_xattn_Wv': 8.0,
     'L1_xattn_bv': 23.787,
     'L1_xattn_Wo': 8.0,
     'L1_xattn_bo': 64.0,
     'L1_attn_Wq': 44.961,
     'L1_attn_Wk': 45.876,
     'L1_attn_Wv': 8.0,
     'L1_attn_conv_q_w': 43.37,
     'L1_attn_conv_k_w': 42.621,
     'L1_attn_conv_v_w': 8.0,
     'L1_attn_Wa': 23.466,
     'L1_attn_dt_bias': 8.0,
     'L1_attn_A_log': 22.071,
     'L1_attn_Wb': 8.0,
     'L1_attn_Wg': 8.0,
     'L1_attn_Wo': 8.0,
     'L1_attn_W2': 8.0,
     'L1_ffn_W1': 8.0,
     'L1_ffn_b1': 55.95,
     'L1_ffn_W2': 8.0,
     'L1_ffn_b2': 64.0,
     'L1_ffn_Wr': 8.0,
     'L1_ffn_br': 8.0}
    for name, (base, spread) in spreads.items():
        noise = np.random.default_rng([zlib.crc32(name.encode()), seed]).standard_normal(out[name].shape)
        drawn = base * np.exp(spread * noise) if base else spread * noise
        out[name] = jnp.asarray(drawn.astype(out[name].dtype))
    for name, factor in factors.items():
        out[name] = (out[name] * factor).astype(out[name].dtype)
    return out
```

```python
import concourse.bass as bass
from concourse import mybir
from contextlib import ExitStack, contextmanager
import numpy as np

F32 = mybir.dt.float32
BF16 = mybir.dt.bfloat16
U8 = mybir.dt.uint8
U32 = mybir.dt.uint32
ALU = mybir.AluOpType
ACT = mybir.ActivationFunctionType
AXX = mybir.AxisListType.X

P = 128
B, S, D = 16, 64, 256
SK = 1024
N = B * S
NT = N // P
KC = D // P
H, HD = 16, 16
KR = 256
HA, DA = 16, 64
QKV = HA * DA
HG, KD, VD = 4, 64, 128
E, F = 8, 1024
BIG = 1.0e9

COLS, ROWS = {}, {}


def _layout():
    at = 0
    for name, n in (("a_bq", 2), ("a_bk", 2), ("a_bv", 2), ("b_qg", 1), ("b_qb", 1), ("b_kg", 1), ("b_kb", 1),
                    ("d_bq", 2), ("d_bk", 2), ("d_bv", 2), ("e_g2", 2), ("e_b2", 2),
                    ("e_cw", 32), ("f_b1", 64)):
        COLS[name] = (at, n)
        at += n
    COLS["_"] = (at, 0)
    at = 0
    for name, n in (("a_bo", 256), ("c_scale", 256), ("c_bias", 256), ("d_bo", 256), ("e_g1", 256), ("e_b1", 256),
                    ("e_rms", 256), ("e_w2b", 256), ("e_on", 128), ("e_dt", 4), ("e_alog", 4), ("f_b2", 2048),
                    ("f_br", 8)):
        ROWS[name] = (at, n)
        at += n
    ROWS["_"] = (at, 0)


class Names:
    pass


_layout()
NCOLS, NROWS = COLS["_"][0], ROWS["_"][0]


@contextmanager
def stage_semaphores(nc):
    with ExitStack() as ctx:
        taken = []
        ctx.taken = taken
        yield ctx
    nc.clear_and_free_semaphores(taken)
    nc.all_engine_barrier()


def stage_semaphore(nc, ctx, name):
    ctx.taken.append(nc.alloc_semaphore(name))
    return ctx.taken[-1]


def ln_sems(sem, tag):
    s = Names()
    s.stats, s.mv, s.veps, s.std, s.rstd, s.xn, s.tp, s.xt = (
        sem(f"{tag}_{n}") for n in ("stats", "meanvar", "vareps", "std", "rstd", "normed", "transposed", "xt"))
    return s


def ln_vector(dve, c, s, src, dst, w):
    for t in range(NT):
        dve.bn_stats(w.st[:, t, :], src[:, t, :]).then_inc(s.stats, 1)
    dve.wait_ge(s.stats, NT)
    for t in range(NT):
        dve.bn_aggr(w.mv[:, t, :], w.st[:, t, :]).then_inc(s.mv, 1)
    dve.wait_ge(s.mv, NT)
    dve.tensor_scalar(w.ve[:, :], w.mv[:, :, 1], 1e-5, None, ALU.add).then_inc(s.veps, 1)
    dve.wait_ge(s.std, 1)
    dve.reciprocal(w.rs[:, :], w.sd[:, :]).then_inc(s.rstd, 1)
    dve.wait_ge(s.rstd, 1)
    for t in range(NT):
        dve.tensor_scalar(dst[:, t, :], src[:, t, :], w.mv[:, t, 0:1], w.rs[:, t:t + 1],
                          ALU.subtract, ALU.mult).then_inc(s.xn, 1)


def ln_scalar(act, s, w):
    act.wait_ge(s.veps, 1)
    act.activation(w.sd[:, :], w.ve[:, :], ACT.Sqrt).then_inc(s.std, 1)


def xt_tensor(pe, c, s, src, banks, ready):
    for g in range(2):
        for k in range(KC):
            for t in range(4 * g, 4 * g + 4):
                if k == 0 and ready is not None:
                    pe.wait_ge(ready, t + 1)
                pe.transpose(banks[2 * g + k][:, (t - 4 * g) * P:(t - 4 * g + 1) * P],
                             src[:, t, k * P:(k + 1) * P], c.ident[:, :]).then_inc(s.tp, 1)


def xt_scalar(act, s, banks, xt, scale=None, bias=None):
    for g in range(2):
        for k in range(KC):
            act.wait_ge(s.tp, 4 * (2 * g + k + 1))
            kw = {} if scale is None else dict(scale=scale[:, k:k + 1], bias=bias[:, k:k + 1])
            act.activation(xt[:, k, g * 512:(g + 1) * 512], banks[2 * g + k][:, :],
                           ACT.Copy if scale is None else ACT.Identity, **kw).then_inc(s.xt, 1)


def stage_a(nc, c):
    with stage_semaphores(nc) as ctx:
        def sb(name, shape, dt=F32):
            return ctx.enter_context(nc.sbuf_tensor("a_" + name, shape, dt))

        def pb(name):
            return ctx.enter_context(nc.psum_tensor("a_" + name, [P, 512], F32))

        def sem(name):
            return stage_semaphore(nc, ctx, "a_" + name)

        w = c.w
        xn = sb("xn", [P, NT, D])
        xt = sb("xt", [P, KC, N])
        wq, wk, wv, wo = (sb(n, [P, KC, D]) for n in ("wq", "wk", "wv", "wo"))
        mask32 = sb("mask32", [P, SK // 4], U32)
        maskf = sb("maskf", [P, SK])
        madd = sb("madd", [P, SK], BF16)
        anyk = sb("anyk", [P, 1])
        anyb = sb("anyb", [P, P])
        seen = sb("seen", [P, SK // KR + 1])
        ones = sb("ones", [P, 1])
        count = sb("count", [1, SK // KR + 1])
        act_r = sb("act_r", [1, SK // KR])
        ends = sb("ends", [1, 2, SK // KR])
        lohi = sb("lohi", [1, 2])
        rng = sb("rng", [1, 2], mybir.dt.int32)
        ri = sb("ri", [1, 2 * (SK // KR)])
        actq = sb("actq", [P, S])
        q = sb("q", [P, KC, N])
        q2 = sb("q2", [P, KC, N])
        qbd = sb("qbd", [P, KC, B, P])
        ct = sb("ct", [P, 2, KC, KR])
        qw = sb("qw", [P, 2, KC, P])
        ks = sb("ks", [P, 2, KC, KR])
        vs = sb("vs", [P, 2, 2, D])
        pr = sb("pr", [P, 2, 4, KC, KR])
        pt = sb("pt", [P, 4, 512])
        nm_step = sb("nm_step", [P, 2, 4, KC])
        negmx = sb("negmx", [P, 2, 4, KC])
        diff = sb("diff", [P, 2, 8])
        alpha = sb("alpha", [P, 2, 8])
        rsum = sb("rsum", [P, 2, 4, KC])
        nm = sb("nm", [P, B, 8])
        lsum = sb("lsum", [P, B, 8])
        linv = sb("linv", [P, B, 8])
        o = sb("o", [P, B, 4, KC, 32])
        on = sb("on", [P, 4, KC, 4, 32])
        tmp = sb("tmp", [P, 2, 4, S])
        ot = sb("ot", [P, KC, B, S])
        bank = [pb(f"bank{i}") for i in range(8)]
        s_bank, t_bank, k_bank, v_bank, o_bank = bank[0:4], bank[4], bank[5], bank[6], bank[7]

        ln = ln_sems(sem, "ln")
        (s_w, s_mask, s_x) = (sem(n) for n in ("weights", "mask", "x"))
        s_ct = [sem("ctx0"), sem("ctx1")]
        names = ("maskf seen ones counts count act_r ends lohi span anyk madd anyb actp actq init qproj qbias qact qbd0 qbd1 kproj kevac vproj vevac qw "
                 "scores negmx nm probs diff nmkept alpha lscaled lsummed transposed pt pv oscaled osummed "
                 "linv onorm otp otmp ot oproj xout xbo")
        z = {n: sem(n) for n in names.split()}
        NR = SK // KR
        block = ctx.enter_context(nc.Block())

        def span(eng):
            eng.wait_ge(z["span"], 2)
            return (eng.value_load(rng[0:1, 0:1], min_val=0, max_val=NR - 1),
                    eng.value_load(rng[0:1, 1:2], min_val=0, max_val=NR - 1))

        def pairs(eng, body, more):
            body(0, 0, True, False)
            body(1, 1, False, False)
            with eng.Fori(1, more * (B // 2) + (B // 2 - 1)) as i:
                body(2 * i, 0, False, False)
                body(2 * i + 1, 1, False, False)
            body(more * B + (B - 2), 0, False, False)
            body(more * B + (B - 1), 1, False, True)

        @block.sync
        def _(sp):
            sp.dma_start(c.x[:, :, :], c.d["x"].rearrange("(t p) d -> p t d", p=P)).then_inc(s_x, 16)
            sp.dma_start(c.ident[:, :], c.d["ident"]).then_inc(s_w, 16)
            sp.dma_start(c.identb[:, :], c.d["identb"]).then_inc(s_w, 16)
            sp.dma_start(c.eo[:, :], c.d["evenodd"]).then_inc(s_w, 16)
            sp.dma_start(c.cols[:, :], c.d["cols"]).then_inc(s_w, 16)
            for t, n in ((wq, "a_wq"), (wk, "a_wk"), (wv, "a_wv"), (wo, "a_wo")):
                sp.dma_start(t[:, :, :], c.d[n].rearrange("(k p) n -> p k n", p=P)).then_inc(s_w, 16)
            sp.dma_start(c.rows[:, :], c.d["rows"].partition_broadcast(P)).then_inc(s_w, 16)

            r0, more = span(sp)

            def load(s, p, first, last):
                if not (first or (isinstance(s, int) and s < 2)):
                    sp.wait_ge(z["vproj"], s - 1)
                b, r = s % B, (r0 + s // B).with_bounds(min_val=0, max_val=NR - 1)
                sp.dma_start(ct[:, p, :, :], c.d["ctxt"][bass.ds(b, 1), :, bass.ds(r * KR, KR)]
                             .rearrange("b (k p) n -> p (b k) n", p=P)).then_inc(s_ct[p], 16)
            pairs(sp, load, more)

        @block.gpsimd
        def _(pool):
            pool.dma_start(mask32[:, :], c.d["mask2"]).then_inc(s_mask, 16)
            pool.dma_start(ri[:, :], c.d["rounds"]).then_inc(s_mask, 16)
            pool.memset(o[:, :, :, :, :], 0.0).then_inc(z["init"], 1)
            pool.memset(lsum[:, :, :], 0.0).then_inc(z["init"], 1)
            pool.memset(nm[:, :, :], 3.0e38).then_inc(z["init"], 1)
            pool.wait_ge(z["qbd0"], 4)
            pool.wait_ge(z["qbd1"], 4)

            def take(s, p, first, last):
                if not (isinstance(s, int) and s < 2):
                    pool.wait_ge(z["scores"], 4 * s - 4)
                    pool.nop(nofuse=True)
                pool.tensor_copy(qw[:, p, :, :], qbd[:, :, bass.ds(s % B, 1), :].rearrange("p k b n -> p k (b n)")
                                 ).then_inc(z["qw"], 1)
            pairs(pool, take, span(pool)[1])

        @block.scalar
        def _(act):
            ln_scalar(act, ln, w)
            xt_scalar(act, ln, bank, xt)
            for i in range(4):
                k, g = i // 2, i % 2
                act.wait_ge(z["qact"], i + 1)
                src = q2[:, k, g * 512:(g + 1) * 512].rearrange("p (b s) -> p b s", s=S)
                act.activation(qbd[:, k, 8 * g:8 * g + 8, 0:S], src, ACT.Copy, scale=c.eo[:, 0:1]).then_inc(z["qbd0"], 1)
                act.activation(qbd[:, k, 8 * g:8 * g + 8, S:P], src, ACT.Copy, scale=c.eo[:, 1:2]).then_inc(z["qbd1"], 1)

            def keys_out(s, p):
                act.wait_ge(z["kproj"], s + 1)
                if not (isinstance(s, int) and s < 2):
                    act.wait_ge(z["scores"], 4 * s - 4)
                for k in range(KC):
                    i = act.activation(ks[:, p, k, :], k_bank[:, k * KR:(k + 1) * KR], ACT.Identity,
                                       bias=c.col("a_bk", k))
                i.then_inc(z["kevac"], 1)

            def step(s, p, first, last):
                if first:
                    keys_out(0, 0)
                for j in range(4):
                    act.wait_ge(z["nm"], 4 * s + j + 1)
                    for k in range(KC):
                        i = act.activation(pr[:, p, j, k, :], s_bank[j][:, k * KR:(k + 1) * KR], ACT.Exp,
                                           bias=nm_step[:, p, j, k:k + 1], accum_out=rsum[:, p, j, k:k + 1])
                    i.then_inc(z["probs"], 1)
                    if j == 1 and not last:
                        keys_out(s + 1, 1 - p)
                    if j == 2:
                        act.wait_ge(z["vproj"], s + 1)
                        if not (isinstance(s, int) and s < 2):
                            act.wait_ge(z["pv"], s - 1)
                        act.activation(vs[:, p, :, :].rearrange("p a n -> p (a n)"), v_bank[:, :], ACT.Copy).then_inc(z["vevac"], 1)
                act.wait_ge(z["diff"], s + 1)
                act.activation(alpha[:, p, :], diff[:, p, :], ACT.Exp).then_inc(z["alpha"], 1)
            pairs(act, step, span(act)[1])

        @block.vector
        def _(dve):
            dve.memset(ones[:, :], 1.0).then_inc(z["ones"], 1)
            dve.wait_ge(s_mask, 32)
            dve.tensor_copy(maskf[:, :], mask32[:, :].bitcast(U8)).then_inc(z["maskf"], 1)
            dve.wait_ge(z["maskf"], 1)
            dve.reduce_max(anyk[:, :], maskf[:, :], AXX).then_inc(z["anyk"], 1)
            dve.reduce_max(seen[:, 0:NR], maskf[:, :].rearrange("p (r n) -> p r n", n=KR), AXX).then_inc(z["seen"], 1)
            dve.wait_ge(z["anyk"], 1)
            dve.tensor_scalar(seen[:, NR:NR + 1], anyk[:, :], -1.0, 1.0, ALU.mult, ALU.add).then_inc(z["seen"], 1)
            dve.tensor_copy(anyb[:, :], anyk[:, 0:1].to_broadcast([P, P])).then_inc(z["anyb"], 1)
            dve.wait_ge(z["seen"], 2)
            dve.tensor_scalar(maskf[:, :], maskf[:, :], 1.0, BIG, ALU.subtract, ALU.mult).then_inc(z["maskf"], 1)
            dve.wait_ge(z["maskf"], 2)
            dve.tensor_scalar(madd[:, :], maskf[:, :], anyk[:, 0:1], None, ALU.mult).then_inc(z["madd"], 1)
            dve.wait_ge(z["counts"], 1)
            dve.tensor_copy(count[:, :], bank[6][0:1, 0:NR + 1]).then_inc(z["count"], 1)
            dve.wait_ge(z["count"], 1)
            dve.tensor_scalar(act_r[:, :], count[:, 0:NR], count[:, NR:NR + 1], 0.5, ALU.add, ALU.is_ge).then_inc(z["act_r"], 1)
            dve.wait_ge(z["act_r"], 1)
            dve.scalar_tensor_tensor(ends[:, 0, :], act_r[:, :], -2.0 * NR, ri[:, 0:NR], ALU.mult, ALU.add).then_inc(z["ends"], 1)
            dve.tensor_tensor(ends[:, 1, :], act_r[:, :], ri[:, NR:2 * NR], ALU.mult).then_inc(z["ends"], 1)
            dve.wait_ge(z["ends"], 2)
            dve.tensor_reduce(lohi[:, 0:1], ends[:, 0, :], AXX, ALU.min).then_inc(z["lohi"], 1)
            dve.tensor_reduce(lohi[:, 1:2], ends[:, 1, :], AXX, ALU.max).then_inc(z["lohi"], 1)
            dve.wait_ge(z["lohi"], 2)
            dve.tensor_copy(rng[:, 0:1], lohi[:, 0:1]).then_inc(z["span"], 1)
            dve.tensor_tensor(rng[:, 1:2], lohi[:, 1:2], lohi[:, 0:1], ALU.subtract).then_inc(z["span"], 1)
            dve.wait_ge(s_x, 16)
            ln_vector(dve, c, ln, c.x, xn, w)
            dve.wait_ge(z["actp"], 1)
            dve.tensor_copy(actq[:, :], bank[7][:, 0:S]).then_inc(z["actq"], 1)
            dve.wait_ge(s_w, 16 * 9)
            for i in range(4):
                k, g = i // 2, i % 2
                dve.wait_ge(z["qproj"], i + 1)
                dve.tensor_scalar(q[:, k, g * 512:(g + 1) * 512], bank[i][:, :], c.col("a_bq", k), HD ** -0.5,
                                  ALU.add, ALU.mult).then_inc(z["qbias"], 1)
            dve.wait_ge(z["actq"], 1)
            for i in range(4):
                k, g = i // 2, i % 2
                dve.wait_ge(z["qbias"], i + 1)
                dve.tensor_tensor(q2[:, k, g * 512:(g + 1) * 512].rearrange("p (b s) -> p b s", s=S),
                                  q[:, k, g * 512:(g + 1) * 512].rearrange("p (b s) -> p b s", s=S),
                                  actq[:, :].unsqueeze(1).to_broadcast([P, 8, S]), ALU.mult).then_inc(z["qact"], 1)
            dve.wait_ge(z["init"], 3)

            def turned(s, p, j):
                dve.wait_ge(z["transposed"], 4 * s + j + 1)
                dve.tensor_copy(pt[:, j, :], t_bank[:, :]).then_inc(z["pt"], 1)

            def fold(s, p):
                b = s % B
                dve.wait_ge(z["alpha"], s + 1)
                ob = o[:, bass.ds(b, 1), :, :, :].rearrange("p b j k n -> p (b j k) n")
                lb = lsum[:, bass.ds(b, 1), :].rearrange("p b n -> p (b n)")
                dve.tensor_tensor(ob, ob, alpha[:, p, :].unsqueeze(2).to_broadcast([P, 8, 32]),
                                  ALU.mult).then_inc(z["oscaled"], 1)
                dve.tensor_tensor(lb, lb, alpha[:, p, :], ALU.mult).then_inc(z["lscaled"], 1)
                dve.wait_ge(z["oscaled"], s + 1)
                dve.wait_ge(z["pv"], s + 1)
                dve.tensor_tensor(ob, ob, o_bank[:, 0:256].rearrange("p (j n) -> p j n", n=32),
                                  ALU.add).then_inc(z["osummed"], 1)
                dve.wait_ge(z["lscaled"], s + 1)
                dve.tensor_tensor(lb, lb, rsum[:, p, :, :].rearrange("p j k -> p (j k)"), ALU.add).then_inc(z["lsummed"], 1)

            def step(s, p, first, last):
                b = s % B
                for j in range(4):
                    dve.wait_ge(z["scores"], 4 * s + j + 1)
                    dve.tensor_reduce(negmx[:, p, j, :], s_bank[j][:, :].rearrange("p (k n) -> p k n", n=KR),
                                      AXX, ALU.max, negate=True).then_inc(z["negmx"], 1)
                    if not first:
                        turned(s - 1, 1 - p, j)
                    if j == 0 and not first:
                        dve.wait_ge(z["nmkept"], s)
                    dve.wait_ge(z["negmx"], 4 * s + j + 1)
                    dve.tensor_tensor(nm_step[:, p, j, :], negmx[:, p, j, :],
                                      nm[:, bass.ds(b, 1), 2 * j:2 * j + 2].rearrange("p b n -> p (b n)"),
                                      ALU.min).then_inc(z["nm"], 1)
                nb = nm[:, bass.ds(b, 1), :].rearrange("p b n -> p (b n)")
                dve.wait_ge(z["nm"], 4 * s + 4)
                dve.tensor_tensor(diff[:, p, :], nm_step[:, p, :, :].rearrange("p j k -> p (j k)"), nb,
                                  ALU.subtract).then_inc(z["diff"], 1)
                dve.wait_ge(z["diff"], s + 1)
                dve.tensor_scalar(nb, nm_step[:, p, :, :].rearrange("p j k -> p (j k)"), 1.0, None, ALU.mult).then_inc(z["nmkept"], 1)
                if not first:
                    fold(s - 1, 1 - p)
                if last:
                    for j in range(4):
                        turned(s, p, j)
                    fold(s, p)
            more = span(dve)[1]
            pairs(dve, step, more)
            steps = more * B + B

            dve.wait_ge(z["lsummed"], steps)
            dve.reciprocal(linv[:, :, :], lsum[:, :, :]).then_inc(z["linv"], 1)
            dve.wait_ge(z["linv"], 1)
            dve.wait_ge(z["osummed"], steps)
            for g in range(4):
                if g:
                    dve.wait_ge(z["otp"], 2 * g)
                for k in range(KC):
                    for b in range(4 * g, 4 * g + 4):
                        i = dve.tensor_tensor(on[:, b - 4 * g, k, :, :], o[:, b, :, k, :],
                                              linv[:, b, :].rearrange("p (j k) -> p j k", k=KC)[:, :, k].unsqueeze(2)
                                              .to_broadcast([P, 4, 32]), ALU.mult)
                    i.then_inc(z["onorm"], 1)
                for k in range(KC):
                    dve.wait_ge(z["otp"], 2 * g + k + 1)
                    src = bank[k][:, :].rearrange("p (b h s) -> p b h s", b=4, h=2)
                    if g:
                        dve.wait_ge(z["ot"], 2 * g + k - 1)
                    dve.tensor_scalar(tmp[:, k, :, :], src[:, :, 0, :], c.eo[:, 0:1], c.col("a_bv", k), ALU.mult,
                                      ALU.add).then_inc(z["otmp"], 1)
                    dve.wait_ge(z["otmp"], 2 * g + k + 1)
                    dve.scalar_tensor_tensor(ot[:, k, 4 * g:4 * g + 4, :], src[:, :, 1, :], c.eo[:, 1:2],
                                             tmp[:, k, :, :], ALU.mult, ALU.add).then_inc(z["ot"], 1)
            dve.wait_ge(s_w, 16 * 9)
            for t in range(NT):
                dve.tensor_tensor(c.x[:, t, :], c.x[:, t, :], c.row("a_bo"), ALU.add).then_inc(z["xbo"], 1)
            for t in range(NT):
                dve.wait_ge(z["xbo"], t + 1)
                dve.wait_ge(z["oproj"], 2 * (t // 2) + 2)
                dve.tensor_tensor(c.x[:, t, :], c.x[:, t, :], bank[2 + t // 2][:, (t % 2) * D:(t % 2 + 1) * D],
                                  ALU.add).then_inc(z["xout"], 1)

        @block.tensor
        def _(pe):
            pe.wait_ge(z["ones"], 1)
            pe.wait_ge(z["seen"], 2)
            pe.matmul(bank[6][0:1, 0:NR + 1], ones[:, 0:1], seen[:, :], start=True, stop=True).then_inc(z["counts"], 1)
            pe.wait_ge(s_w, 16 * 9)
            pe.wait_ge(z["anyb"], 1)
            xt_tensor(pe, c, ln, xn, bank, ln.xn)
            pe.matmul(bank[7][:, 0:S], anyb[0:S, :], c.ident[0:S, 0:S], start=True, stop=True).then_inc(z["actp"], 1)
            pe.wait_ge(ln.xt, 4)
            for i in range(4):
                k, g = i // 2, i % 2
                for kk in range(KC):
                    m = pe.matmul(bank[i][:, :], wq[:, kk, k * P:(k + 1) * P], xt[:, kk, g * 512:(g + 1) * 512],
                                  start=(kk == 0), stop=(kk == KC - 1))
                m.then_inc(z["qproj"], 1)
            pe.wait_ge(z["qbias"], 4)
            pe.wait_ge(z["madd"], 1)

            r0, more = span(pe)

            def keys(s, p):
                pe.wait_ge(s_ct[p], 8 * s + 16 - 8 * p)
                if not (isinstance(s, int) and s < 1):
                    pe.wait_ge(z["kevac"], s)
                for k in range(KC):
                    for kk in range(KC):
                        m = pe.matmul(k_bank[:, k * KR:(k + 1) * KR], wk[:, kk, k * P:(k + 1) * P], ct[:, p, kk, :],
                                      start=(kk == 0), stop=(kk == KC - 1))
                m.then_inc(z["kproj"], 1)

            def values(s, p):
                if not (isinstance(s, int) and s < 1):
                    pe.wait_ge(z["vevac"], s)
                for a in range(2):
                    for kk in range(KC):
                        m = pe.matmul(v_bank[:, a * D:(a + 1) * D], ct[:, p, kk, a * P:(a + 1) * P], wv[:, kk, :],
                                      start=(kk == 0), stop=(kk == KC - 1))
                m.then_inc(z["vproj"], 1)

            def scores(s, p, j):
                if not (isinstance(s, int) and s < 1):
                    pe.wait_ge(z["probs"], 4 * s - 4 + j + 1)
                for k in range(KC):
                    pe.matmul(s_bank[j][:, k * KR:(k + 1) * KR], c.identb[:, :], madd[:, bass.ds((r0 + s // B).with_bounds(min_val=0, max_val=NR - 1) * KR, KR)],
                              start=(k == 0), stop=False, skip_group_check=True)
                for k in range(KC):
                    m = pe.matmul(s_bank[j][:, k * KR:(k + 1) * KR], qw[32 * j:32 * j + 32, p, k, :],
                                  ks[32 * j:32 * j + 32, p, k, :], start=False, stop=(k == KC - 1),
                                  tile_position=(32 * j, 0), skip_group_check=True)
                m.then_inc(z["scores"], 1)

            def turn(s, p, j):
                if j == 0:
                    if not (isinstance(s, int) and s < 1):
                        pe.wait_ge(z["pt"], 4 * s)
                else:
                    pe.wait_ge(z["pt"], 4 * s + j)
                pe.wait_ge(z["probs"], 4 * s + j + 1)
                for k in range(KC):
                    for a in range(2):
                        m = pe.transpose(t_bank[:, (2 * k + a) * P:(2 * k + a + 1) * P],
                                         pr[:, p, j, k, a * P:(a + 1) * P], c.ident[:, :])
                m.then_inc(z["transposed"], 1)

            def weigh(s, p, j):
                if j == 0:
                    pe.wait_ge(z["vevac"], s + 1)
                    if not (isinstance(s, int) and s < 1):
                        pe.wait_ge(z["osummed"], s)
                pe.wait_ge(z["pt"], 4 * s + j + 1)
                for k in range(KC):
                    for a in range(2):
                        f = k * P + 32 * j
                        m = pe.matmul(o_bank[:, (2 * j + k) * 32:(2 * j + k + 1) * 32],
                                      pt[:, j, (2 * k + a) * P:(2 * k + a + 1) * P], vs[:, p, a, f:f + 32],
                                      start=(a == 0), stop=(a == 1))
                if j == 3:
                    m.then_inc(z["pv"], 1)

            def step(s, p, first, last):
                if first:
                    keys(0, 0)
                pe.wait_ge(z["qw"], s + 1)
                pe.wait_ge(z["kevac"], s + 1)
                for j in range(4):
                    scores(s, p, j)
                    if not first:
                        turn(s - 1, 1 - p, j)
                    if j == 0 and not last:
                        keys(s + 1, 1 - p)
                    if j > 0 and not first:
                        weigh(s - 1, 1 - p, j - 1)
                    if j == 1:
                        values(s, p)
                if not first:
                    weigh(s - 1, 1 - p, 3)
                if last:
                    for j in range(4):
                        turn(s, p, j)
                        weigh(s, p, j)
            pairs(pe, step, more)

            for g in range(4):
                for k in range(KC):
                    pe.wait_ge(z["onorm"], 2 * g + k + 1)
                    if g:
                        pe.wait_ge(z["ot"], 2 * g + k - 1)
                    for b in range(4):
                        m = pe.transpose(bank[k][:, b * P:(b + 1) * P], on[:, b, k, :, :].rearrange("p j n -> p (j n)"), c.ident[:, :])
                    m.then_inc(z["otp"], 1)
            for t in range(NT):
                pe.wait_ge(z["ot"], 2 * (t // 2) + 2)
                for k in range(KC):
                    m = pe.matmul(bank[2 + t // 2][:, (t % 2) * D:(t % 2 + 1) * D],
                                  ot[:, k, 2 * t:2 * t + 2, :].rearrange("p b s -> p (b s)"), wo[:, k, :],
                                  start=(k == 0), stop=(k == KC - 1))
                m.then_inc(z["oproj"], 1)


def stage_kit(nc, ctx, tag, banks=True):
    def sb(name, shape, dt=F32):
        return ctx.enter_context(nc.sbuf_tensor(f"{tag}_{name}", shape, dt))

    def sem(name):
        return stage_semaphore(nc, ctx, f"{tag}_{name}")

    def sems(names):
        return {n: sem(n) for n in names.split()}
    bank = [ctx.enter_context(nc.psum_tensor(f"{tag}_bank{i}", [P, 512], F32)) for i in range(8)] if banks else None
    return sb, sem, sems, bank


def stage_b(nc, c):
    with stage_semaphores(nc) as ctx:
        sb, sem, sems, bank = stage_kit(nc, ctx, "b")
        w = c.w
        xn = sb("xn", [P, NT, D])
        xt = sb("xt", [P, KC, N])
        wq, wk, wv = (sb(n, [P, KC, QKV]) for n in ("wq", "wk", "wv"))
        wo = sb("wo", [P, QKV // P, D])
        wm = sb("wm", [P, 2, KC * HA])
        cm = sb("causal", [P, P])
        xtt = sb("xtt", [P, 2, KC, P])
        sq = sb("sq", [P, QKV])
        ss = sb("ss", [P, 2, HA])
        sv = sb("sv", [P, 2, HA])
        sd = sb("sd", [P, 2, HA])
        rs = sb("rs", [P, 2, HA])
        qh = sb("qh", [P, 2, QKV])
        kh = sb("kh", [P, 2, QKV])
        v = sb("v", [P, 2, QKV])
        qt = sb("qt", [P, 8, P])
        kt = sb("kt", [P, 8, P])
        sc = sb("sc", [P, 2, 8, P])
        ot = sb("ot", [P, 8, P])
        ln = ln_sems(sem, "ln")
        s_w = sem("weights")
        z = sems("wsum wmean wcent xtt qproj kproj vproj qsq ksq qss kss qve kve qsd ksd qrs krs qh kh v "
                 "qtp ktp qt kt scores masked av ot oproj xout")
        QG, KG = (z["qsq"], z["qss"], z["qve"], z["qsd"], z["qrs"], z["qh"]), (z["ksq"], z["kss"], z["kve"], z["ksd"], z["krs"], z["kh"])
        block = ctx.enter_context(nc.Block())

        def tiles(eng, body):
            body(0, 0, True, False)
            body(1, 1, False, False)
            with eng.Fori(1, NT // 2 - 1) as i:
                body(2 * i, 0, False, False)
                body(2 * i + 1, 1, False, False)
            body(NT - 2, 0, False, False)
            body(NT - 1, 1, False, True)

        @block.sync
        def _(sp):
            for t, n in ((wq, "b_wq"), (wk, "b_wk"), (wv, "b_wv"), (wo, "b_wo")):
                sp.dma_start(t[:, :, :], c.d[n].rearrange("(k p) n -> p k n", p=P)).then_inc(s_w, 16)
            sp.dma_start(cm[:, :], c.d["causal"]).then_inc(s_w, 16)

        @block.gpsimd
        def _(pool):
            for i, t in enumerate((wq, wk)):
                pool.wait_ge(z["wmean"], i + 1)
                tv = t[:, :, :].rearrange("p k (h n) -> p (k h) n", n=DA)
                pool.tensor_tensor(tv, tv, wm[:, i, :].unsqueeze(2).to_broadcast([P, KC * HA, DA]),
                                   ALU.add).then_inc(z["wcent"], 1)
            pool.wait_ge(ln.xt, 4)

            def take(s, p, first, last):
                if not (isinstance(s, int) and s < 2):
                    pool.wait_ge(z["vproj"], s - 1)
                pool.tensor_copy(xtt[:, p, :, :], xt[:, :, bass.ds(s * P, P)]).then_inc(z["xtt"], 1)
            tiles(pool, take)

        @block.scalar
        def _(act):
            ln_scalar(act, ln, w)
            xt_scalar(act, ln, bank, xt)

            def squares(s, g, banks, proj, z_sq, z_red):
                act.wait_ge(proj, s + 1)
                if z_red is not None:
                    act.wait_ge(*z_red)
                for i in range(2):
                    a = act.activation(sq[:, i * 512:(i + 1) * 512], banks[i][:, :], ACT.Square)
                a.then_inc(z_sq, 1)

            def root(s, g, z_ve, z_sd):
                act.wait_ge(z_ve, s + 1)
                act.activation(sd[:, g, :], sv[:, g, :], ACT.Sqrt).then_inc(z_sd, 1)

            def turned(s, dst, z_tp, z_t, gname, bname):
                act.wait_ge(z_tp, s + 1)
                for i in range(2):
                    a = act.activation(dst[:, 4 * i:4 * i + 4, :].rearrange("p a n -> p (a n)"), bank[4 + i][:, :],
                                       ACT.Identity, scale=c.col(gname, 0), bias=c.col(bname, 0))
                a.then_inc(z_t, 1)

            def step(s, p, first, last):
                squares(s, 0, bank[0:2], z["qproj"], z["qsq"], None if first else (z["kss"], s))
                if not first:
                    turned(s - 1, qt, z["qtp"], z["qt"], "b_qg", "b_qb")
                root(s, 0, z["qve"], z["qsd"])
                squares(s, 1, bank[2:4], z["kproj"], z["ksq"], (z["qss"], s + 1))
                if not first:
                    turned(s - 1, kt, z["ktp"], z["kt"], "b_kg", "b_kb")
                root(s, 1, z["kve"], z["ksd"])
                act.wait_ge(z["vproj"], s + 1)
                for i in range(2):
                    a = act.activation(v[:, p, i * 512:(i + 1) * 512], bank[i][:, :], ACT.Copy)
                a.then_inc(z["v"], 1)
                if not first:
                    attended(s - 1)
                if last:
                    turned(s, qt, z["qtp"], z["qt"], "b_qg", "b_qb")
                    turned(s, kt, z["ktp"], z["kt"], "b_kg", "b_kb")
                    attended(s)

            def attended(s):
                act.wait_ge(z["av"], s + 1)
                for i in range(2):
                    a = act.activation(ot[:, 4 * i:4 * i + 4, :].rearrange("p a n -> p (a n)"), bank[6 + i][:, :], ACT.Copy)
                a.then_inc(z["ot"], 1)
            tiles(act, step)

        @block.vector
        def _(dve):
            ln_vector(dve, c, ln, c.x, xn, w)
            dve.wait_ge(s_w, 80)
            for i, t in enumerate((wq, wk)):
                dve.reduce_sum(wm[:, i, :], t[:, :, :].rearrange("p k (h n) -> p (k h) n", n=DA), AXX).then_inc(z["wsum"], 1)
                dve.wait_ge(z["wsum"], i + 1)
                dve.tensor_scalar(wm[:, i, :], wm[:, i, :], -1.0 / DA, None, ALU.mult).then_inc(z["wmean"], 1)

            def norm(s, p, g, banks, dst, zs):
                z_sq, z_ss, z_ve, z_sd, z_rs, z_h = zs
                dve.wait_ge(z_sq, s + 1)
                dve.reduce_sum(ss[:, g, :], sq[:, :].rearrange("p (h n) -> p h n", n=DA), AXX).then_inc(z_ss, 1)
                dve.wait_ge(z_ss, s + 1)
                dve.tensor_scalar(sv[:, g, :], ss[:, g, :], 1.0 / DA, 1e-5, ALU.mult, ALU.add).then_inc(z_ve, 1)
                dve.wait_ge(z_sd, s + 1)
                dve.reciprocal(rs[:, g, :], sd[:, g, :]).then_inc(z_rs, 1)
                dve.wait_ge(z_rs, s + 1)
                for i in range(2):
                    a = dve.tensor_tensor(dst[:, p, i * 512:(i + 1) * 512].rearrange("p (h n) -> p h n", n=DA),
                                          banks[i][:, :].rearrange("p (h n) -> p h n", n=DA),
                                          rs[:, g, 8 * i:8 * i + 8].unsqueeze(2).to_broadcast([P, 8, DA]), ALU.mult)
                a.then_inc(z_h, 1)

            def attend(s):
                for half in range(2):
                    dve.wait_ge(z["scores"], 2 * s + half + 1)
                    for par in range(2):
                        a = dve.tensor_tensor(sc[:, par, 4 * half:4 * half + 4, :],
                                              bank[4 + par][:, :].rearrange("p (a n) -> p a n", n=P),
                                              cm[:, :].unsqueeze(1).to_broadcast([P, 4, P]), ALU.mult)
                    a.then_inc(z["masked"], 1)
                dve.wait_ge(z["oproj"], s + 1)
                xs = c.x[:, bass.ds(s, 1), :].rearrange("p a n -> p (a n)")
                dve.tensor_tensor(xs, xs, bank[6][:, 0:D], ALU.add).then_inc(z["xout"], 1)

            def step(s, p, first, last):
                norm(s, p, 0, bank[0:2], qh, QG)
                norm(s, p, 1, bank[2:4], kh, KG)
                if not first:
                    attend(s - 1)
                if last:
                    attend(s)
            tiles(dve, step)

        @block.tensor
        def _(pe):
            xt_tensor(pe, c, ln, xn, bank, ln.xn)
            pe.wait_ge(z["wcent"], 2)
            pe.wait_ge(ln.xt, 4)

            def project(s, p, wt, banks, z_out):
                for i in range(2):
                    for kk in range(KC):
                        m = pe.matmul(banks[i][:, :], xtt[:, p, kk, :], wt[:, kk, i * 512:(i + 1) * 512],
                                      start=(kk == 0), stop=(kk == KC - 1))
                m.then_inc(z_out, 1)

            def turn(p, src, z_tp):
                for i in range(8):
                    m = pe.transpose(bank[4 + i // 4][:, (i % 4) * P:(i % 4 + 1) * P], src[:, p, i * P:(i + 1) * P],
                                     c.ident[:, :])
                m.then_inc(z_tp, 1)

            def turn_q(s, p):
                pe.wait_ge(z["qh"], s + 1)
                if not (isinstance(s, int) and s < 1):
                    pe.wait_ge(z["masked"], 2 * s)
                turn(p, qh, z["qtp"])

            def turn_k(s, p):
                pe.wait_ge(z["kh"], s + 1)
                pe.wait_ge(z["qt"], s + 1)
                turn(p, kh, z["ktp"])

            def scores(s):
                for half in range(2):
                    if half == 0:
                        pe.wait_ge(z["kt"], s + 1)
                    else:
                        pe.wait_ge(z["masked"], 2 * s + 1)
                    for i in range(4):
                        for par in range(2):
                            a = 4 * half + i
                            m = pe.matmul(bank[4 + par][:, i * P:(i + 1) * P], kt[64 * par:64 * par + 64, a, :],
                                          qt[64 * par:64 * par + 64, a, :], start=True, stop=True,
                                          tile_position=(64 * par, 0))
                    m.then_inc(z["scores"], 1)

            def combine(s, p):
                if not (isinstance(s, int) and s < 1):
                    pe.wait_ge(z["xout"], s)
                pe.wait_ge(z["masked"], 2 * s + 2)
                pe.wait_ge(z["v"], s + 1)
                for a in range(8):
                    for par in range(2):
                        m = pe.matmul(bank[6 + a // 4][64 * par:64 * par + 64, (a % 4) * P:(a % 4 + 1) * P],
                                      v[:, p, (2 * a + par) * DA:(2 * a + par + 1) * DA], sc[:, par, a, :],
                                      start=True, stop=True, tile_position=(0, 64 * par))
                m.then_inc(z["av"], 1)
                pe.wait_ge(z["ot"], s + 1)
                for a in range(8):
                    m = pe.matmul(bank[6][:, 0:D], ot[:, a, :], wo[:, a, :], start=(a == 0), stop=(a == 7))
                m.then_inc(z["oproj"], 1)

            def step(s, p, first, last):
                pe.wait_ge(z["xtt"], s + 1)
                if not first:
                    pe.wait_ge(z["v"], s)
                project(s, p, wq, bank[0:2], z["qproj"])
                if not first:
                    turn_q(s - 1, 1 - p)
                    pe.wait_ge(z["kh"], s)
                project(s, p, wk, bank[2:4], z["kproj"])
                if not first:
                    turn_k(s - 1, 1 - p)
                pe.wait_ge(z["qh"], s + 1)
                project(s, p, wv, bank[0:2], z["vproj"])
                if not first:
                    scores(s - 1)
                    combine(s - 1, 1 - p)
                if last:
                    turn_q(s, p)
                    turn_k(s, p)
                    scores(s)
                    combine(s, p)
            tiles(pe, step)


def stage_c(nc, c):
    with stage_semaphores(nc) as ctx:
        sb, sem, sems, bank = stage_kit(nc, ctx, "c")
        w = c.w
        xn = sb("xn", [P, NT, D])
        xt = sb("xt", [P, KC, N])
        wt = sb("wt", [P, KC, D])
        y = sb("y", [P, 4, 2, D])
        ln = ln_sems(sem, "ln")
        z = sems("weights sign binary proj scaled biased clipped xout")
        block = ctx.enter_context(nc.Block())

        @block.sync
        def _(sp):
            sp.dma_start(wt[:, :, :], c.d["c_w"].rearrange("(k p) n -> p k n", p=P)).then_inc(z["weights"], 16)

        @block.scalar
        def _(act):
            ln_scalar(act, ln, w)
            xt_scalar(act, ln, bank, xt)

        @block.vector
        def _(dve):
            ln_vector(dve, c, ln, c.x, xn, w)
            dve.wait_ge(z["weights"], 16)
            dve.tensor_scalar(wt[:, :, :], wt[:, :, :], 0.0, 2.0, ALU.is_ge, ALU.mult).then_inc(z["sign"], 1)
            dve.wait_ge(z["sign"], 1)
            dve.tensor_scalar(wt[:, :, :], wt[:, :, :], 1.0, None, ALU.subtract).then_inc(z["binary"], 1)
            sc = c.row("c_scale").unsqueeze(1).to_broadcast([P, 2, D])
            bi = c.row("c_bias").unsqueeze(1).to_broadcast([P, 2, D])
            for i in range(4):
                ps = bank[4 + i][:, :].rearrange("p (t n) -> p t n", n=D)
                xs = c.x[:, 2 * i:2 * i + 2, :]
                dve.wait_ge(z["proj"], i + 1)
                dve.tensor_tensor(y[:, i, :, :], ps, sc, ALU.mult).then_inc(z["scaled"], 1)
                dve.wait_ge(z["scaled"], i + 1)
                dve.tensor_tensor(y[:, i, :, :], y[:, i, :, :], bi, ALU.add).then_inc(z["biased"], 1)
                dve.wait_ge(z["biased"], i + 1)
                dve.tensor_scalar(y[:, i, :, :], y[:, i, :, :], -100.0, 100.0, ALU.max, ALU.min).then_inc(z["clipped"], 1)
                dve.wait_ge(z["clipped"], i + 1)
                dve.tensor_tensor(xs, xs, y[:, i, :, :], ALU.add).then_inc(z["xout"], 1)

        @block.tensor
        def _(pe):
            xt_tensor(pe, c, ln, xn, bank, ln.xn)
            pe.wait_ge(z["binary"], 1)
            for t in range(NT):
                pe.wait_ge(ln.xt, 2 * (t // 4) + 2)
                for kk in range(KC):
                    m = pe.matmul(bank[4 + t // 2][:, (t % 2) * D:(t % 2 + 1) * D], xt[:, kk, t * P:(t + 1) * P],
                                  wt[:, kk, :], start=(kk == 0), stop=(kk == KC - 1))
                if t % 2:
                    m.then_inc(z["proj"], 1)


def stage_d(nc, c):
    with stage_semaphores(nc) as ctx:
        sb, sem, sems, bank = stage_kit(nc, ctx, "d")
        w = c.w
        G = 4
        NG = B // G
        xn = sb("xn", [P, NT, D])
        xt = sb("xt", [P, KC, N])
        wq, wk, wv, wo = (sb(n, [P, KC, D]) for n in ("wq", "wk", "wv", "wo"))
        cm = sb("causal", [P, S], BF16)
        ct = sb("ct", [P, KC, G, S])
        q = sb("q", [P, KC, G * S])
        qbd = sb("qbd", [P, KC, G, P])
        ks = sb("ks", [P, KC, G * S])
        vs = sb("vs", [P, 2, D])
        ngm = sb("ngm", [P, 4, 8])
        lsum = sb("lsum", [P, 4, 8])
        linv = sb("linv", [P, 4, 8])
        sh = sb("sh", [P, 4, 512])
        pr = sb("pr", [P, 4, 512])
        pt = sb("pt", [P, 4, 512])
        on = sb("on", [P, G, KC, 4, 32])
        tmp = sb("tmp", [P, KC, G, S])
        ot = sb("ot", [P, KC, G, S])
        ln = ln_sems(sem, "ln")
        z = sems("weights ctx xbo qproj kproj vproj qbias qbd ks vs scores negmx shifted probs lsum linv tp pt pv "
                 "onorm otp otmp ot oproj xout")
        block = ctx.enter_context(nc.Block())

        @block.sync
        def _(sp):
            for t, n in ((wq, "d_wq"), (wk, "d_wk"), (wv, "d_wv"), (wo, "d_wo")):
                sp.dma_start(t[:, :, :], c.d[n].rearrange("(k p) n -> p k n", p=P)).then_inc(z["weights"], 16)
            sp.dma_start(cm[:, :], c.d["causalb"]).then_inc(z["weights"], 16)

            def load(g):
                for k in range(KC):
                    sp.dma_start(ct[:, k, :, :], c.d["ctxt"][bass.ds(g * G, G), k * P:(k + 1) * P, 0:S]
                                 .rearrange("b p n -> p b n")).then_inc(z["ctx"], 16)
            load(0)
            with sp.Fori(1, NG) as g:
                sp.wait_ge(z["vproj"], g)
                load(g)

        @block.scalar
        def _(act):
            ln_scalar(act, ln, w)
            xt_scalar(act, ln, bank, xt)

            def turn(g):
                act.wait_ge(z["kproj"], g + 1)
                for k in range(KC):
                    a = act.activation(ks[:, k, :], bank[1][:, k * 256:(k + 1) * 256], ACT.Identity, bias=c.col("d_bk", k))
                a.then_inc(z["ks"], 1)
                act.wait_ge(z["qbias"], g + 1)
                for k in range(KC):
                    src = q[:, k, :].rearrange("p (b s) -> p b s", s=S)
                    act.activation(qbd[:, k, :, 0:S], src, ACT.Copy, scale=c.eo[:, 0:1])
                    a = act.activation(qbd[:, k, :, S:P], src, ACT.Copy, scale=c.eo[:, 1:2])
                a.then_inc(z["qbd"], 1)
                act.wait_ge(z["vproj"], g + 1)
                act.activation(vs[:, :, :].rearrange("p a n -> p (a n)"), bank[2][:, :], ACT.Copy).then_inc(z["vs"], 1)
                for j in range(4):
                    act.wait_ge(z["shifted"], 4 * g + j + 1)
                    act.activation(pr[:, j, :], sh[:, j, :], ACT.Exp).then_inc(z["probs"], 1)
                for j in range(4):
                    act.wait_ge(z["tp"], 4 * g + j + 1)
                    act.activation(pt[:, j, :], bank[3][:, :], ACT.Copy).then_inc(z["pt"], 1)
            turn(0)
            with act.Fori(1, NG) as g:
                turn(g)

        @block.vector
        def _(dve):
            ln_vector(dve, c, ln, c.x, xn, w)
            dve.wait_ge(ln.xn, NT)
            for t in range(NT):
                dve.tensor_tensor(c.x[:, t, :], c.x[:, t, :], c.row("d_bo"), ALU.add).then_inc(z["xbo"], 1)
            dve.wait_ge(z["xbo"], NT)

            def turn(g, first):
                dve.wait_ge(z["qproj"], g + 1)
                for k in range(KC):
                    a = dve.tensor_scalar(q[:, k, :], bank[0][:, k * 256:(k + 1) * 256], c.col("d_bq", k), HD ** -0.5,
                                          ALU.add, ALU.mult)
                a.then_inc(z["qbias"], 1)
                for j in range(4):
                    dve.wait_ge(z["scores"], 4 * g + j + 1)
                    s4 = bank[4 + j][:, :].rearrange("p (a n) -> p a n", n=S)
                    dve.tensor_reduce(ngm[:, j, :], s4, AXX, ALU.max, negate=True).then_inc(z["negmx"], 1)
                    dve.wait_ge(z["negmx"], 4 * g + j + 1)
                    dve.tensor_tensor(sh[:, j, :].rearrange("p (a n) -> p a n", n=S), s4,
                                      ngm[:, j, :].unsqueeze(2).to_broadcast([P, 8, S]), ALU.add).then_inc(z["shifted"], 1)
                for j in range(4):
                    dve.wait_ge(z["probs"], 4 * g + j + 1)
                    dve.reduce_sum(lsum[:, j, :], pr[:, j, :].rearrange("p (a n) -> p a n", n=S), AXX).then_inc(z["lsum"], 1)
                dve.wait_ge(z["lsum"], 4 * g + 4)
                dve.reciprocal(linv[:, :, :], lsum[:, :, :]).then_inc(z["linv"], 1)
                dve.wait_ge(z["linv"], g + 1)
                dve.wait_ge(z["pv"], g + 1)
                for par in range(2):
                    for b in range(2):
                        for k in range(KC):
                            src = bank[par][:, (2 * b + k) * P:(2 * b + k + 1) * P].rearrange("p (j n) -> p j n", n=32)
                            li = linv[:, :, k * G + 2 * b + par].unsqueeze(2).to_broadcast([P, 4, 32])
                            a = dve.tensor_tensor(on[:, 2 * b + par, k, :, :], src, li, ALU.mult)
                a.then_inc(z["onorm"], 1)
                for k in range(KC):
                    dve.wait_ge(z["otp"], 2 * g + k + 1)
                    src = bank[2 + k][:, :].rearrange("p (b h s) -> p b h s", b=G, h=2)
                    dve.tensor_scalar(tmp[:, k, :, :], src[:, :, 0, :], c.eo[:, 0:1], c.col("d_bv", k), ALU.mult,
                                      ALU.add).then_inc(z["otmp"], 1)
                    dve.wait_ge(z["otmp"], 2 * g + k + 1)
                    dve.scalar_tensor_tensor(ot[:, k, :, :], src[:, :, 1, :], c.eo[:, 1:2], tmp[:, k, :, :], ALU.mult,
                                             ALU.add).then_inc(z["ot"], 1)
                dve.wait_ge(z["oproj"], g + 1)
                xs = c.x[:, bass.ds(2 * g, 2), :]
                dve.tensor_tensor(xs, xs, bank[0][:, :].rearrange("p (t n) -> p t n", n=D), ALU.add).then_inc(z["xout"], 1)
            turn(0, True)
            with dve.Fori(1, NG) as g:
                turn(g, False)

        @block.tensor
        def _(pe):
            xt_tensor(pe, c, ln, xn, bank, ln.xn)
            pe.wait_ge(ln.xt, 4)
            pe.wait_ge(z["weights"], 80)

            def turn(g, first):
                if not first:
                    pe.wait_ge(z["xout"], g)
                for k in range(KC):
                    for kk in range(KC):
                        m = pe.matmul(bank[0][:, k * 256:(k + 1) * 256], wq[:, kk, k * P:(k + 1) * P],
                                      xt[:, kk, bass.ds(g * G * S, G * S)], start=(kk == 0), stop=(kk == KC - 1))
                m.then_inc(z["qproj"], 1)
                pe.wait_ge(z["ctx"], 32 * g + 32)
                for k in range(KC):
                    for kk in range(KC):
                        m = pe.matmul(bank[1][:, k * 256:(k + 1) * 256], wk[:, kk, k * P:(k + 1) * P],
                                      ct[:, kk, :, :].rearrange("p b n -> p (b n)"), start=(kk == 0), stop=(kk == KC - 1))
                m.then_inc(z["kproj"], 1)
                for a in range(2):
                    for kk in range(KC):
                        m = pe.matmul(bank[2][:, a * D:(a + 1) * D], ct[:, kk, 2 * a:2 * a + 2, :].rearrange("p b n -> p (b n)"),
                                      wv[:, kk, :], start=(kk == 0), stop=(kk == KC - 1))
                m.then_inc(z["vproj"], 1)
                pe.wait_ge(z["qbd"], g + 1)
                pe.wait_ge(z["ks"], g + 1)
                for j in range(4):
                    if not first:
                        pe.wait_ge(z["shifted"], 4 * g)
                    pe.matmul(bank[4 + j][:, :].rearrange("p (a n) -> p a n", n=S), c.identb[:, :],
                              cm[:, :].unsqueeze(1).to_broadcast([P, 8, S]), start=True, stop=False, skip_group_check=True)
                for b in range(G):
                    for k in range(KC):
                        for j in range(4):
                            m = pe.matmul(bank[4 + j][:, (k * G + b) * S:(k * G + b + 1) * S], qbd[32 * j:32 * j + 32, k, b, :],
                                          ks[32 * j:32 * j + 32, k, b * S:(b + 1) * S], start=False,
                                          stop=(b == G - 1 and k == KC - 1), tile_position=(32 * j, 0), skip_group_check=True)
                            if b == G - 1 and k == KC - 1:
                                m.then_inc(z["scores"], 1)
                for j in range(4):
                    pe.wait_ge(z["probs"], 4 * g + j + 1)
                    if j:
                        pe.wait_ge(z["pt"], 4 * g + j)
                    for a in range(4):
                        m = pe.transpose(bank[3][:, a * P:(a + 1) * P], pr[:, j, a * P:(a + 1) * P], c.ident[:, :])
                    m.then_inc(z["tp"], 1)
                pe.wait_ge(z["vs"], g + 1)
                for j in range(4):
                    pe.wait_ge(z["pt"], 4 * g + j + 1)
                    for k in range(KC):
                        for b in range(2):
                            for par in range(2):
                                f = k * P + 32 * j
                                m = pe.matmul(bank[par][:, (2 * b + k) * P + 32 * j:(2 * b + k) * P + 32 * j + 32],
                                              pt[64 * par:64 * par + 64, j, (2 * k + b) * P:(2 * k + b + 1) * P],
                                              vs[64 * par:64 * par + 64, b, f:f + 32], start=True, stop=True,
                                              tile_position=(64 * par, 0))
                m.then_inc(z["pv"], 1)
                pe.wait_ge(z["onorm"], g + 1)
                for k in range(KC):
                    for b in range(G):
                        m = pe.transpose(bank[2 + k][:, b * P:(b + 1) * P], on[:, b, k, :, :].rearrange("p j n -> p (j n)"),
                                         c.ident[:, :])
                    m.then_inc(z["otp"], 1)
                pe.wait_ge(z["ot"], 2 * g + 2)
                for t in range(2):
                    for kk in range(KC):
                        m = pe.matmul(bank[0][:, t * D:(t + 1) * D], ot[:, kk, 2 * t:2 * t + 2, :].rearrange("p b s -> p (b s)"),
                                      wo[:, kk, :], start=(kk == 0), stop=(kk == KC - 1))
                m.then_inc(z["oproj"], 1)
            turn(0, True)
            with pe.Fori(1, NG) as g:
                turn(g, False)


LEVELS = 6
LOG1P = [1 / 13, 1 / 11, 1 / 9, 1 / 7, 1 / 5, 1 / 3]


def stage_e(nc, c):
    with stage_semaphores(nc) as ctx:
        sb, sem, sems, _ = stage_kit(nc, ctx, "e", banks=False)
        ps = ctx.enter_context(nc.psum_tensor("e_ps", [P, 4096], F32))
        bank = [ps[:, i * 512:(i + 1) * 512] for i in range(8)]
        NB = NT * HG
        w = c.w
        xn = sb("xn", [P, NT, D])
        xl = sb("xl", [P, NT, D])
        h = sb("h", [P, NT, D])
        ht = sb("ht", [P, KC, N])
        wqkv = sb("wqkv", [P, KC, 1024])
        wg = sb("wg", [P, KC, 512])
        wab = sb("wab", [P, KC, 8])
        wo = sb("wo", [P, HG, D])
        w2 = sb("w2", [P, KC, D])
        i2 = sb("i2", [P, S])
        i2z = sb("i2z", [P, S])
        ones = sb("ones", [P, P])
        mt = sb("mt", [P, LEVELS, S])
        i2rep = sb("i2rep", [P, NB, S])
        ms = sb("ms", [P, NT])
        mroot = sb("mroot", [P, NT])
        mrs = sb("mrs", [P, NT])
        cv = sb("cv", [P, 2, B, S])
        lm = cv[:, :, :, :].rearrange("p a b s -> p (a b) s")
        y = xn[:, :, :].rearrange("p t (a s) -> p (t a) s", s=S)
        da = h[:, :, :].rearrange("p t (a s) -> p (t a) s", s=S)
        qkv = sb("qkv", [P, 8, N])
        gate = sb("gate", [P, NT, HG, VD])
        gw = sb("gw", [P, NT, HG, VD])
        u, nabs, ex, den, rden, zz, z2, po, re, sp, dec, beta = (
            sb(n, [P, NT, HG]) for n in "u nabs ex den rden zz z2 po re sp dec beta".split())
        ea = sb("ea", [P, HG])
        eps = sb("eps", [P, 3])
        dt = sb("dt", [P, NB, S])
        dts = sb("dts", [P, NB, S])
        x_ = sb("xinv", [P, NB, S])
        xT = sb("xinvT", [P, NB, S])
        lT, aT = dts, dt
        bv = qkv[:, 0:4, :].rearrange("p a (t h n) -> p (a t) h n", h=HG, n=VD)
        de = gate
        oss = sb("oss", [P, NB])
        osd = sb("osd", [P, NB])
        ors = sb("ors", [P, NB])
        x1 = wqkv[:, :, :].rearrange("p k (t n) -> p (k t) n", n=D)
        l0, ln, l2 = ln_sems(sem, "l0"), ln_sems(sem, "ln"), ln_sems(sem, "l2")
        z = sems("weights consts eps h0 h1 hsq hms hroot hrs h i2rep proj conv qkv gate gw ab u nabs ex den rden zz "
                 "z2 po lp re sp ea g dec beta da dabc scan db dbbc dts sq ss root rrec qk kk lT aT lm y yout zx xx "
                 "xt vt bv dl de o osq oss osv osd ors on og ogt ogs enc x1 xs f2 b2 gel xout initx")
        block = ctx.enter_context(nc.Block())

        def blk(t, hh):
            return (hh % 2) * 16 + t * 2 + hh // 2

        def ordered():
            for hh in range(HG):
                for t in range(NT):
                    yield t, hh, 0
                    yield (t + 4) % NT, (hh + 2) % HG, 1

        @block.sync
        def _(sp_):
            for t, n in ((wqkv, "e_wqkv"), (wg, "e_wg"), (wab, "e_wab"), (wo, "e_wo"), (w2, "e_w2")):
                sp_.dma_start(t[:, :, :], c.d[n].rearrange("(k p) n -> p k n", p=P)).then_inc(z["weights"], 16)
            for t, n in ((i2, "i2"), (i2z, "i2z"), (ones, "ones64")):
                sp_.dma_start(t[:, :], c.d[n]).then_inc(z["consts"], 16)
            sp_.dma_start(mt[:, :, :], c.d["levels"]).then_inc(z["consts"], 16)

        @block.gpsimd
        def _(pool):
            pool.memset(eps[:, 0:1], 1e-6).then_inc(z["eps"], 1)
            pool.memset(eps[:, 1:2], 64e-6).then_inc(z["eps"], 1)
            pool.wait_ge(z["consts"], 64)
            pool.tensor_copy(i2rep[:, :, :], i2[:, :].unsqueeze(1).to_broadcast([P, NB, S])).then_inc(z["i2rep"], 1)
            pool.tensor_copy(x_[:, :, :], i2[:, :].unsqueeze(1).to_broadcast([P, NB, S])).then_inc(z["initx"], 1)
            pool.tensor_copy(xT[:, :, :], i2[:, :].unsqueeze(1).to_broadcast([P, NB, S])).then_inc(z["initx"], 1)
            for t in range(NT):
                pool.wait_ge(z["gate"], t + 1)
                pool.tensor_tensor(gw[:, t, :, :], gate[:, t, :, :],
                                   c.row("e_on").unsqueeze(1).to_broadcast([P, HG, VD]), ALU.mult).then_inc(z["gw"], 1)
            for t in range(NT):
                pool.wait_ge(z["x1"], t + 1)
                pool.tensor_tensor(c.x[:, t, :], c.x[:, t, :], x1[:, t, :], ALU.add).then_inc(z["xs"], 1)

        @block.scalar
        def _(act):
            ln_scalar(act, l0, w)
            ln_scalar(act, ln, w)
            for t in range(NT):
                act.wait_ge(z["h1"], t + 1)
                act.activation(xn[:, t, :], h[:, t, :], ACT.Square, accum_out=ms[:, t:t + 1]).then_inc(z["hsq"], 1)
            act.wait_ge(z["hms"], 1)
            act.activation(mroot[:, :], ms[:, :], ACT.Sqrt).then_inc(z["hroot"], 1)
            xt_scalar(act, ln, bank, ht)
            for m in range(8):
                act.wait_ge(z["conv"], m + 1)
                act.activation(qkv[:, m, :], cv[:, m % 2, :, :].rearrange("p b s -> p (b s)"), ACT.Silu).then_inc(z["qkv"], 1)
            for t in range(NT):
                act.wait_ge(z["proj"], 8 + t + 1)
                act.activation(gate[:, t, :, :].rearrange("p h n -> p (h n)"), bank[t % 4], ACT.Silu).then_inc(z["gate"], 1)
            act.wait_ge(z["ab"], 1)
            act.activation(beta[:, :, :], bank[4][:, 0:64].rearrange("p (t n) -> p t n", n=8)[:, :, 4:8],
                           ACT.Sigmoid).then_inc(z["beta"], 1)
            act.wait_ge(z["nabs"], 1)
            act.activation(ex[:, :, :], nabs[:, :, :], ACT.Exp).then_inc(z["ex"], 1)
            act.activation(ea[:, :], c.row("e_alog"), ACT.Exp).then_inc(z["ea"], 1)
            act.wait_ge(z["g"], 1)
            act.activation(dec[:, :, :], sp[:, :, :], ACT.Exp).then_inc(z["dec"], 1)
            act.wait_ge(z["eps"], 2)
            for m in range(4):
                act.wait_ge(z["qkv"], m + 1)
                if m:
                    act.wait_ge(z["ss"], m)
                act.activation(cv[:, 0, :, :].rearrange("p b s -> p (b s)"), qkv[:, m, :], ACT.Square).then_inc(z["sq"], 1)
                act.wait_ge(z["ss"], m + 1)
                if m:
                    act.wait_ge(z["rrec"], m)
                act.activation(cv[:, 1, :, :].rearrange("p b s -> p (b s)"), ps[:, 1024 * (m % 2):1024 * (m % 2) + 1024],
                               ACT.Sqrt, scale=64.0 if m < 2 else 1.0, bias=eps[:, 1:2] if m < 2 else eps[:, 0:1]
                               ).then_inc(z["root"], 1)
            with act.Fori(0, LEVELS) as lv:
                for g in range(4):
                    act.wait_ge(z["y"], 4 * lv + g + 1)
                    act.activation(y[:, 8 * g:8 * g + 8, :].rearrange("p a n -> p (a n)"), bank[g], ACT.Copy).then_inc(z["yout"], 1)
            act.wait_ge(z["gw"], NT)
            for t in range(NT):
                act.wait_ge(z["dl"], t + 1)
                act.activation(de[:, t, :, :].rearrange("p h n -> p (h n)"), bank[t], ACT.Copy).then_inc(z["de"], 1)
            for t in range(NT):
                act.wait_ge(z["o"], t + 1)
                act.activation(bv[:, t, :, :].rearrange("p h n -> p (h n)"), bank[t], ACT.Square).then_inc(z["osq"], 1)
            act.wait_ge(z["oss"], NT)
            act.activation(osd[:, :], oss[:, :], ACT.Sqrt, scale=1.0 / VD, bias=eps[:, 0:1]).then_inc(z["osd"], 1)
            for t in range(NT):
                act.wait_ge(z["ogt"], t + 1)
                act.activation(de[:, t, :, :].rearrange("p h n -> p (h n)"), bank[t], ACT.Copy).then_inc(z["ogs"], 1)
            ln_scalar(act, l2, w)
            xt_scalar(act, l2, bank, ht, c.cols[:, COLS["e_g2"][0]:COLS["e_g2"][0] + 2],
                      c.cols[:, COLS["e_b2"][0]:COLS["e_b2"][0] + 2])
            for t in range(NT):
                act.wait_ge(z["b2"], t + 1)
                act.activation(xn[:, t, :], h[:, t, :], ACT.Gelu).then_inc(z["gel"], 1)

        @block.vector
        def _(dve):
            ln_vector(dve, c, l0, c.x, xl, w)
            dve.wait_ge(l0.xn, NT)
            ln_vector(dve, c, ln, xl, xn, w)
            for t in range(NT):
                dve.wait_ge(ln.xn, t + 1)
                dve.tensor_tensor(h[:, t, :], xn[:, t, :], c.row("e_g1"), ALU.mult).then_inc(z["h0"], 1)
            for t in range(NT):
                dve.wait_ge(z["h0"], t + 1)
                dve.tensor_tensor(h[:, t, :], h[:, t, :], c.row("e_b1"), ALU.add).then_inc(z["h1"], 1)
            dve.wait_ge(z["hsq"], NT)
            dve.tensor_scalar(ms[:, :], ms[:, :], 1.0 / D, 1e-6, ALU.mult, ALU.add).then_inc(z["hms"], 1)
            dve.wait_ge(z["hroot"], 1)
            dve.reciprocal(mrs[:, :], mroot[:, :]).then_inc(z["hrs"], 1)
            dve.wait_ge(z["hrs"], 1)
            for t in range(NT):
                dve.scalar_tensor_tensor(h[:, t, :], h[:, t, :], mrs[:, t:t + 1], c.row("e_rms"), ALU.mult,
                                         ALU.mult).then_inc(z["h"], 1)
            nconv = 0
            for m in range(8):
                src = ps[:, 1024 * ((m + 2) % 4):1024 * ((m + 2) % 4) + 1024].rearrange("p (b s) -> p b s", s=S)
                tap = lambda i: c.col("e_cw", 4 * m + i)
                dve.wait_ge(z["proj"], m + 1)
                if m > 1:
                    dve.wait_ge(z["qkv"], m - 1)
                o_ = cv[:, m % 2, :, :]
                dve.tensor_scalar(o_, src, tap(3), None, ALU.mult).then_inc(z["xx"], 1)
                nconv += 1
                for back in range(1, 4):
                    dve.wait_ge(z["xx"], nconv)
                    i = dve.scalar_tensor_tensor(o_[:, :, back:S], src[:, :, 0:S - back], tap(3 - back), o_[:, :, back:S],
                                                 ALU.mult, ALU.add)
                    if back < 3:
                        i.then_inc(z["xx"], 1)
                        nconv += 1
                i.then_inc(z["conv"], 1)
            dve.wait_ge(z["ab"], 1)
            dve.wait_ge(z["beta"], 1)
            dve.tensor_tensor(u[:, :, :], bank[4][:, 0:64].rearrange("p (t n) -> p t n", n=8)[:, :, 0:4],
                              c.row("e_dt").unsqueeze(1).to_broadcast([P, NT, HG]), ALU.add).then_inc(z["u"], 1)
            dve.wait_ge(z["u"], 1)
            dve.tensor_scalar(re[:, :, :], u[:, :, :], 0.0, None, ALU.max).then_inc(z["re"], 1)
            dve.wait_ge(z["re"], 1)
            dve.scalar_tensor_tensor(nabs[:, :, :], re[:, :, :], -2.0, u[:, :, :], ALU.mult, ALU.add).then_inc(z["nabs"], 1)
            dve.wait_ge(z["ex"], 1)
            dve.tensor_scalar(den[:, :, :], ex[:, :, :], 2.0, None, ALU.add).then_inc(z["den"], 1)
            dve.wait_ge(z["den"], 1)
            dve.reciprocal(rden[:, :, :], den[:, :, :]).then_inc(z["rden"], 1)
            dve.wait_ge(z["rden"], 1)
            dve.tensor_tensor(zz[:, :, :], ex[:, :, :], rden[:, :, :], ALU.mult).then_inc(z["zz"], 1)
            dve.wait_ge(z["zz"], 1)
            dve.tensor_tensor(z2[:, :, :], zz[:, :, :], zz[:, :, :], ALU.mult).then_inc(z["z2"], 1)
            dve.wait_ge(z["z2"], 1)
            dve.tensor_scalar(po[:, :, :], z2[:, :, :], 1 / 15, None, ALU.mult).then_inc(z["po"], 1)
            for i, k in enumerate(LOG1P):
                dve.wait_ge(z["po"], i + 1)
                dve.scalar_tensor_tensor(po[:, :, :], po[:, :, :], k, z2[:, :, :], ALU.add, ALU.mult).then_inc(z["po"], 1)
            dve.wait_ge(z["po"], len(LOG1P) + 1)
            dve.scalar_tensor_tensor(po[:, :, :], po[:, :, :], 1.0, zz[:, :, :], ALU.add, ALU.mult).then_inc(z["lp"], 1)
            dve.wait_ge(z["lp"], 1)
            dve.wait_ge(z["re"], 1)
            dve.scalar_tensor_tensor(sp[:, :, :], po[:, :, :], 2.0, re[:, :, :], ALU.mult, ALU.add).then_inc(z["sp"], 1)
            dve.wait_ge(z["sp"], 1)
            dve.wait_ge(z["ea"], 1)
            dve.scalar_tensor_tensor(sp[:, :, :], sp[:, :, :], -1.0, ea[:, :].unsqueeze(1).to_broadcast([P, NT, HG]),
                                     ALU.mult, ALU.mult).then_inc(z["g"], 1)

            def spread(dst, eye, val, s_):
                for r in range(2):
                    i = dve.tensor_tensor(
                        dst[:, 16 * r:16 * r + 16, :].rearrange("p (t c) n -> p t c n", c=2),
                        eye[:, :].unsqueeze(1).unsqueeze(1).to_broadcast([P, NT, 2, S]),
                        val[:, :, :].rearrange("p t (c r) -> p r t c", r=2)[:, r, :, :].unsqueeze(3)
                        .to_broadcast([P, NT, 2, S]), ALU.mult)
                i.then_inc(s_, 1)
            dve.wait_ge(z["consts"], 64)
            dve.wait_ge(z["dec"], 1)
            spread(da, i2z, dec, z["da"])
            dve.wait_ge(z["beta"], 1)
            spread(dts, i2, beta, z["db"])
            for m in range(4):
                dve.wait_ge(z["root"], m + 1)
                if m:
                    dve.wait_ge(z["qk"], m)
                pp = ps[:, 1024 * (m % 2):1024 * (m % 2) + 1024]
                dve.reciprocal(pp, cv[:, 1, :, :].rearrange("p b s -> p (b s)")).then_inc(z["rrec"], 1)
                dve.wait_ge(z["rrec"], m + 1)
                dve.tensor_tensor(qkv[:, m, :], qkv[:, m, :], pp, ALU.mult).then_inc(z["qk"], 1)
            dve.wait_ge(z["dabc"], 4)
            dve.wait_ge(z["i2rep"], 1)
            flat = lambda a: a[:, :, :].rearrange("p a n -> p (a n)")
            dve.tensor_tensor_scan(flat(dt), ps[:, 0:2048], flat(i2rep), 0.0, ALU.mult, ALU.add).then_inc(z["scan"], 1)
            dve.wait_ge(z["scan"], 1)
            dve.wait_ge(z["dbbc"], 4)
            dve.tensor_tensor(flat(da), flat(dt), flat(i2rep), ALU.subtract).then_inc(z["scan"], 1)
            dve.wait_ge(z["scan"], 2)
            dve.tensor_tensor(flat(dts), flat(da), ps[:, 2048:4096], ALU.mult).then_inc(z["dts"], 1)
            dve.wait_ge(z["dts"], 1)
            dve.wait_ge(z["kk"], 1)
            dve.tensor_tensor(flat(lT), flat(dts), ps[:, 0:2048], ALU.mult).then_inc(z["lT"], 1)
            dve.wait_ge(z["kk"], 2)
            dve.tensor_tensor(flat(aT), flat(dt), ps[:, 2048:4096], ALU.mult).then_inc(z["aT"], 1)
            dve.wait_ge(z["lT"], 1)
            dve.wait_ge(z["initx"], 2)
            with dve.Fori(0, LEVELS) as lv:
                dve.tensor_tensor(lm[:, :, :], lT[:, :, :], mt[:, bass.ds(lv, 1), :].to_broadcast([P, NB, S]),
                                  ALU.mult).then_inc(z["lm"], 1)
                for g in range(4):
                    dve.wait_ge(z["zx"], 8 * lv + 2 * g + 1)
                    xg = x_[:, 8 * g:8 * g + 8, :].rearrange("p a n -> p (a n)")
                    dve.tensor_tensor(xg, xg, bank[4 + g], ALU.subtract).then_inc(z["xt"], 1)
                    dve.wait_ge(z["zx"], 8 * lv + 2 * g + 2)
                    tg = xT[:, 8 * g:8 * g + 8, :].rearrange("p a n -> p (a n)")
                    dve.tensor_tensor(tg, tg, bank[g], ALU.subtract).then_inc(z["xt"], 1)
            for t in range(NT):
                dve.wait_ge(z["vt"], t + 1)
                dve.tensor_tensor(bv[:, t, :, :], bank[t].rearrange("p (h n) -> p h n", n=VD),
                                  beta[:, t, :].unsqueeze(2).to_broadcast([P, HG, VD]), ALU.mult).then_inc(z["bv"], 1)
            for t in range(NT):
                dve.wait_ge(z["osq"], t + 1)
                dve.reduce_sum(oss[:, 4 * t:4 * t + 4], bv[:, t, :, :], AXX).then_inc(z["oss"], 1)
            dve.wait_ge(z["osd"], 1)
            dve.reciprocal(ors[:, :], osd[:, :]).then_inc(z["ors"], 1)
            dve.wait_ge(z["ors"], 1)
            for t in range(NT):
                dve.tensor_tensor(de[:, t, :, :], bank[t].rearrange("p (h n) -> p h n", n=VD),
                                  ors[:, 4 * t:4 * t + 4].unsqueeze(2).to_broadcast([P, HG, VD]), ALU.mult).then_inc(z["on"], 1)
            for t in range(NT):
                dve.wait_ge(z["on"], t + 1)
                dve.wait_ge(z["gw"], t + 1)
                dve.tensor_tensor(bv[:, t, :, :], de[:, t, :, :], gw[:, t, :, :], ALU.mult).then_inc(z["og"], 1)
            for t in range(NT):
                dve.wait_ge(z["enc"], 2 * (t // 2) + 2)
                dve.tensor_tensor(x1[:, t, :], xl[:, t, :], bank[t // 2][:, (t % 2) * D:(t % 2 + 1) * D],
                                  ALU.add).then_inc(z["x1"], 1)
            dve.wait_ge(z["x1"], NT)
            ln_vector(dve, c, l2, x1, xn, w)
            for t in range(NT):
                dve.wait_ge(z["f2"], t // 2 + 1)
                dve.tensor_tensor(h[:, t, :], bank[4 + t // 2][:, (t % 2) * D:(t % 2 + 1) * D], c.row("e_w2b"),
                                  ALU.add).then_inc(z["b2"], 1)
            for t in range(NT):
                dve.wait_ge(z["gel"], t + 1)
                dve.wait_ge(z["xs"], t + 1)
                dve.tensor_tensor(c.x[:, t, :], c.x[:, t, :], xn[:, t, :], ALU.add).then_inc(z["xout"], 1)

        @block.tensor
        def _(pe):
            xt_tensor(pe, c, ln, h, bank, z["h"])
            pe.wait_ge(z["weights"], 80)
            for m in range(8):
                pe.wait_ge(ln.xt, 4)
                if m > 3:
                    pe.wait_ge(z["conv"], m - 3)
                at = 1024 * ((m + 2) % 4)
                for g in range(2):
                    for kk in range(KC):
                        i = pe.matmul(ps[:, at + 512 * g:at + 512 * g + 512], wqkv[:, kk, m * P:(m + 1) * P],
                                      ht[:, kk, 512 * g:512 * g + 512], start=(kk == 0), stop=(kk == KC - 1))
                i.then_inc(z["proj"], 1)
            for t in range(NT):
                if t == 0:
                    pe.wait_ge(z["conv"], 8)
                if t > 3:
                    pe.wait_ge(z["gate"], t - 3)
                for kk in range(KC):
                    i = pe.matmul(bank[t % 4], ht[:, kk, t * P:(t + 1) * P], wg[:, kk, :], start=(kk == 0), stop=(kk == KC - 1))
                i.then_inc(z["proj"], 1)
            for t in range(NT):
                for kk in range(KC):
                    i = pe.matmul(bank[4][:, 8 * t:8 * t + 8], ht[:, kk, t * P:(t + 1) * P], wab[:, kk, :],
                                  start=(kk == 0), stop=(kk == KC - 1))
            i.then_inc(z["ab"], 1)
            pe.wait_ge(z["consts"], 64)
            pe.wait_ge(z["gate"], NT)
            for m in range(4):
                pe.wait_ge(z["sq"], m + 1)
                if m > 1:
                    pe.wait_ge(z["qk"], m - 1)
                for g in range(2):
                    i = pe.matmul(bank[2 * (m % 2) + g], ones[:, :],
                                  cv[:, 0, 8 * g:8 * g + 8, :].rearrange("p b s -> p (b s)"), start=True, stop=True)
                i.then_inc(z["ss"], 1)
            pe.wait_ge(z["qk"], 4)
            pe.wait_ge(z["da"], 1)
            for g in range(4):
                pe.matmul(bank[g], ones[:, :], da[:, 8 * g:8 * g + 8, :].rearrange("p a n -> p (a n)"),
                          start=True, stop=True).then_inc(z["dabc"], 1)
            pe.wait_ge(z["db"], 1)
            pe.wait_ge(z["beta"], 1)
            pe.wait_ge(z["u"], 1)
            for g in range(4):
                pe.matmul(bank[4 + g], ones[:, :], dts[:, 8 * g:8 * g + 8, :].rearrange("p a n -> p (a n)"),
                          start=True, stop=True).then_inc(z["dbbc"], 1)
            for which in range(2):
                if which == 0:
                    pe.wait_ge(z["scan"], 1)
                else:
                    pe.wait_ge(z["dts"], 1)
                for t in range(NT):
                    for b2 in range(2):
                        for cc in range(2):
                            for r in range(2):
                                at = 2048 * which + S * blk(t, 2 * cc + r)
                                tok = t * P + b2 * S
                                kx = qkv[64 * r:64 * r + 64, 2 + cc, tok:tok + S]
                                rx = kx if which == 0 else qkv[64 * r:64 * r + 64, cc, tok:tok + S]
                                i = pe.matmul(ps[64 * b2:64 * b2 + 64, at:at + S], kx, rx, start=True, stop=True,
                                              tile_position=(64 * r, 64 * b2))
                i.then_inc(z["kk"], 1)

            def product(dst, lhs, rhs, g):
                for a in range(8 * g, 8 * g + 8):
                    for b2 in range(2):
                        r = slice(64 * b2, 64 * b2 + 64)
                        i = pe.matmul(dst[r, (a % 8) * S:(a % 8 + 1) * S], lhs[r, a, :], rhs[r, a, :], start=True,
                                      stop=True, tile_position=(64 * b2, 64 * b2))
                return i
            pe.wait_ge(z["lT"], 1)
            pe.wait_ge(z["aT"], 1)
            pe.wait_ge(z["initx"], 2)

            def level(lv):
                pe.wait_ge(z["lm"], lv + 1)
                for g in range(4):
                    if not isinstance(lv, int) and g == 0:
                        pe.wait_ge(z["xt"], 8 * lv)
                        pe.nop(nofuse=True)
                    product(bank[g], lm, x_, g).then_inc(z["y"], 1)
                for g in range(4):
                    pe.wait_ge(z["yout"], 4 * lv + g + 1)
                    pe.nop(nofuse=True)
                    product(bank[4 + g], xT, y, g).then_inc(z["zx"], 1)
                    product(bank[g], y, xT, g).then_inc(z["zx"], 1)
            level(0)
            with pe.Fori(1, LEVELS) as lv:
                level(lv)
            pe.wait_ge(z["xt"], 8 * LEVELS)
            for t in range(NT):
                for hh in range(HG):
                    i = pe.transpose(bank[t][:, hh * P:(hh + 1) * P], qkv[:, 4 + hh, t * P:(t + 1) * P], c.ident[:, :])
                i.then_inc(z["vt"], 1)

            def apply(matT, vec, ready, done):
                for t in range(NT):
                    pe.wait_ge(ready, t + 1)
                    for hh in range(HG):
                        for b2 in range(2):
                            r = slice(64 * b2, 64 * b2 + 64)
                            i = pe.matmul(bank[t][r, hh * VD:(hh + 1) * VD], matT[r, blk(t, hh), :], vec[r, t, hh, :],
                                          start=True, stop=True, tile_position=(64 * b2, 64 * b2))
                    i.then_inc(done, 1)
            apply(xT, bv, z["bv"], z["dl"])
            apply(aT, de, z["de"], z["o"])
            for t in range(NT):
                pe.wait_ge(z["og"], t + 1)
                for hh in range(HG):
                    i = pe.transpose(bank[t][:, hh * P:(hh + 1) * P], bv[:, t, hh, :], c.ident[:, :])
                i.then_inc(z["ogt"], 1)
            for t in range(NT):
                pe.wait_ge(z["ogs"], max(t + 1, min(NT, t // 2 + 1)))
                for hh in range(HG):
                    i = pe.matmul(bank[t // 2][:, (t % 2) * D:(t % 2 + 1) * D], de[:, t, hh, :], wo[:, hh, :],
                                  start=(hh == 0), stop=(hh == HG - 1))
                i.then_inc(z["enc"], 1)
            pe.wait_ge(z["x1"], NT)
            xt_tensor(pe, c, l2, xn, bank, l2.xn)
            for t in range(NT):
                pe.wait_ge(l2.xt, 4)
                for kk in range(KC):
                    i = pe.matmul(bank[4 + t // 2][:, (t % 2) * D:(t % 2 + 1) * D], ht[:, kk, t * P:(t + 1) * P], w2[:, kk, :],
                                  start=(kk == 0), stop=(kk == KC - 1))
                if t % 2:
                    i.then_inc(z["f2"], 1)


def stage_f(nc, c):
    with stage_semaphores(nc) as ctx:
        sb, sem, sems, bank = stage_kit(nc, ctx, "f")
        FC = F // P
        MAXT = E - 1 + N // P
        slots_x = nc.dram_tensor("slots_x", ((MAXT + 1) * P, D), F32, kind="Internal").ap()
        slots_y = nc.dram_tensor("slots_y", (MAXT * P, D), F32, kind="Internal").ap()
        xn = sb("xn", [P, NT, D])
        xt = sb("xt", [P, KC, N])
        w1 = sb("w1", [P, E, KC, F])
        w2 = sb("w2", [P, E, FC, D])
        wr = sb("wr", [P, KC, E])
        before = sb("before", [P, P])
        ones = sb("ones", [P, P])
        tab = sb("tab", [P, E + E * NT + E * E])
        iota = tab[:, 0:E]
        over = tab[:, E:E + E * NT].rearrange("p (e k) -> p e k", e=E)
        prior = tab[:, E + E * NT:].rearrange("p (e f) -> p e f", e=E)
        zero = sb("zero", [P, D])
        lg, sh, ex, eq, cand, hot, posm, posh = (sb(n, [P, NT, E]) for n in "lg sh ex eq cand hot posm posh".split())
        mx, se, rse, ix, pos = (sb(n, [P, NT]) for n in "mx se rse ix pos".split())
        run = sb("run", [P, NT + 1, E])
        cmp_ = sb("cmp", [P, E, NT])
        more, cnt, first = (sb(n, [P, E]) for n in "more cnt first".split())
        pri = sb("pri", [P, E, E])
        posi = sb("posi", [P, NT], U32)
        ends = sb("ends", [1, E + 1], mybir.dt.int32)
        xs = sb("xs", [P, D])
        xts = sb("xts", [P, 2, KC, P])
        hb = sb("hb", [P, FC, P])
        yb = sb("yb", [P, D])
        yg = sb("yg", [P, NT, D])
        s = ln_sems(sem, "ln")
        z = sems("small zero cleared logits lg mx sh ex se rse eq cand ix hot rank tot run cmp more cnt pri first posa "
                 "posb posh pos posi ends scattered xs xst xts hid act ypr yb stored gathered xout")
        s_w = [sem(f"w{e}") for e in range(E)]
        block = ctx.enter_context(nc.Block())

        def tiles(eng, body):
            eng.wait_ge(z["ends"], 2)
            at = 0
            for e in range(E):
                end = eng.value_load(ends[0:1, e:e + 1], min_val=e + 1, max_val=MAXT)
                with eng.Fori(at, end) as i:
                    body(e, i)
                at = end
            return at

        @block.sync
        def _(sp):
            sp.dma_start(wr[:, :, :], c.d["f_wr"].rearrange("(k p) n -> p k n", p=P)).then_inc(z["small"], 16)
            sp.dma_start(before[:, :], c.d["before"]).then_inc(z["small"], 16)
            sp.dma_start(ones[:, :], c.d["ones"]).then_inc(z["small"], 16)
            sp.dma_start(tab[:, :], c.d["f_tab"]).then_inc(z["small"], 16)
            for e in range(E):
                sp.dma_start(w1[:, e, :, :], c.d["f_w1"][e, :, :].rearrange("(k p) n -> p k n", p=P)).then_inc(s_w[e], 16)
                sp.dma_start(w2[:, e, :, :], c.d["f_w2"][e, :, :].rearrange("(k p) n -> p k n", p=P)).then_inc(s_w[e], 16)
            sp.wait_ge(z["scattered"], 16 * NT)
            sp.dma_start(xs[:, :], slots_x[0:P, :]).then_inc(z["xs"], 16)

            def load(e, i):
                sp.wait_ge(z["xst"], i + 1)
                sp.nop(nofuse=True)
                sp.dma_start(xs[:, :], slots_x[bass.ds(i * P + P, P), :]).then_inc(z["xs"], 16)
            end = tiles(sp, load)
            sp.wait_ge(z["xs"], end * 16 + 16)
            sp.nop(nofuse=True)

        @block.gpsimd
        def _(pool):
            pool.memset(zero[:, :], 0.0).then_inc(z["zero"], 1)
            pool.wait_ge(z["zero"], 1)
            pool.dma_start(slots_x.rearrange("(t p) d -> p t d", p=P),
                           zero[:, :].unsqueeze(1).to_broadcast([P, MAXT + 1, D])).then_inc(z["stored"], 16)
            pool.dma_start(slots_y.rearrange("(t p) d -> p t d", p=P),
                           zero[:, :].unsqueeze(1).to_broadcast([P, MAXT, D])).then_inc(z["cleared"], 16)
            pool.wait_ge(z["stored"], 16)
            pool.wait_ge(z["cleared"], 16)
            pool.wait_ge(z["posi"], 1)
            for t in range(NT):
                pool.indirect_dma_start(slots_x, bass.IndirectOffsetOnAxis(ap=posi[:, t:t + 1], axis=0),
                                        xn[:, t, :], None).then_inc(z["scattered"], 16)

            def store(e, i):
                pool.wait_ge(z["yb"], i + 2)
                pool.nop(nofuse=True)
                pool.dma_start(slots_y[bass.ds(i * P, P), :], yb[:, :]).then_inc(z["stored"], 16)
            end = tiles(pool, store)
            pool.wait_ge(z["stored"], end * 16 + 16)
            pool.nop(nofuse=True)
            for t in range(NT):
                pool.indirect_dma_start(yg[:, t, :], None, slots_y,
                                        bass.IndirectOffsetOnAxis(ap=posi[:, t:t + 1], axis=0)).then_inc(z["gathered"], 16)

        @block.scalar
        def _(act):
            ln_scalar(act, s, c.w)
            xt_scalar(act, s, bank, xt)
            act.wait_ge(z["sh"], NT)
            act.activation(ex[:, :, :], sh[:, :, :], ACT.Exp).then_inc(z["ex"], 1)
            act.sem_inc(z["act"], 4)

            def hidden(e, i):
                for m in range(FC):
                    act.wait_ge(z["hid"], i * FC + (m + 1))
                    act.activation(hb[:, m, :], bank[m % 4][:, 0:P], ACT.Gelu, bias=c.col("f_b1", e * FC + m)
                                   ).then_inc(z["act"], 1)
            tiles(act, hidden)

        @block.vector
        def _(dve):
            ln_vector(dve, c, s, c.x, xn, c.w)
            dve.wait_ge(z["logits"], 1)
            dve.tensor_tensor(lg[:, :, :], bank[4][:, 0:64].rearrange("p (t n) -> p t n", n=E),
                              c.row("f_br").unsqueeze(1).to_broadcast([P, NT, E]), ALU.add).then_inc(z["lg"], 1)
            dve.wait_ge(z["lg"], 1)
            dve.reduce_max(mx[:, :], lg[:, :, :], AXX).then_inc(z["mx"], 1)
            dve.wait_ge(z["mx"], 1)
            for t in range(NT):
                dve.tensor_scalar(sh[:, t, :], lg[:, t, :], mx[:, t:t + 1], None, ALU.subtract).then_inc(z["sh"], 1)
            dve.wait_ge(z["sh"], NT)
            dve.tensor_scalar(eq[:, :, :], sh[:, :, :], 0.0, -float(E), ALU.is_ge, ALU.mult).then_inc(z["eq"], 1)
            dve.wait_ge(z["eq"], 1)
            dve.wait_ge(z["small"], 64)
            dve.tensor_tensor(cand[:, :, :], eq[:, :, :], iota.unsqueeze(1).to_broadcast([P, NT, E]), ALU.add
                              ).then_inc(z["cand"], 1)
            dve.wait_ge(z["cand"], 1)
            dve.tensor_reduce(ix[:, :], cand[:, :, :], AXX, ALU.min).then_inc(z["ix"], 1)
            dve.wait_ge(z["ix"], 1)
            dve.tensor_tensor(hot[:, :, :], cand[:, :, :], ix[:, :].unsqueeze(2).to_broadcast([P, NT, E]),
                              ALU.is_equal).then_inc(z["hot"], 1)
            dve.memset(run[:, 0, :], 0.0).then_inc(z["run"], 1)
            dve.wait_ge(z["tot"], 1)
            for t in range(NT):
                dve.wait_ge(z["run"], t + 1)
                dve.tensor_tensor(run[:, t + 1, :], run[:, t, :], bank[5][:, E * t:E * t + E], ALU.add).then_inc(z["run"], 1)
            dve.wait_ge(z["run"], NT + 1)
            dve.tensor_tensor(cmp_[:, :, :], run[:, NT, :].unsqueeze(2).to_broadcast([P, E, NT]), over,
                              ALU.is_gt).then_inc(z["cmp"], 1)
            dve.tensor_tensor(posm[:, :, :], run[:, 0:NT, :], bank[4][:, 64:128].rearrange("p (t n) -> p t n", n=E),
                              ALU.add).then_inc(z["posa"], 1)
            dve.wait_ge(z["cmp"], 1)
            dve.reduce_sum(more[:, :], cmp_[:, :, :], AXX).then_inc(z["more"], 1)
            dve.wait_ge(z["more"], 1)
            dve.tensor_scalar(cnt[:, :], more[:, :], 1.0, None, ALU.add).then_inc(z["cnt"], 1)
            dve.wait_ge(z["cnt"], 1)
            dve.tensor_tensor(pri[:, :, :], cnt[:, :].unsqueeze(1).to_broadcast([P, E, E]), prior, ALU.mult).then_inc(z["pri"], 1)
            dve.wait_ge(z["pri"], 1)
            dve.reduce_sum(first[:, :], pri[:, :, :], AXX).then_inc(z["first"], 1)
            dve.wait_ge(z["first"], 1)
            dve.wait_ge(z["posa"], 1)
            dve.scalar_tensor_tensor(posm[:, :, :], first[:, :].unsqueeze(1).to_broadcast([P, NT, E]), float(P),
                                     posm[:, :, :], ALU.mult, ALU.add).then_inc(z["posb"], 1)
            dve.wait_ge(z["posb"], 1)
            dve.tensor_tensor(posh[:, :, :], posm[:, :, :], hot[:, :, :], ALU.mult).then_inc(z["posh"], 1)
            dve.wait_ge(z["posh"], 1)
            dve.reduce_sum(pos[:, :], posh[:, :, :], AXX).then_inc(z["pos"], 1)
            dve.wait_ge(z["pos"], 1)
            dve.tensor_copy(posi[:, :], pos[:, :]).then_inc(z["posi"], 1)
            dve.tensor_tensor(ends[:, 0:E], first[0:1, :], cnt[0:1, :], ALU.add).then_inc(z["ends"], 1)
            dve.memset(ends[:, E:E + 1], 0).then_inc(z["ends"], 1)
            dve.wait_ge(z["ex"], 1)
            dve.reduce_sum(se[:, :], ex[:, :, :], AXX).then_inc(z["se"], 1)
            dve.wait_ge(z["se"], 1)
            dve.reciprocal(rse[:, :], se[:, :]).then_inc(z["rse"], 1)

            def turned(i, slot):
                dve.wait_ge(z["xst"], i + 1)
                dve.tensor_copy(xts[:, slot, :, :].rearrange("p k n -> p (k n)"), bank[4][:, 0:D]).then_inc(z["xts"], 1)
            dve.wait_ge(z["xst"], 1)
            dve.tensor_copy(xts[:, 0, :, :].rearrange("p k n -> p (k n)"), bank[4][:, 0:D]).then_inc(z["xts"], 1)
            dve.sem_inc(z["yb"], 1)

            def out_(e, i):
                dve.wait_ge(z["xst"], i + 2)
                dve.tensor_scalar(xts[:, bass.ds((i + 1) % 2, 1), :, :].rearrange("p b k n -> p (b k n)"), bank[4][:, 0:D],
                                  1.0, None, ALU.mult).then_inc(z["xts"], 1)
                dve.wait_ge(z["ypr"], i + 1)
                dve.wait_ge(z["stored"], i * 16 + 16)
                dve.tensor_tensor(yb[:, :], bank[5][:, 0:D], c.row("f_b2", e * D, D), ALU.add).then_inc(z["yb"], 1)
            tiles(dve, out_)
            dve.wait_ge(z["rse"], 1)
            dve.wait_ge(z["gathered"], 16 * NT)
            for t in range(NT):
                dve.scalar_tensor_tensor(c.x[:, t, :], yg[:, t, :], rse[:, t:t + 1], c.x[:, t, :], ALU.mult,
                                         ALU.add).then_inc(z["xout"], 1)

        @block.tensor
        def _(pe):
            xt_tensor(pe, c, s, xn, bank, s.xn)
            pe.wait_ge(z["small"], 64)
            for t in range(NT):
                pe.wait_ge(s.xt, 2 * (t // 4) + 2)
                for kk in range(KC):
                    m = pe.matmul(bank[4][:, E * t:E * t + E], xt[:, kk, t * P:(t + 1) * P], wr[:, kk, :],
                                  start=(kk == 0), stop=(kk == KC - 1))
            m.then_inc(z["logits"], 1)
            pe.wait_ge(z["lg"], 1)
            pe.wait_ge(z["hot"], 1)
            hv = hot[:, :, :].rearrange("p t e -> p (t e)")
            pe.matmul(bank[4][:, 64:128], before[:, :], hv, start=True, stop=True)
            pe.matmul(bank[5][:, 0:64], ones[:, :], hv, start=True, stop=True).then_inc(z["tot"], 1)
            pe.wait_ge(z["posa"], 1)

            def turn():
                for k in range(KC):
                    m = pe.transpose(bank[4][:, k * P:(k + 1) * P], xs[:, k * P:(k + 1) * P], c.ident[:, :])
                m.then_inc(z["xst"], 1)
            pe.wait_ge(z["xs"], 16)
            turn()
            seen = [0]

            def tile(e, i):
                pe.wait_ge(z["xts"], i + 1)
                for m in range(FC):
                    pe.wait_ge(z["act"], i * FC + (m + 1))
                    for kk in range(KC):
                        j = pe.matmul(bank[m % 4][:, 0:P], w1[:, e, kk, m * P:(m + 1) * P],
                                      xts[:, bass.ds(i % 2, 1), kk, :].rearrange("p b n -> p (b n)"),
                                      start=(kk == 0), stop=(kk == KC - 1))
                    j.then_inc(z["hid"], 1)
                    if m == 3:
                        pe.wait_ge(z["xs"], i * 16 + 32)
                        turn()
                pe.wait_ge(z["yb"], i + 1)
                for m in range(FC):
                    pe.wait_ge(z["act"], i * FC + (m + 5))
                    j = pe.matmul(bank[5][:, 0:D], hb[:, m, :], w2[:, e, m, :], start=(m == 0), stop=(m == FC - 1))
                j.then_inc(z["ypr"], 1)

            def body(e, i):
                pe.wait_ge(s_w[e], 32)
                tile(e, i)
            tiles(pe, body)


def build(nc, d, out):
    ctx = ExitStack()
    with ctx:
        c = Names()
        c.d = d

        def sb(name, shape, dt=F32):
            return ctx.enter_context(nc.sbuf_tensor(name, shape, dt))
        c.x = sb("x", [P, NT, D])
        c.ident = sb("ident", [P, P])
        c.identb = sb("identb", [P, P], BF16)
        c.eo = sb("evenodd", [P, 2])
        c.cols = sb("cols", [P, NCOLS])
        c.rows = sb("rows", [P, NROWS])
        c.w = Names()
        c.w.st = sb("ln_st", [P, NT, 6])
        c.w.mv = sb("ln_mv", [P, NT, 2])
        c.w.ve = sb("ln_ve", [P, NT])
        c.w.sd = sb("ln_sd", [P, NT])
        c.w.rs = sb("ln_rs", [P, NT])
        c.col = lambda n, i: c.cols[:, COLS[n][0] + i:COLS[n][0] + i + 1]
        c.row = lambda n, i=0, m=None: c.rows[:, ROWS[n][0] + i:ROWS[n][0] + i + (m or ROWS[n][1])]
        stage_a(nc, c)
        stage_b(nc, c)
        stage_c(nc, c)
        stage_d(nc, c)
        stage_e(nc, c)
        stage_f(nc, c)
        finish(nc, c, out)


def finish(nc, c, out):
    with nc.semaphore("stored") as stored, nc.Block() as block:
        @block.sync
        def _(sp):
            sp.dma_start(out.rearrange("(t p) d -> p t d", p=P), c.x[:, :, :]).then_inc(stored, 16)
            sp.wait_ge(stored, 16)


def kernel(**inputs):
    import numpy as _np
    import concourse.bacc as _bacc
    import ml_dtypes as _ml
    from concourse import mybir as _mybir
    from concourse.bass_utils import run_bass_kernel_spmd as _run

    a = {k: _np.asarray(v) for k, v in inputs.items()}
    col = lambda v: v.reshape(-1, P).T
    mask = _np.ascontiguousarray(a["mask_1x1xSxS2_bk0"][0, 0]).view(_np.uint32)
    cw = _np.concatenate([a["L1_attn_conv_q_w"], a["L1_attn_conv_k_w"], a["L1_attn_conv_v_w"]])
    cols = _np.concatenate(
        [col(a["L0_xattn_bq"]), col(a["L0_xattn_bk"]), col(a["L0_xattn_bv"])]
        + [_np.concatenate([a[n]] * 2).reshape(P, 1) for n in ("L0_attn_q_gamma", "L0_attn_q_beta", "L0_attn_k_gamma",
                                                               "L0_attn_k_beta")]
        + [col(a["L1_xattn_bq"]), col(a["L1_xattn_bk"]), col(a["L1_xattn_bv"]), col(a["L1_attn_ln2_g"]),
           col(a["L1_attn_ln2_b"]), cw.reshape(8, P, 4).transpose(1, 0, 2).reshape(P, 32),
           a["L1_ffn_b1"].reshape(64, P).T], axis=1)
    rows = _np.concatenate([a[n].ravel() for n in (
        "L0_xattn_bo", "L0_ffn_scale", "L0_ffn_bias", "L1_xattn_bo", "L1_attn_ln1_g", "L1_attn_ln1_b",
        "L1_attn_rms_in_w", "L1_attn_b2", "L1_attn_o_norm_w", "L1_attn_dt_bias", "L1_attn_A_log", "L1_ffn_b2",
        "L1_ffn_br")])
    part = _np.arange(P)
    NR = SK // KR
    eye = _np.eye(P, dtype=_np.float32)
    even = (part // HD % 2 == 0)
    i2 = _np.tile(_np.eye(S, dtype=_np.float32), (2, 1))
    s_, t_ = _np.arange(S)[:, None], _np.arange(S)[None, :]
    levels = [(s_ // (2 * n) == t_ // (2 * n)) & (s_ // n % 2 == 0) & (t_ // n % 2 == 1) for n in (1, 2, 4, 8, 16, 32)]
    tab = _np.concatenate([_np.arange(E), _np.tile(P * _np.append(_np.arange(1, NT), N), E),
                           _np.tril(_np.ones((E, E)), -1).ravel()])
    arrays = {
        "x": a["x"].reshape(N, D),
        "ctxt": a["ctx_1024"].transpose(0, 2, 1),
        "mask2": _np.concatenate([mask, mask]),
        "cols": cols, "rows": rows,
        "ident": eye, "identb": eye.astype(_ml.bfloat16),
        "rounds": _np.concatenate([_np.arange(NR) + 2 * NR, _np.arange(NR)])[None].astype(_np.float32),
        "evenodd": _np.stack([even, ~even], 1).astype(_np.float32),
        "a_wq": a["L0_xattn_Wq"], "a_wk": a["L0_xattn_Wk"], "a_wv": a["L0_xattn_Wv"], "a_wo": a["L0_xattn_Wo"],
        "b_wq": a["L0_attn_Wq"].T, "b_wk": a["L0_attn_Wk"].T, "b_wv": a["L0_attn_Wv"].T, "b_wo": a["L0_attn_Wo"].T,
        "causal": _np.kron(_np.eye(2), _np.triu(_np.ones((S, S)))).astype(_np.float32),
        "c_w": a["L0_ffn_weights"].T,
        "d_wq": a["L1_xattn_Wq"].T, "d_wk": a["L1_xattn_Wk"].T, "d_wv": a["L1_xattn_Wv"].T, "d_wo": a["L1_xattn_Wo"].T,
        "causalb": _np.tile(_np.triu(_np.full((S, S), -1e30), 1), (2, 1)).astype(_ml.bfloat16),
        "e_wqkv": _np.concatenate([a["L1_attn_Wq"], a["L1_attn_Wk"], a["L1_attn_Wv"]], axis=1),
        "e_wg": a["L1_attn_Wg"], "e_wab": _np.concatenate([a["L1_attn_Wa"], a["L1_attn_Wb"]], axis=1),
        "e_wo": a["L1_attn_Wo"], "e_w2": a["L1_attn_W2"],
        "i2": i2, "i2z": i2 * (_np.arange(S) > 0).astype(_np.float32),
        "ones64": _np.kron(_np.eye(2), _np.ones((S, S))).astype(_np.float32),
        "levels": _np.tile(_np.stack(levels, 1), (2, 1, 1)).astype(_np.float32),
        "f_w1": a["L1_ffn_W1"], "f_w2": a["L1_ffn_W2"], "f_wr": a["L1_ffn_Wr"],
        "before": _np.triu(_np.ones((P, P)), 1).astype(_np.float32), "ones": _np.ones((P, P), _np.float32),
        "f_tab": _np.tile(tab.astype(_np.float32), (P, 1)),
    }
    nc = _bacc.Bacc("TRN2", target_bir_lowering=False, num_devices=1)
    ins, d = {}, {}
    for name, v in arrays.items():
        v = _np.ascontiguousarray(v)
        ins["in_" + name] = v
        d[name] = nc.dram_tensor("in_" + name, v.shape, _mybir.dt.from_np(v.dtype), kind="ExternalInput").ap()
    out = nc.dram_tensor("out_0_dram", (N, D), _mybir.dt.float32, kind="ExternalOutput").ap()
    build(nc, d, out)
    r = _run(nc, [ins], core_ids=[0])
    return _np.asarray(r.results[0]["out_0_dram"]).reshape(B, S, D)
```

```python
import concourse.bass as bass
from concourse import mybir
from contextlib import ExitStack, contextmanager
import numpy as np

F32 = mybir.dt.float32
BF16 = mybir.dt.bfloat16
U8 = mybir.dt.uint8
U32 = mybir.dt.uint32
ALU = mybir.AluOpType
ACT = mybir.ActivationFunctionType
AXX = mybir.AxisListType.X

P = 128
B, S, D = 16, 64, 256
SK = 1024
N = B * S
NT = N // P
KC = D // P
H, HD = 16, 16
KR = 256
HA, DA = 16, 64
QKV = HA * DA
HG, KD, VD = 4, 64, 128
E, F = 8, 1024
BIG = 1.0e9

COLS, ROWS = {}, {}


def _layout():
    at = 0
    for name, n in (("a_bq", 2), ("a_bk", 2), ("a_bv", 2), ("b_qg", 1), ("b_qb", 1), ("b_kg", 1), ("b_kb", 1),
                    ("d_bq", 2), ("d_bk", 2), ("d_bv", 2), ("e_g2", 2), ("e_b2", 2),
                    ("e_cw", 32), ("f_b1", 64)):
        COLS[name] = (at, n)
        at += n
    COLS["_"] = (at, 0)
    at = 0
    for name, n in (("a_bo", 256), ("c_scale", 256), ("c_bias", 256), ("d_bo", 256), ("e_g1", 256), ("e_b1", 256),
                    ("e_rms", 256), ("e_w2b", 256), ("e_on", 128), ("e_dt", 4), ("e_alog", 4), ("f_b2", 2048),
                    ("f_br", 8)):
        ROWS[name] = (at, n)
        at += n
    ROWS["_"] = (at, 0)


class Names:
    pass


_layout()
NCOLS, NROWS = COLS["_"][0], ROWS["_"][0]


@contextmanager
def stage_semaphores(nc):
    with ExitStack() as ctx:
        taken = []
        ctx.taken = taken
        yield ctx
    nc.clear_and_free_semaphores(taken)
    nc.all_engine_barrier()


def stage_semaphore(nc, ctx, name):
    ctx.taken.append(nc.alloc_semaphore(name))
    return ctx.taken[-1]


def ln_sems(sem, tag):
    s = Names()
    s.stats, s.mv, s.veps, s.std, s.rstd, s.xn, s.tp, s.xt = (
        sem(f"{tag}_{n}") for n in ("stats", "meanvar", "vareps", "std", "rstd", "normed", "transposed", "xt"))
    return s


def ln_vector(dve, c, s, src, dst, w):
    HT = NT // 2
    for g in range(2):
        half = slice(HT * g, HT * g + HT)
        for t in range(HT * g, HT * g + HT):
            dve.bn_stats(w.st[:, t, :], src[:, t, :]).then_inc(s.stats, 1)
        for t in range(HT * g, HT * g + HT):
            dve.wait_ge(s.stats, t + 1)
            dve.bn_aggr(w.mv[:, t, :], w.st[:, t, :]).then_inc(s.mv, 1)
        dve.wait_ge(s.mv, HT * g + HT)
        dve.tensor_scalar(w.ve[:, half], w.mv[:, half, 1], 1e-5, None, ALU.add).then_inc(s.veps, 1)
    for g in range(2):
        half = slice(HT * g, HT * g + HT)
        dve.wait_ge(s.std, g + 1)
        dve.reciprocal(w.rs[:, half], w.sd[:, half]).then_inc(s.rstd, 1)
        dve.wait_ge(s.rstd, g + 1)
        for t in range(HT * g, HT * g + HT):
            dve.tensor_scalar(dst[:, t, :], src[:, t, :], w.mv[:, t, 0:1], w.rs[:, t:t + 1],
                              ALU.subtract, ALU.mult).then_inc(s.xn, 1)


def ln_scalar(act, s, w):
    for g in range(2):
        half = slice(NT // 2 * g, NT // 2 * (g + 1))
        act.wait_ge(s.veps, g + 1)
        act.activation(w.sd[:, half], w.ve[:, half], ACT.Sqrt).then_inc(s.std, 1)


def xt_tensor(pe, c, s, src, banks, ready):
    for g in range(2):
        for k in range(KC):
            for t in range(4 * g, 4 * g + 4):
                if k == 0 and ready is not None:
                    pe.wait_ge(ready, t + 1)
                pe.transpose(banks[2 * g + k][:, (t - 4 * g) * P:(t - 4 * g + 1) * P],
                             src[:, t, k * P:(k + 1) * P], c.ident[:, :]).then_inc(s.tp, 1)


def xt_scalar(act, s, banks, xt, scale=None, bias=None):
    for g in range(2):
        for k in range(KC):
            act.wait_ge(s.tp, 4 * (2 * g + k + 1))
            kw = {} if scale is None else dict(scale=scale[:, k:k + 1], bias=bias[:, k:k + 1])
            act.activation(xt[:, k, g * 512:(g + 1) * 512], banks[2 * g + k][:, :],
                           ACT.Copy if scale is None else ACT.Identity, **kw).then_inc(s.xt, 1)


def stage_a(nc, c):
    with stage_semaphores(nc) as ctx:
        def sb(name, shape, dt=F32):
            return ctx.enter_context(nc.sbuf_tensor("a_" + name, shape, dt))

        def pb(name):
            return ctx.enter_context(nc.psum_tensor("a_" + name, [P, 512], F32))

        def sem(name):
            return stage_semaphore(nc, ctx, "a_" + name)

        w = c.w
        xn = sb("xn", [P, NT, D])
        xt = sb("xt", [P, KC, N])
        wq, wk, wv, wo = (sb(n, [P, KC, D]) for n in ("wq", "wk", "wv", "wo"))
        mask32 = sb("mask32", [P, SK // 4], U32)
        maskf = sb("maskf", [P, SK])
        madd = sb("madd", [P, SK], BF16)
        anyk = sb("anyk", [P, 1])
        anyb = sb("anyb", [P, P])
        seen = sb("seen", [P, SK // KR + 1])
        ones = sb("ones", [P, 1])
        count = sb("count", [1, SK // KR + 1])
        act_r = sb("act_r", [1, SK // KR])
        ends = sb("ends", [1, 2, SK // KR])
        lohi = sb("lohi", [1, 2])
        rng = sb("rng", [1, 2], mybir.dt.int32)
        ri = sb("ri", [1, 2 * (SK // KR)])
        actq = sb("actq", [P, S])
        q = sb("q", [P, KC, N])
        q2 = sb("q2", [P, KC, N])
        qbd = sb("qbd", [P, KC, B, P])
        ct = sb("ct", [P, 2, KC, KR])
        qw = sb("qw", [P, 2, KC, P])
        ks = sb("ks", [P, 2, KC, KR])
        vs = sb("vs", [P, 2, 2, D])
        pr = sb("pr", [P, 2, 4, KC, KR])
        pt = sb("pt", [P, 4, 512])
        nm_step = sb("nm_step", [P, 2, 4, KC])
        negmx = sb("negmx", [P, 2, 4, KC])
        diff = sb("diff", [P, 2, 8])
        alpha = sb("alpha", [P, 2, 8])
        rsum = sb("rsum", [P, 2, 4, KC])
        nm = sb("nm", [P, B, 8])
        lsum = sb("lsum", [P, B, 8])
        linv = sb("linv", [P, B, 8])
        o = sb("o", [P, B, 4, KC, 32])
        on = sb("on", [P, 4, KC, 4, 32])
        tmp = sb("tmp", [P, 2, 4, S])
        ot = sb("ot", [P, KC, B, S])
        bank = [pb(f"bank{i}") for i in range(8)]
        s_bank, t_bank, k_bank, v_bank, o_bank = bank[0:4], bank[4], bank[5], bank[6], bank[7]

        ln = ln_sems(sem, "ln")
        (s_w, s_mask, s_x) = (sem(n) for n in ("weights", "mask", "x"))
        s_ct = [sem("ctx0"), sem("ctx1")]
        names = ("maskf seen ones counts count act_r ends lohi span anyk madd anyb actp actq init qproj qbias qact qbd0 qbd1 kproj kevac vproj vevac qw "
                 "scores negmx nm probs diff nmkept alpha lscaled lsummed transposed pt pv oscaled osummed "
                 "linv onorm otp otmp ot oproj xout xbo b_weights")
        z = {n: sem(n) for n in names.split()}
        NR = SK // KR
        block = ctx.enter_context(nc.Block())

        def span(eng):
            eng.wait_ge(z["span"], 2)
            return (eng.value_load(rng[0:1, 0:1], min_val=0, max_val=NR - 1),
                    eng.value_load(rng[0:1, 1:2], min_val=0, max_val=NR - 1))

        def pairs(eng, body, more):
            body(0, 0, True, False)
            body(1, 1, False, False)
            with eng.Fori(1, more * (B // 2) + (B // 2 - 1)) as i:
                body(2 * i, 0, False, False)
                body(2 * i + 1, 1, False, False)
            body(more * B + (B - 2), 0, False, False)
            body(more * B + (B - 1), 1, False, True)

        @block.sync
        def _(sp):
            sp.dma_start(c.x[:, :, :], c.d["x"].rearrange("(t p) d -> p t d", p=P)).then_inc(s_x, 16)
            sp.dma_start(c.ident[:, :], c.d["ident"]).then_inc(s_w, 16)
            sp.dma_start(c.identb[:, :], c.d["identb"]).then_inc(s_w, 16)
            sp.dma_start(c.eo[:, :], c.d["evenodd"]).then_inc(s_w, 16)
            sp.dma_start(c.cols[:, :], c.d["cols"]).then_inc(s_w, 16)
            for t, n in ((wq, "a_wq"), (wk, "a_wk"), (wv, "a_wv"), (wo, "a_wo")):
                sp.dma_start(t[:, :, :], c.d[n].rearrange("(k p) n -> p k n", p=P)).then_inc(s_w, 16)
            sp.dma_start(c.rows[:, :], c.d["rows"].partition_broadcast(P)).then_inc(s_w, 16)

            r0, more = span(sp)

            def load(s, p, first, last):
                if not (first or (isinstance(s, int) and s < 2)):
                    sp.wait_ge(z["vproj"], s - 1)
                b, r = s % B, (r0 + s // B).with_bounds(min_val=0, max_val=NR - 1)
                sp.dma_start(ct[:, p, :, :], c.d["ctxt"][bass.ds(b, 1), :, bass.ds(r * KR, KR)]
                             .rearrange("b (k p) n -> p (b k) n", p=P)).then_inc(s_ct[p], 16)
            pairs(sp, load, more)
            for t, n in zip(c.b_weights, ("b_wq", "b_wk", "b_wv", "b_wo")):
                sp.dma_start(t[:, :, :], c.d[n].rearrange("(k p) n -> p k n", p=P)).then_inc(z["b_weights"], 16)
            sp.wait_ge(z["b_weights"], 64)

        @block.gpsimd
        def _(pool):
            pool.dma_start(mask32[:, :], c.d["mask2"]).then_inc(s_mask, 16)
            pool.dma_start(ri[:, :], c.d["rounds"]).then_inc(s_mask, 16)
            pool.memset(o[:, :, :, :, :], 0.0).then_inc(z["init"], 1)
            pool.memset(lsum[:, :, :], 0.0).then_inc(z["init"], 1)
            pool.memset(nm[:, :, :], 3.0e38).then_inc(z["init"], 1)
            pool.wait_ge(z["qbd0"], 4)
            pool.wait_ge(z["qbd1"], 4)

            def take(s, p, first, last):
                if not (isinstance(s, int) and s < 2):
                    pool.wait_ge(z["scores"], 4 * s - 4)
                    pool.nop(nofuse=True)
                pool.tensor_copy(qw[:, p, :, :], qbd[:, :, bass.ds(s % B, 1), :].rearrange("p k b n -> p k (b n)")
                                 ).then_inc(z["qw"], 1)
            pairs(pool, take, span(pool)[1])

        @block.scalar
        def _(act):
            ln_scalar(act, ln, w)
            xt_scalar(act, ln, bank, xt)
            for i in range(4):
                k, g = i // 2, i % 2
                act.wait_ge(z["qact"], i + 1)
                src = q2[:, k, g * 512:(g + 1) * 512].rearrange("p (b s) -> p b s", s=S)
                act.activation(qbd[:, k, 8 * g:8 * g + 8, 0:S], src, ACT.Copy, scale=c.eo[:, 0:1]).then_inc(z["qbd0"], 1)
                act.activation(qbd[:, k, 8 * g:8 * g + 8, S:P], src, ACT.Copy, scale=c.eo[:, 1:2]).then_inc(z["qbd1"], 1)

            def keys_out(s, p):
                act.wait_ge(z["kproj"], s + 1)
                if not (isinstance(s, int) and s < 2):
                    act.wait_ge(z["scores"], 4 * s - 4)
                for k in range(KC):
                    i = act.activation(ks[:, p, k, :], k_bank[:, k * KR:(k + 1) * KR], ACT.Identity,
                                       bias=c.col("a_bk", k))
                i.then_inc(z["kevac"], 1)

            def step(s, p, first, last):
                if first:
                    keys_out(0, 0)
                for j in range(4):
                    act.wait_ge(z["nm"], 4 * s + j + 1)
                    for k in range(KC):
                        i = act.activation(pr[:, p, j, k, :], s_bank[j][:, k * KR:(k + 1) * KR], ACT.Exp,
                                           bias=nm_step[:, p, j, k:k + 1], accum_out=rsum[:, p, j, k:k + 1])
                    i.then_inc(z["probs"], 1)
                    if j == 1 and not last:
                        keys_out(s + 1, 1 - p)
                    if j == 2:
                        act.wait_ge(z["vproj"], s + 1)
                        if not (isinstance(s, int) and s < 2):
                            act.wait_ge(z["pv"], s - 1)
                        act.activation(vs[:, p, :, :].rearrange("p a n -> p (a n)"), v_bank[:, :], ACT.Copy).then_inc(z["vevac"], 1)
                act.wait_ge(z["diff"], s + 1)
                act.activation(alpha[:, p, :], diff[:, p, :], ACT.Exp).then_inc(z["alpha"], 1)
            pairs(act, step, span(act)[1])

        @block.vector
        def _(dve):
            dve.memset(ones[:, :], 1.0).then_inc(z["ones"], 1)
            dve.wait_ge(s_mask, 32)
            dve.tensor_copy(maskf[:, :], mask32[:, :].bitcast(U8)).then_inc(z["maskf"], 1)
            dve.wait_ge(z["maskf"], 1)
            dve.reduce_max(anyk[:, :], maskf[:, :], AXX).then_inc(z["anyk"], 1)
            dve.reduce_max(seen[:, 0:NR], maskf[:, :].rearrange("p (r n) -> p r n", n=KR), AXX).then_inc(z["seen"], 1)
            dve.wait_ge(z["anyk"], 1)
            dve.tensor_scalar(seen[:, NR:NR + 1], anyk[:, :], -1.0, 1.0, ALU.mult, ALU.add).then_inc(z["seen"], 1)
            dve.tensor_copy(anyb[:, :], anyk[:, 0:1].to_broadcast([P, P])).then_inc(z["anyb"], 1)
            dve.wait_ge(z["seen"], 2)
            dve.tensor_scalar(maskf[:, :], maskf[:, :], 1.0, BIG, ALU.subtract, ALU.mult).then_inc(z["maskf"], 1)
            dve.wait_ge(z["maskf"], 2)
            dve.tensor_scalar(madd[:, :], maskf[:, :], anyk[:, 0:1], None, ALU.mult).then_inc(z["madd"], 1)
            dve.wait_ge(z["counts"], 1)
            dve.tensor_copy(count[:, :], bank[6][0:1, 0:NR + 1]).then_inc(z["count"], 1)
            dve.wait_ge(z["count"], 1)
            dve.tensor_scalar(act_r[:, :], count[:, 0:NR], count[:, NR:NR + 1], 0.5, ALU.add, ALU.is_ge).then_inc(z["act_r"], 1)
            dve.wait_ge(z["act_r"], 1)
            dve.scalar_tensor_tensor(ends[:, 0, :], act_r[:, :], -2.0 * NR, ri[:, 0:NR], ALU.mult, ALU.add).then_inc(z["ends"], 1)
            dve.tensor_tensor(ends[:, 1, :], act_r[:, :], ri[:, NR:2 * NR], ALU.mult).then_inc(z["ends"], 1)
            dve.wait_ge(z["ends"], 2)
            dve.tensor_reduce(lohi[:, 0:1], ends[:, 0, :], AXX, ALU.min).then_inc(z["lohi"], 1)
            dve.tensor_reduce(lohi[:, 1:2], ends[:, 1, :], AXX, ALU.max).then_inc(z["lohi"], 1)
            dve.wait_ge(z["lohi"], 2)
            dve.tensor_copy(rng[:, 0:1], lohi[:, 0:1]).then_inc(z["span"], 1)
            dve.tensor_tensor(rng[:, 1:2], lohi[:, 1:2], lohi[:, 0:1], ALU.subtract).then_inc(z["span"], 1)
            dve.wait_ge(s_x, 16)
            ln_vector(dve, c, ln, c.x, xn, w)
            dve.wait_ge(z["actp"], 1)
            dve.tensor_copy(actq[:, :], bank[7][:, 0:S]).then_inc(z["actq"], 1)
            dve.wait_ge(s_w, 16 * 9)
            for i in range(4):
                k, g = i // 2, i % 2
                dve.wait_ge(z["qproj"], i + 1)
                dve.tensor_scalar(q[:, k, g * 512:(g + 1) * 512], bank[i][:, :], c.col("a_bq", k), HD ** -0.5,
                                  ALU.add, ALU.mult).then_inc(z["qbias"], 1)
            dve.wait_ge(z["actq"], 1)
            for i in range(4):
                k, g = i // 2, i % 2
                dve.wait_ge(z["qbias"], i + 1)
                dve.tensor_tensor(q2[:, k, g * 512:(g + 1) * 512].rearrange("p (b s) -> p b s", s=S),
                                  q[:, k, g * 512:(g + 1) * 512].rearrange("p (b s) -> p b s", s=S),
                                  actq[:, :].unsqueeze(1).to_broadcast([P, 8, S]), ALU.mult).then_inc(z["qact"], 1)
            dve.wait_ge(z["init"], 3)

            def turned(s, p, j):
                dve.wait_ge(z["transposed"], 4 * s + j + 1)
                dve.tensor_copy(pt[:, j, :], t_bank[:, :]).then_inc(z["pt"], 1)

            def fold(s, p):
                b = s % B
                dve.wait_ge(z["alpha"], s + 1)
                ob = o[:, bass.ds(b, 1), :, :, :].rearrange("p b j k n -> p (b j k) n")
                lb = lsum[:, bass.ds(b, 1), :].rearrange("p b n -> p (b n)")
                dve.tensor_tensor(ob, ob, alpha[:, p, :].unsqueeze(2).to_broadcast([P, 8, 32]),
                                  ALU.mult).then_inc(z["oscaled"], 1)
                dve.tensor_tensor(lb, lb, alpha[:, p, :], ALU.mult).then_inc(z["lscaled"], 1)
                dve.wait_ge(z["oscaled"], s + 1)
                dve.wait_ge(z["pv"], s + 1)
                dve.tensor_tensor(ob, ob, o_bank[:, 0:256].rearrange("p (j n) -> p j n", n=32),
                                  ALU.add).then_inc(z["osummed"], 1)
                dve.wait_ge(z["lscaled"], s + 1)
                dve.tensor_tensor(lb, lb, rsum[:, p, :, :].rearrange("p j k -> p (j k)"), ALU.add).then_inc(z["lsummed"], 1)

            def step(s, p, first, last):
                b = s % B
                for j in range(4):
                    dve.wait_ge(z["scores"], 4 * s + j + 1)
                    dve.tensor_reduce(negmx[:, p, j, :], s_bank[j][:, :].rearrange("p (k n) -> p k n", n=KR),
                                      AXX, ALU.max, negate=True).then_inc(z["negmx"], 1)
                    if not first:
                        turned(s - 1, 1 - p, j)
                    if j == 0 and not first:
                        dve.wait_ge(z["nmkept"], s)
                    dve.wait_ge(z["negmx"], 4 * s + j + 1)
                    dve.tensor_tensor(nm_step[:, p, j, :], negmx[:, p, j, :],
                                      nm[:, bass.ds(b, 1), 2 * j:2 * j + 2].rearrange("p b n -> p (b n)"),
                                      ALU.min).then_inc(z["nm"], 1)
                nb = nm[:, bass.ds(b, 1), :].rearrange("p b n -> p (b n)")
                dve.wait_ge(z["nm"], 4 * s + 4)
                dve.tensor_tensor(diff[:, p, :], nm_step[:, p, :, :].rearrange("p j k -> p (j k)"), nb,
                                  ALU.subtract).then_inc(z["diff"], 1)
                dve.wait_ge(z["diff"], s + 1)
                dve.tensor_scalar(nb, nm_step[:, p, :, :].rearrange("p j k -> p (j k)"), 1.0, None, ALU.mult).then_inc(z["nmkept"], 1)
                if not first:
                    fold(s - 1, 1 - p)
                if last:
                    for j in range(4):
                        turned(s, p, j)
                    fold(s, p)
            more = span(dve)[1]
            pairs(dve, step, more)
            steps = more * B + B

            dve.wait_ge(z["lsummed"], steps)
            dve.reciprocal(linv[:, :, :], lsum[:, :, :]).then_inc(z["linv"], 1)
            dve.wait_ge(z["linv"], 1)
            dve.wait_ge(z["osummed"], steps)
            for g in range(4):
                if g:
                    dve.wait_ge(z["otp"], 2 * g)
                for k in range(KC):
                    for b in range(4 * g, 4 * g + 4):
                        i = dve.tensor_tensor(on[:, b - 4 * g, k, :, :], o[:, b, :, k, :],
                                              linv[:, b, :].rearrange("p (j k) -> p j k", k=KC)[:, :, k].unsqueeze(2)
                                              .to_broadcast([P, 4, 32]), ALU.mult)
                    i.then_inc(z["onorm"], 1)
                for k in range(KC):
                    dve.wait_ge(z["otp"], 2 * g + k + 1)
                    src = bank[k][:, :].rearrange("p (b h s) -> p b h s", b=4, h=2)
                    if g:
                        dve.wait_ge(z["ot"], 2 * g + k - 1)
                    dve.tensor_scalar(tmp[:, k, :, :], src[:, :, 0, :], c.eo[:, 0:1], c.col("a_bv", k), ALU.mult,
                                      ALU.add).then_inc(z["otmp"], 1)
                    dve.wait_ge(z["otmp"], 2 * g + k + 1)
                    dve.scalar_tensor_tensor(ot[:, k, 4 * g:4 * g + 4, :], src[:, :, 1, :], c.eo[:, 1:2],
                                             tmp[:, k, :, :], ALU.mult, ALU.add).then_inc(z["ot"], 1)
            dve.wait_ge(s_w, 16 * 9)
            for t in range(NT):
                dve.tensor_tensor(c.x[:, t, :], c.x[:, t, :], c.row("a_bo"), ALU.add).then_inc(z["xbo"], 1)
            for t in range(NT):
                dve.wait_ge(z["xbo"], t + 1)
                dve.wait_ge(z["oproj"], 2 * (t // 2) + 2)
                dve.tensor_tensor(c.x[:, t, :], c.x[:, t, :], bank[2 + t // 2][:, (t % 2) * D:(t % 2 + 1) * D],
                                  ALU.add).then_inc(z["xout"], 1)

        @block.tensor
        def _(pe):
            pe.wait_ge(z["ones"], 1)
            pe.wait_ge(z["seen"], 2)
            pe.matmul(bank[6][0:1, 0:NR + 1], ones[:, 0:1], seen[:, :], start=True, stop=True).then_inc(z["counts"], 1)
            pe.wait_ge(s_w, 16 * 9)
            pe.wait_ge(z["anyb"], 1)
            xt_tensor(pe, c, ln, xn, bank, ln.xn)
            pe.matmul(bank[7][:, 0:S], anyb[0:S, :], c.ident[0:S, 0:S], start=True, stop=True).then_inc(z["actp"], 1)
            pe.wait_ge(ln.xt, 4)
            for i in range(4):
                k, g = i // 2, i % 2
                for kk in range(KC):
                    m = pe.matmul(bank[i][:, :], wq[:, kk, k * P:(k + 1) * P], xt[:, kk, g * 512:(g + 1) * 512],
                                  start=(kk == 0), stop=(kk == KC - 1))
                m.then_inc(z["qproj"], 1)
            pe.wait_ge(z["qbias"], 4)
            pe.wait_ge(z["madd"], 1)

            r0, more = span(pe)

            def keys(s, p):
                pe.wait_ge(s_ct[p], 8 * s + 16 - 8 * p)
                if not (isinstance(s, int) and s < 1):
                    pe.wait_ge(z["kevac"], s)
                for k in range(KC):
                    for kk in range(KC):
                        m = pe.matmul(k_bank[:, k * KR:(k + 1) * KR], wk[:, kk, k * P:(k + 1) * P], ct[:, p, kk, :],
                                      start=(kk == 0), stop=(kk == KC - 1))
                m.then_inc(z["kproj"], 1)

            def values(s, p):
                if not (isinstance(s, int) and s < 1):
                    pe.wait_ge(z["vevac"], s)
                for a in range(2):
                    for kk in range(KC):
                        m = pe.matmul(v_bank[:, a * D:(a + 1) * D], ct[:, p, kk, a * P:(a + 1) * P], wv[:, kk, :],
                                      start=(kk == 0), stop=(kk == KC - 1))
                m.then_inc(z["vproj"], 1)

            def scores(s, p, j):
                if not (isinstance(s, int) and s < 1):
                    pe.wait_ge(z["probs"], 4 * s - 4 + j + 1)
                for k in range(KC):
                    pe.matmul(s_bank[j][:, k * KR:(k + 1) * KR], c.identb[:, :], madd[:, bass.ds((r0 + s // B).with_bounds(min_val=0, max_val=NR - 1) * KR, KR)],
                              start=(k == 0), stop=False, skip_group_check=True)
                for k in range(KC):
                    m = pe.matmul(s_bank[j][:, k * KR:(k + 1) * KR], qw[32 * j:32 * j + 32, p, k, :],
                                  ks[32 * j:32 * j + 32, p, k, :], start=False, stop=(k == KC - 1),
                                  tile_position=(32 * j, 0), skip_group_check=True)
                m.then_inc(z["scores"], 1)

            def turn(s, p, j):
                if j == 0:
                    if not (isinstance(s, int) and s < 1):
                        pe.wait_ge(z["pt"], 4 * s)
                else:
                    pe.wait_ge(z["pt"], 4 * s + j)
                pe.wait_ge(z["probs"], 4 * s + j + 1)
                for k in range(KC):
                    for a in range(2):
                        m = pe.transpose(t_bank[:, (2 * k + a) * P:(2 * k + a + 1) * P],
                                         pr[:, p, j, k, a * P:(a + 1) * P], c.ident[:, :])
                m.then_inc(z["transposed"], 1)

            def weigh(s, p, j):
                if j == 0:
                    pe.wait_ge(z["vevac"], s + 1)
                    if not (isinstance(s, int) and s < 1):
                        pe.wait_ge(z["osummed"], s)
                pe.wait_ge(z["pt"], 4 * s + j + 1)
                for k in range(KC):
                    for a in range(2):
                        f = k * P + 32 * j
                        m = pe.matmul(o_bank[:, (2 * j + k) * 32:(2 * j + k + 1) * 32],
                                      pt[:, j, (2 * k + a) * P:(2 * k + a + 1) * P], vs[:, p, a, f:f + 32],
                                      start=(a == 0), stop=(a == 1))
                if j == 3:
                    m.then_inc(z["pv"], 1)

            def step(s, p, first, last):
                if first:
                    keys(0, 0)
                pe.wait_ge(z["qw"], s + 1)
                pe.wait_ge(z["kevac"], s + 1)
                for j in range(4):
                    scores(s, p, j)
                    if not first:
                        turn(s - 1, 1 - p, j)
                    if j == 0 and not last:
                        keys(s + 1, 1 - p)
                    if j > 0 and not first:
                        weigh(s - 1, 1 - p, j - 1)
                    if j == 1:
                        values(s, p)
                if not first:
                    weigh(s - 1, 1 - p, 3)
                if last:
                    for j in range(4):
                        turn(s, p, j)
                        weigh(s, p, j)
            pairs(pe, step, more)

            for g in range(4):
                for k in range(KC):
                    pe.wait_ge(z["onorm"], 2 * g + k + 1)
                    if g:
                        pe.wait_ge(z["ot"], 2 * g + k - 1)
                    for b in range(4):
                        m = pe.transpose(bank[k][:, b * P:(b + 1) * P], on[:, b, k, :, :].rearrange("p j n -> p (j n)"), c.ident[:, :])
                    m.then_inc(z["otp"], 1)
            for t in range(NT):
                pe.wait_ge(z["ot"], 2 * (t // 2) + 2)
                for k in range(KC):
                    m = pe.matmul(bank[2 + t // 2][:, (t % 2) * D:(t % 2 + 1) * D],
                                  ot[:, k, 2 * t:2 * t + 2, :].rearrange("p b s -> p (b s)"), wo[:, k, :],
                                  start=(k == 0), stop=(k == KC - 1))
                m.then_inc(z["oproj"], 1)


def stage_kit(nc, ctx, tag, banks=True):
    def sb(name, shape, dt=F32):
        return ctx.enter_context(nc.sbuf_tensor(f"{tag}_{name}", shape, dt))

    def sem(name):
        return stage_semaphore(nc, ctx, f"{tag}_{name}")

    def sems(names):
        return {n: sem(n) for n in names.split()}
    bank = [ctx.enter_context(nc.psum_tensor(f"{tag}_bank{i}", [P, 512], F32)) for i in range(8)] if banks else None
    return sb, sem, sems, bank


def stage_b(nc, c):
    with stage_semaphores(nc) as ctx:
        sb, sem, sems, bank = stage_kit(nc, ctx, "b")
        w = c.w
        xn = sb("xn", [P, NT, D])
        xt = sb("xt", [P, KC, N])
        wq, wk, wv, wo = c.b_weights
        wm = sb("wm", [P, 2, KC * HA])
        cm = sb("causal", [P, P])
        xtt = sb("xtt", [P, 2, KC, P])
        sq = sb("sq", [P, QKV])
        ss = sb("ss", [P, 2, HA])
        sv = sb("sv", [P, 2, HA])
        sd = sb("sd", [P, 2, HA])
        rs = sb("rs", [P, 2, HA])
        qh = sb("qh", [P, 2, QKV])
        kh = sb("kh", [P, 2, QKV])
        v = sb("v", [P, 2, QKV])
        qt = sb("qt", [P, 8, P])
        kt = sb("kt", [P, 8, P])
        sc = sb("sc", [P, 2, 8, P])
        ot = sb("ot", [P, 8, P])
        ln = ln_sems(sem, "ln")
        s_w = sem("weights")
        z = sems("wsum wmean wcent xtt qproj kproj vproj qsq ksq qss kss qve kve qsd ksd qrs krs qh kh v "
                 "qtp ktp qt kt scores masked av ot oproj xout")
        QG, KG = (z["qsq"], z["qss"], z["qve"], z["qsd"], z["qrs"], z["qh"]), (z["ksq"], z["kss"], z["kve"], z["ksd"], z["krs"], z["kh"])
        block = ctx.enter_context(nc.Block())

        def tiles(eng, body):
            body(0, 0, True, False)
            body(1, 1, False, False)
            with eng.Fori(1, NT // 2 - 1) as i:
                body(2 * i, 0, False, False)
                body(2 * i + 1, 1, False, False)
            body(NT - 2, 0, False, False)
            body(NT - 1, 1, False, True)

        @block.sync
        def _(sp):
            sp.dma_start(cm[:, :], c.d["causal"]).then_inc(s_w, 16)

        @block.gpsimd
        def _(pool):
            for i, t in enumerate((wq, wk)):
                pool.wait_ge(z["wmean"], i + 1)
                tv = t[:, :, :].rearrange("p k (h n) -> p (k h) n", n=DA)
                pool.tensor_tensor(tv, tv, wm[:, i, :].unsqueeze(2).to_broadcast([P, KC * HA, DA]),
                                   ALU.add).then_inc(z["wcent"], 1)
            pool.wait_ge(ln.xt, 4)

            def take(s, p, first, last):
                if not (isinstance(s, int) and s < 2):
                    pool.wait_ge(z["vproj"], s - 1)
                pool.tensor_copy(xtt[:, p, :, :], xt[:, :, bass.ds(s * P, P)]).then_inc(z["xtt"], 1)
            tiles(pool, take)

        @block.scalar
        def _(act):
            ln_scalar(act, ln, w)
            xt_scalar(act, ln, bank, xt)

            def squares(s, g, banks, proj, z_sq, z_red):
                act.wait_ge(proj, s + 1)
                if z_red is not None:
                    act.wait_ge(*z_red)
                for i in range(2):
                    a = act.activation(sq[:, i * 512:(i + 1) * 512], banks[i][:, :], ACT.Square)
                a.then_inc(z_sq, 1)

            def root(s, g, z_ve, z_sd):
                act.wait_ge(z_ve, s + 1)
                act.activation(sd[:, g, :], sv[:, g, :], ACT.Sqrt).then_inc(z_sd, 1)

            def turned(s, dst, z_tp, z_t, gname, bname):
                act.wait_ge(z_tp, s + 1)
                for i in range(2):
                    a = act.activation(dst[:, 4 * i:4 * i + 4, :].rearrange("p a n -> p (a n)"), bank[4 + i][:, :],
                                       ACT.Identity, scale=c.col(gname, 0), bias=c.col(bname, 0))
                a.then_inc(z_t, 1)

            def step(s, p, first, last):
                squares(s, 0, bank[0:2], z["qproj"], z["qsq"], None if first else (z["kss"], s))
                if not first:
                    turned(s - 1, qt, z["qtp"], z["qt"], "b_qg", "b_qb")
                root(s, 0, z["qve"], z["qsd"])
                squares(s, 1, bank[2:4], z["kproj"], z["ksq"], (z["qss"], s + 1))
                if not first:
                    turned(s - 1, kt, z["ktp"], z["kt"], "b_kg", "b_kb")
                root(s, 1, z["kve"], z["ksd"])
                act.wait_ge(z["vproj"], s + 1)
                for i in range(2):
                    a = act.activation(v[:, p, i * 512:(i + 1) * 512], bank[i][:, :], ACT.Copy)
                a.then_inc(z["v"], 1)
                if not first:
                    attended(s - 1)
                if last:
                    turned(s, qt, z["qtp"], z["qt"], "b_qg", "b_qb")
                    turned(s, kt, z["ktp"], z["kt"], "b_kg", "b_kb")
                    attended(s)

            def attended(s):
                act.wait_ge(z["av"], s + 1)
                for i in range(2):
                    a = act.activation(ot[:, 4 * i:4 * i + 4, :].rearrange("p a n -> p (a n)"), bank[6 + i][:, :], ACT.Copy)
                a.then_inc(z["ot"], 1)
            tiles(act, step)

        @block.vector
        def _(dve):
            ln_vector(dve, c, ln, c.x, xn, w)
            dve.wait_ge(s_w, 16)
            for i, t in enumerate((wq, wk)):
                dve.reduce_sum(wm[:, i, :], t[:, :, :].rearrange("p k (h n) -> p (k h) n", n=DA), AXX).then_inc(z["wsum"], 1)
                dve.wait_ge(z["wsum"], i + 1)
                dve.tensor_scalar(wm[:, i, :], wm[:, i, :], -1.0 / DA, None, ALU.mult).then_inc(z["wmean"], 1)

            def norm(s, p, g, banks, dst, zs):
                z_sq, z_ss, z_ve, z_sd, z_rs, z_h = zs
                dve.wait_ge(z_sq, s + 1)
                dve.reduce_sum(ss[:, g, :], sq[:, :].rearrange("p (h n) -> p h n", n=DA), AXX).then_inc(z_ss, 1)
                dve.wait_ge(z_ss, s + 1)
                dve.tensor_scalar(sv[:, g, :], ss[:, g, :], 1.0 / DA, 1e-5, ALU.mult, ALU.add).then_inc(z_ve, 1)
                dve.wait_ge(z_sd, s + 1)
                dve.reciprocal(rs[:, g, :], sd[:, g, :]).then_inc(z_rs, 1)
                dve.wait_ge(z_rs, s + 1)
                for i in range(2):
                    a = dve.tensor_tensor(dst[:, p, i * 512:(i + 1) * 512].rearrange("p (h n) -> p h n", n=DA),
                                          banks[i][:, :].rearrange("p (h n) -> p h n", n=DA),
                                          rs[:, g, 8 * i:8 * i + 8].unsqueeze(2).to_broadcast([P, 8, DA]), ALU.mult)
                a.then_inc(z_h, 1)

            def attend(s):
                for half in range(2):
                    dve.wait_ge(z["scores"], 2 * s + half + 1)
                    for par in range(2):
                        a = dve.tensor_tensor(sc[:, par, 4 * half:4 * half + 4, :],
                                              bank[4 + par][:, :].rearrange("p (a n) -> p a n", n=P),
                                              cm[:, :].unsqueeze(1).to_broadcast([P, 4, P]), ALU.mult)
                    a.then_inc(z["masked"], 1)
                dve.wait_ge(z["oproj"], s + 1)
                xs = c.x[:, bass.ds(s, 1), :].rearrange("p a n -> p (a n)")
                dve.tensor_tensor(xs, xs, bank[6][:, 0:D], ALU.add).then_inc(z["xout"], 1)

            def step(s, p, first, last):
                norm(s, p, 0, bank[0:2], qh, QG)
                norm(s, p, 1, bank[2:4], kh, KG)
                if not first:
                    attend(s - 1)
                if last:
                    attend(s)
            tiles(dve, step)

        @block.tensor
        def _(pe):
            xt_tensor(pe, c, ln, xn, bank, ln.xn)
            pe.wait_ge(z["wcent"], 2)
            pe.wait_ge(ln.xt, 4)

            def project(s, p, wt, banks, z_out):
                for i in range(2):
                    for kk in range(KC):
                        m = pe.matmul(banks[i][:, :], xtt[:, p, kk, :], wt[:, kk, i * 512:(i + 1) * 512],
                                      start=(kk == 0), stop=(kk == KC - 1))
                m.then_inc(z_out, 1)

            def turn(p, src, z_tp):
                for i in range(8):
                    m = pe.transpose(bank[4 + i // 4][:, (i % 4) * P:(i % 4 + 1) * P], src[:, p, i * P:(i + 1) * P],
                                     c.ident[:, :])
                m.then_inc(z_tp, 1)

            def turn_q(s, p):
                pe.wait_ge(z["qh"], s + 1)
                if not (isinstance(s, int) and s < 1):
                    pe.wait_ge(z["masked"], 2 * s)
                turn(p, qh, z["qtp"])

            def turn_k(s, p):
                pe.wait_ge(z["kh"], s + 1)
                pe.wait_ge(z["qt"], s + 1)
                turn(p, kh, z["ktp"])

            def scores(s):
                for half in range(2):
                    if half == 0:
                        pe.wait_ge(z["kt"], s + 1)
                    else:
                        pe.wait_ge(z["masked"], 2 * s + 1)
                    for i in range(4):
                        for par in range(2):
                            a = 4 * half + i
                            m = pe.matmul(bank[4 + par][:, i * P:(i + 1) * P], kt[64 * par:64 * par + 64, a, :],
                                          qt[64 * par:64 * par + 64, a, :], start=True, stop=True,
                                          tile_position=(64 * par, 0))
                    m.then_inc(z["scores"], 1)

            def combine(s, p):
                if not (isinstance(s, int) and s < 1):
                    pe.wait_ge(z["xout"], s)
                pe.wait_ge(z["masked"], 2 * s + 2)
                pe.wait_ge(z["v"], s + 1)
                for a in range(8):
                    for par in range(2):
                        m = pe.matmul(bank[6 + a // 4][64 * par:64 * par + 64, (a % 4) * P:(a % 4 + 1) * P],
                                      v[:, p, (2 * a + par) * DA:(2 * a + par + 1) * DA], sc[:, par, a, :],
                                      start=True, stop=True, tile_position=(0, 64 * par))
                m.then_inc(z["av"], 1)
                pe.wait_ge(z["ot"], s + 1)
                for a in range(8):
                    m = pe.matmul(bank[6][:, 0:D], ot[:, a, :], wo[:, a, :], start=(a == 0), stop=(a == 7))
                m.then_inc(z["oproj"], 1)

            def step(s, p, first, last):
                pe.wait_ge(z["xtt"], s + 1)
                if not first:
                    pe.wait_ge(z["v"], s)
                project(s, p, wq, bank[0:2], z["qproj"])
                if not first:
                    turn_q(s - 1, 1 - p)
                    pe.wait_ge(z["kh"], s)
                project(s, p, wk, bank[2:4], z["kproj"])
                if not first:
                    turn_k(s - 1, 1 - p)
                pe.wait_ge(z["qh"], s + 1)
                project(s, p, wv, bank[0:2], z["vproj"])
                if not first:
                    scores(s - 1)
                    combine(s - 1, 1 - p)
                if last:
                    turn_q(s, p)
                    turn_k(s, p)
                    scores(s)
                    combine(s, p)
            tiles(pe, step)


def stage_c(nc, c):
    with stage_semaphores(nc) as ctx:
        sb, sem, sems, bank = stage_kit(nc, ctx, "c")
        w = c.w
        xn = sb("xn", [P, NT, D])
        xt = sb("xt", [P, KC, N])
        wt = sb("wt", [P, KC, D])
        y = sb("y", [P, 4, 2, D])
        ln = ln_sems(sem, "ln")
        z = sems("weights sign binary proj scaled biased clipped xout")
        block = ctx.enter_context(nc.Block())

        @block.sync
        def _(sp):
            sp.dma_start(wt[:, :, :], c.d["c_w"].rearrange("(k p) n -> p k n", p=P)).then_inc(z["weights"], 16)

        @block.scalar
        def _(act):
            ln_scalar(act, ln, w)
            xt_scalar(act, ln, bank, xt)

        @block.vector
        def _(dve):
            ln_vector(dve, c, ln, c.x, xn, w)
            dve.wait_ge(z["weights"], 16)
            dve.tensor_scalar(wt[:, :, :], wt[:, :, :], 0.0, 2.0, ALU.is_ge, ALU.mult).then_inc(z["sign"], 1)
            dve.wait_ge(z["sign"], 1)
            dve.tensor_scalar(wt[:, :, :], wt[:, :, :], 1.0, None, ALU.subtract).then_inc(z["binary"], 1)
            sc = c.row("c_scale").unsqueeze(1).to_broadcast([P, 2, D])
            bi = c.row("c_bias").unsqueeze(1).to_broadcast([P, 2, D])
            for i in range(4):
                ps = bank[4 + i][:, :].rearrange("p (t n) -> p t n", n=D)
                xs = c.x[:, 2 * i:2 * i + 2, :]
                dve.wait_ge(z["proj"], i + 1)
                dve.tensor_tensor(y[:, i, :, :], ps, sc, ALU.mult).then_inc(z["scaled"], 1)
                dve.wait_ge(z["scaled"], i + 1)
                dve.tensor_tensor(y[:, i, :, :], y[:, i, :, :], bi, ALU.add).then_inc(z["biased"], 1)
                dve.wait_ge(z["biased"], i + 1)
                dve.tensor_scalar(y[:, i, :, :], y[:, i, :, :], -100.0, 100.0, ALU.max, ALU.min).then_inc(z["clipped"], 1)
                dve.wait_ge(z["clipped"], i + 1)
                dve.tensor_tensor(xs, xs, y[:, i, :, :], ALU.add).then_inc(z["xout"], 1)

        @block.tensor
        def _(pe):
            xt_tensor(pe, c, ln, xn, bank, ln.xn)
            pe.wait_ge(z["binary"], 1)
            for t in range(NT):
                pe.wait_ge(ln.xt, 2 * (t // 4) + 2)
                for kk in range(KC):
                    m = pe.matmul(bank[4 + t // 2][:, (t % 2) * D:(t % 2 + 1) * D], xt[:, kk, t * P:(t + 1) * P],
                                  wt[:, kk, :], start=(kk == 0), stop=(kk == KC - 1))
                if t % 2:
                    m.then_inc(z["proj"], 1)


def stage_d(nc, c):
    with stage_semaphores(nc) as ctx:
        sb, sem, sems, bank = stage_kit(nc, ctx, "d")
        w = c.w
        G = 4
        NG = B // G
        NH = P // HD
        xn = sb("xn", [P, NT, D])
        xt = sb("xt", [P, KC, N])
        wq, wk, wv, wo = (sb(n, [P, KC, D]) for n in ("wq", "wk", "wv", "wo"))
        cm = sb("causal", [P, S], BF16)
        masks = sb("masks", [P, NH + 2])
        ct = sb("ct", [P, KC, G, 2, S])
        q = sb("q", [P, KC, G * S])
        ks = sb("ks", [P, KC, G * S])
        kbd = sb("kbd", [P, KC, G, NH, S])
        vn = sb("vn", [P, G, D])
        vs = sb("vs", [P, G, D])
        ngm = sb("ngm", [P, 4, NH])
        lsum = sb("lsum", [P, 4, NH])
        linv = sb("linv", [P, 4, NH])
        sh = sb("sh", [P, 4, 512])
        pr = sb("pr", [P, 4, 512])
        pt = sb("pt", [P, 4, 512])
        on = sb("on", [P, 2, KC, P])
        ot = sb("ot", [P, KC, 2, P])
        ln = ln_sems(sem, "ln")
        zero = sb("zero", [P, 3 * D])
        z = sems("zero cleared weights ctx xbo qproj kproj vproj q ks kspread0 kspread1 vn vs scores negmx shifted "
                 "probs lsum linv tp pt pv onorm otp ot oproj xout")
        block = ctx.enter_context(nc.Block())

        @block.sync
        def _(sp):
            for t, n in ((wq, "d_wq"), (wk, "d_wk"), (wv, "d_wv"), (wo, "d_wo")):
                sp.dma_start(t[:, :, :], c.d[n].rearrange("(k p) n -> p k n", p=P)).then_inc(z["weights"], 16)
            sp.dma_start(cm[:, :], c.d["causalb"]).then_inc(z["weights"], 16)
            sp.dma_start(masks[:, :], c.d["d_masks"]).then_inc(z["weights"], 16)

            def load(g):
                for k in range(KC):
                    for r in range(2):
                        sp.dma_start(ct[:, k, :, r, :], c.d["ctxt"][bass.ds(g * G, G), k * P:(k + 1) * P, 0:S]
                                     .rearrange("b p n -> p b n")).then_inc(z["ctx"], 16)
            load(0)
            with sp.Fori(1, NG) as g:
                sp.wait_ge(z["vproj"], g)
                load(g)
            sp.wait_ge(z["cleared"], 32)

        def spread(eng, g, k, done):
            return eng.tensor_tensor(
                kbd[:, k, :, :, :], ks[:, k, :].rearrange("p (b s) -> p b s", s=S).unsqueeze(2).to_broadcast([P, G, NH, S]),
                masks[:, 0:NH].unsqueeze(1).unsqueeze(3).to_broadcast([P, G, NH, S]), ALU.mult).then_inc(done, 1)

        @block.gpsimd
        def _(pool):
            pool.memset(zero[:, :], 0.0).then_inc(z["zero"], 1)
            pool.wait_ge(z["zero"], 1)
            for slots in (c.slots_x, c.slots_y):
                pool.dma_start(slots[0:MAXT * P, :].rearrange("(p a r) d -> p a (r d)", a=MAXT // 3, r=3),
                               zero[:, :].unsqueeze(1).to_broadcast([P, MAXT // 3, 3 * D])).then_inc(z["cleared"], 16)

            def front(g, first):
                pool.wait_ge(z["ks"], g + 1)
                if not first:
                    pool.wait_ge(z["scores"], 4 * g)
                pool.nop(nofuse=True)
                spread(pool, g, 1, z["kspread1"])
                pool.wait_ge(z["vn"], g + 1)
                if not first:
                    pool.wait_ge(z["pv"], g)
                pool.nop(nofuse=True)
                pool.tensor_copy(vs[:, :, :], vn[:, :, :]).then_inc(z["vs"], 1)
            pool.wait_ge(z["weights"], 96)
            front(0, True)
            with pool.Fori(1, NG) as g:
                front(g, False)

        @block.scalar
        def _(act):
            ln_scalar(act, ln, w)
            xt_scalar(act, ln, bank, xt)

            def front(g, first):
                act.wait_ge(z["kproj"], g + 1)
                if not first:
                    act.wait_ge(z["kspread0"], g)
                    act.wait_ge(z["kspread1"], g)
                for k in range(KC):
                    a = act.activation(ks[:, k, :], bank[1][:, k * 256:(k + 1) * 256], ACT.Identity, bias=c.col("d_bk", k))
                a.then_inc(z["ks"], 1)
                act.wait_ge(z["vproj"], g + 1)
                if not first:
                    act.wait_ge(z["vs"], g)
                for i in range(2):
                    for r in range(2):
                        a = act.activation(vn[:, 2 * i:2 * i + 2, :].rearrange("p b (a r n) -> p (b a) r n", r=2, n=HD)[:, :, r, :],
                                           bank[2 + i][:, :].rearrange("p (a r n) -> p a r n", r=2, n=HD)[:, :, r, :],
                                           ACT.Copy, scale=masks[:, NH + r:NH + r + 1])
                a.then_inc(z["vn"], 1)

            def weigh(g, first):
                for j in range(4):
                    act.wait_ge(z["shifted"], 4 * g + j + 1)
                    if not first:
                        act.wait_ge(z["lsum"], 4 * g + j - 3)
                    act.activation(pr[:, j, :], sh[:, j, :], ACT.Exp).then_inc(z["probs"], 1)

            def turn(g, last):
                if not last:
                    front(g + 1, False)
                for j in range(4):
                    act.wait_ge(z["tp"], 4 * g + j + 1)
                    act.activation(pt[:, j, :], bank[3][:, :], ACT.Copy).then_inc(z["pt"], 1)
                if not last:
                    weigh(g + 1, False)
                act.wait_ge(z["otp"], g + 1)
                for k in range(KC):
                    a = act.activation(ot[:, k, :, :].rearrange("p t n -> p (t n)"), bank[3][:, k * 256:(k + 1) * 256],
                                       ACT.Identity, bias=c.col("d_bv", k))
                a.then_inc(z["ot"], 1)
            act.wait_ge(z["weights"], 96)
            front(0, True)
            weigh(0, True)
            turn(0, False)
            with act.Fori(1, NG - 1) as g:
                turn(g, False)
            turn(NG - 1, True)

        @block.vector
        def _(dve):
            ln_vector(dve, c, ln, c.x, xn, w)
            dve.wait_ge(ln.xn, NT)
            for t in range(NT):
                dve.tensor_tensor(c.x[:, t, :], c.x[:, t, :], c.row("d_bo"), ALU.add).then_inc(z["xbo"], 1)
            dve.wait_ge(z["xbo"], NT)

            def front(g, first):
                dve.wait_ge(z["qproj"], g + 1)
                if not first:
                    dve.wait_ge(z["scores"], 4 * g)
                for k in range(KC):
                    a = dve.tensor_scalar(q[:, k, :], bank[0][:, k * 256:(k + 1) * 256], c.col("d_bq", k), HD ** -0.5,
                                          ALU.add, ALU.mult)
                a.then_inc(z["q"], 1)
                dve.wait_ge(z["ks"], g + 1)
                spread(dve, g, 0, z["kspread0"])

            def shift(g):
                for j in range(4):
                    dve.wait_ge(z["scores"], 4 * g + j + 1)
                    s4 = bank[4 + j][:, :].rearrange("p (a n) -> p a n", n=S)
                    dve.tensor_reduce(ngm[:, j, :], s4, AXX, ALU.max, negate=True).then_inc(z["negmx"], 1)
                    dve.wait_ge(z["negmx"], 4 * g + j + 1)
                    dve.tensor_tensor(sh[:, j, :].rearrange("p (a n) -> p a n", n=S), s4,
                                      ngm[:, j, :].unsqueeze(2).to_broadcast([P, NH, S]), ALU.add).then_inc(z["shifted"], 1)

            def turn(g, last):
                if not last:
                    front(g + 1, False)
                for j in range(4):
                    dve.wait_ge(z["probs"], 4 * g + j + 1)
                    dve.reduce_sum(lsum[:, j, :], pr[:, j, :].rearrange("p (a n) -> p a n", n=S), AXX).then_inc(z["lsum"], 1)
                dve.wait_ge(z["lsum"], 4 * g + 4)
                dve.reciprocal(linv[:, :, :], lsum[:, :, :]).then_inc(z["linv"], 1)
                if not last:
                    shift(g + 1)
                dve.wait_ge(z["linv"], g + 1)
                dve.wait_ge(z["pv"], g + 1)
                for bb in range(2):
                    li = linv[:, :, :].rearrange("p (k b) h -> p b k h", b=2)[:, bb, :, :]
                    a = dve.tensor_tensor(on[:, bb, :, :].rearrange("p k (h n) -> p k h n", n=HD),
                                          bank[1][:, bb * D:(bb + 1) * D].rearrange("p (k h n) -> p k h n", k=KC, n=HD),
                                          li.unsqueeze(3).to_broadcast([P, KC, NH, HD]), ALU.mult)
                a.then_inc(z["onorm"], 1)
                dve.wait_ge(z["oproj"], g + 1)
                xs = c.x[:, bass.ds(2 * g, 2), :]
                dve.tensor_tensor(xs, xs, bank[0][:, :].rearrange("p (t n) -> p t n", n=D), ALU.add).then_inc(z["xout"], 1)
            dve.wait_ge(z["weights"], 96)
            front(0, True)
            shift(0)
            turn(0, False)
            with dve.Fori(1, NG - 1) as g:
                turn(g, False)
            turn(NG - 1, True)

        @block.tensor
        def _(pe):
            xt_tensor(pe, c, ln, xn, bank, ln.xn)
            pe.wait_ge(ln.xt, 4)
            pe.wait_ge(z["weights"], 96)

            def front(g):
                first = isinstance(g, int) and g == 0
                if not isinstance(g, int) or g > 1:
                    pe.wait_ge(z["xout"], g - 1)
                for k in range(KC):
                    for kk in range(KC):
                        m = pe.matmul(bank[0][:, k * 256:(k + 1) * 256], wq[:, kk, k * P:(k + 1) * P],
                                      xt[:, kk, bass.ds(g * G * S, G * S)], start=(kk == 0), stop=(kk == KC - 1))
                m.then_inc(z["qproj"], 1)
                pe.wait_ge(z["ctx"], 64 * g + 64)
                for k in range(KC):
                    for kk in range(KC):
                        m = pe.matmul(bank[1][:, k * 256:(k + 1) * 256].rearrange("p (b s) -> p b s", s=S), wk[:, kk, k * P:(k + 1) * P],
                                      ct[:, kk, :, 0, :], start=(kk == 0), stop=(kk == KC - 1))
                m.then_inc(z["kproj"], 1)
                if not first:
                    pe.wait_ge(z["vn"], g)
                for b in range(G):
                    for kk in range(KC):
                        m = pe.matmul(bank[2 + b // 2][:, (b % 2) * D:(b % 2 + 1) * D],
                                      ct[:, kk, b, :, :].rearrange("p r s -> p (r s)"), wv[:, kk, :],
                                      start=(kk == 0), stop=(kk == KC - 1))
                m.then_inc(z["vproj"], 1)
                for j in range(4):
                    if not first:
                        pe.wait_ge(z["shifted"], 4 * g)
                    pe.matmul(bank[4 + j][:, :].rearrange("p (a n) -> p a n", n=S), c.identb[:, :],
                              cm[:, :].unsqueeze(1).to_broadcast([P, NH, S]), start=True, stop=False, skip_group_check=True)
                pe.wait_ge(z["q"], g + 1)
                for k in range(KC):
                    pe.wait_ge(z[f"kspread{k}"], g + 1)
                    for bb in range(2):
                        for b2 in range(2):
                            b = 2 * bb + b2
                            m = pe.matmul(bank[4 + 2 * k + bb][64 * b2:64 * b2 + 64, :], q[:, k, b * S:(b + 1) * S],
                                          kbd[:, k, b, :, :].rearrange("p h s -> p (h s)"), start=False, stop=True,
                                          tile_position=(0, 64 * b2), skip_group_check=True)
                        m.then_inc(z["scores"], 1)

            def back(g, last):
                if not last:
                    pe.wait_ge(z["vn"], g + 2)
                for j in range(4):
                    pe.wait_ge(z["probs"], 4 * g + j + 1)
                    if j:
                        pe.wait_ge(z["pt"], 4 * g + j)
                    for a in range(4):
                        m = pe.transpose(bank[3][:, a * P:(a + 1) * P], pr[:, j, a * P:(a + 1) * P], c.ident[:, :])
                    m.then_inc(z["tp"], 1)
                pe.wait_ge(z["vs"], g + 1)
                for k in range(KC):
                    for bb in range(2):
                        j = 2 * k + bb
                        pe.wait_ge(z["pt"], 4 * g + j + 1)
                        for a in range(4):
                            for b2 in range(2):
                                m = pe.matmul(bank[1][64 * b2:64 * b2 + 64, bb * D + k * P + 32 * a:bb * D + k * P + 32 * a + 32],
                                              pt[:, j, a * P + 64 * b2:a * P + 64 * b2 + 64],
                                              vs[:, 2 * bb + b2, k * P + 32 * a:k * P + 32 * a + 32], start=True, stop=True,
                                              tile_position=(0, 64 * b2))
                m.then_inc(z["pv"], 1)
                pe.wait_ge(z["onorm"], g + 1)
                for k in range(KC):
                    for bb in range(2):
                        m = pe.transpose(bank[3][:, (2 * k + bb) * P:(2 * k + bb + 1) * P], on[:, bb, k, :], c.ident[:, :])
                m.then_inc(z["otp"], 1)
                pe.wait_ge(z["ot"], g + 1)
                for t in range(2):
                    for kk in range(KC):
                        m = pe.matmul(bank[0][:, t * D:(t + 1) * D], ot[:, kk, t, :], wo[:, kk, :],
                                      start=(kk == 0), stop=(kk == KC - 1))
                m.then_inc(z["oproj"], 1)
            front(0)
            front(1)
            back(0, False)
            with pe.Fori(2, NG) as g:
                front(g)
                back(g - 1, False)
            pe.wait_ge(z["xout"], NG - 1)
            back(NG - 1, True)


MAXT = E - 1 + N // P
LEVELS = 6
LOG1P = [1 / 13, 1 / 11, 1 / 9, 1 / 7, 1 / 5, 1 / 3]


def stage_e(nc, c):
    with stage_semaphores(nc) as ctx:
        sb, sem, sems, _ = stage_kit(nc, ctx, "e", banks=False)
        ps = ctx.enter_context(nc.psum_tensor("e_ps", [P, 4096], F32))
        bank = [ps[:, i * 512:(i + 1) * 512] for i in range(8)]
        NB = NT * HG
        w = c.w
        xn = sb("xn", [P, NT, D])
        xl = sb("xl", [P, NT, D])
        h = sb("h", [P, NT, D])
        ht = sb("ht", [P, KC, N])
        wqkv = sb("wqkv", [P, KC, 1024])
        wg = sb("wg", [P, KC, 512])
        wab = sb("wab", [P, KC, 8])
        wo = sb("wo", [P, HG, D])
        w2 = sb("w2", [P, KC, D])
        i2 = sb("i2", [P, S])
        i2z = sb("i2z", [P, S])
        ones = sb("ones", [P, P])
        mt = sb("mt", [P, LEVELS, S])
        i2rep = sb("i2rep", [P, NB, S])
        ms = sb("ms", [P, NT])
        mroot = sb("mroot", [P, NT])
        mrs = sb("mrs", [P, NT])
        cv = sb("cv", [P, 2, B, S])
        lm = cv[:, :, :, :].rearrange("p a b s -> p (a b) s")
        y = xn[:, :, :].rearrange("p t (a s) -> p (t a) s", s=S)
        da = h[:, :, :].rearrange("p t (a s) -> p (t a) s", s=S)
        qkv = sb("qkv", [P, 8, N])
        gate = sb("gate", [P, NT, HG, VD])
        gw = sb("gw", [P, NT, HG, VD])
        u, nabs, ex, den, rden, zz, z2, po, re, sp, dec, beta = (
            sb(n, [P, NT, HG]) for n in "u nabs ex den rden zz z2 po re sp dec beta".split())
        ea = sb("ea", [P, HG])
        eps = sb("eps", [P, 3])
        dt = sb("dt", [P, NB, S])
        dts = sb("dts", [P, NB, S])
        x_ = sb("xinv", [P, NB, S])
        xT = sb("xinvT", [P, NB, S])
        lT, aT = dts, dt
        bv = qkv[:, 0:4, :].rearrange("p a (t h n) -> p (a t) h n", h=HG, n=VD)
        de = gate
        oss = sb("oss", [P, NB])
        osd = sb("osd", [P, NB])
        ors = sb("ors", [P, NB])
        x1 = wqkv[:, :, :].rearrange("p k (t n) -> p (k t) n", n=D)
        pairs_of = lambda flat: flat.rearrange("p (a n) -> p a n", n=P)
        abd = (pairs_of(ht[:, :, :].rearrange("p k n -> p (k n)")), pairs_of(i2rep[:, :, :].rearrange("p a n -> p (a n)")))
        xbd = (pairs_of(h[:, :, :].rearrange("p t n -> p (t n)")), pairs_of(wqkv[:, :, :].rearrange("p k n -> p (k n)")))
        l0, ln, l2 = ln_sems(sem, "l0"), ln_sems(sem, "ln"), ln_sems(sem, "l2")
        z = sems("weights consts eps h0 h1 hsq hms hroot hrs h i2rep proj conv qkv gate gw ab u nabs ex den rden zz "
                 "z2 po lp re sp ea g dec beta da dabc scan db dbbc dts sq ss root rrec qk kk lT aT lm bdz abd y yout zx xx tap xt0 "
                 "xt vt bv dl de o osq oss osv osd ors on og ogt ogs enc x1 xs f2 b2 gel xout initx")
        block = ctx.enter_context(nc.Block())

        def blk(t, hh):
            return (hh % 2) * 16 + t * 2 + hh // 2

        def ordered():
            for hh in range(HG):
                for t in range(NT):
                    yield t, hh, 0
                    yield (t + 4) % NT, (hh + 2) % HG, 1

        @block.sync
        def _(sp_):
            for t, n in ((wqkv, "e_wqkv"), (wg, "e_wg"), (wab, "e_wab"), (wo, "e_wo"), (w2, "e_w2")):
                sp_.dma_start(t[:, :, :], c.d[n].rearrange("(k p) n -> p k n", p=P)).then_inc(z["weights"], 16)
            for t, n in ((i2, "i2"), (i2z, "i2z"), (ones, "ones64")):
                sp_.dma_start(t[:, :], c.d[n]).then_inc(z["consts"], 16)
            sp_.dma_start(mt[:, :, :], c.d["levels"]).then_inc(z["consts"], 16)

        @block.gpsimd
        def _(pool):
            pool.memset(eps[:, 0:1], 1e-6).then_inc(z["eps"], 1)
            pool.memset(eps[:, 1:2], 64e-6).then_inc(z["eps"], 1)
            pool.wait_ge(z["consts"], 64)
            pool.tensor_copy(i2rep[:, :, :], i2[:, :].unsqueeze(1).to_broadcast([P, NB, S])).then_inc(z["i2rep"], 1)
            pool.tensor_copy(x_[:, :, :], i2[:, :].unsqueeze(1).to_broadcast([P, NB, S])).then_inc(z["initx"], 1)
            pool.tensor_copy(xT[:, :, :], i2[:, :].unsqueeze(1).to_broadcast([P, NB, S])).then_inc(z["initx"], 1)
            for t in range(NT):
                pool.wait_ge(z["gate"], t + 1)
                pool.tensor_tensor(gw[:, t, :, :], gate[:, t, :, :],
                                   c.row("e_on").unsqueeze(1).to_broadcast([P, HG, VD]), ALU.mult).then_inc(z["gw"], 1)
            pool.wait_ge(z["aT"], 1)
            pool.wait_ge(z["lT"], 1)
            for a in abd + xbd:
                pool.memset(a, 0.0).then_inc(z["bdz"], 1)
            pool.wait_ge(z["bdz"], 4)
            for r in range(2):
                for b2 in range(2):
                    rows = slice(64 * b2, 64 * b2 + 64)
                    pool.tensor_copy(abd[r][rows, :, rows], aT[rows, 16 * r:16 * r + 16, :]).then_inc(z["abd"], 1)
            for t in range(NT):
                pool.wait_ge(z["x1"], t + 1)
                pool.tensor_tensor(c.x[:, t, :], c.x[:, t, :], x1[:, t, :], ALU.add).then_inc(z["xs"], 1)

        @block.scalar
        def _(act):
            ln_scalar(act, l0, w)
            ln_scalar(act, ln, w)
            for t in range(NT):
                act.wait_ge(z["h1"], t + 1)
                act.activation(xn[:, t, :], h[:, t, :], ACT.Square, accum_out=ms[:, t:t + 1]).then_inc(z["hsq"], 1)
            act.wait_ge(z["hms"], 1)
            act.activation(mroot[:, :], ms[:, :], ACT.Sqrt).then_inc(z["hroot"], 1)
            xt_scalar(act, ln, bank, ht)
            for m in range(9):
                if m < 8:
                    act.wait_ge(z["proj"], m + 1)
                    if m > 1:
                        act.wait_ge(z["qkv"], m - 1)
                    at = 1024 * ((m + 2) % 4)
                    act.activation(cv[:, m % 2, :, :].rearrange("p b s -> p (b s)"), ps[:, at:at + 1024], ACT.Copy,
                                   scale=c.col("e_cw", 4 * m + 3)).then_inc(z["tap"], 1)
                if m:
                    act.wait_ge(z["conv"], m)
                    act.activation(qkv[:, m - 1, :], cv[:, (m - 1) % 2, :, :].rearrange("p b s -> p (b s)"), ACT.Silu
                                   ).then_inc(z["qkv"], 1)
            act.wait_ge(z["ab"], 1)
            act.activation(beta[:, :, :], bank[4][:, 0:64].rearrange("p (t n) -> p t n", n=8)[:, :, 4:8],
                           ACT.Sigmoid).then_inc(z["beta"], 1)
            act.activation(ea[:, :], c.row("e_alog"), ACT.Exp).then_inc(z["ea"], 1)
            act.wait_ge(z["nabs"], 1)
            act.activation(ex[:, :, :], nabs[:, :, :], ACT.Exp).then_inc(z["ex"], 1)
            for t in range(NT):
                act.wait_ge(z["proj"], 8 + t + 1)
                act.activation(gate[:, t, :, :].rearrange("p h n -> p (h n)"), bank[t % 4], ACT.Silu).then_inc(z["gate"], 1)
            act.wait_ge(z["g"], 1)
            act.activation(dec[:, :, :], sp[:, :, :], ACT.Exp).then_inc(z["dec"], 1)
            act.wait_ge(z["eps"], 2)
            for m in range(4):
                act.wait_ge(z["qkv"], m + 1)
                if m:
                    act.wait_ge(z["ss"], m)
                act.activation(cv[:, 0, :, :].rearrange("p b s -> p (b s)"), qkv[:, m, :], ACT.Square).then_inc(z["sq"], 1)
                act.wait_ge(z["ss"], m + 1)
                if m:
                    act.wait_ge(z["rrec"], m)
                act.activation(cv[:, 1, :, :].rearrange("p b s -> p (b s)"), ps[:, 1024 * (m % 2):1024 * (m % 2) + 1024],
                               ACT.Sqrt, scale=64.0 if m < 2 else 1.0, bias=eps[:, 1:2] if m < 2 else eps[:, 0:1]
                               ).then_inc(z["root"], 1)
            with act.Fori(1, LEVELS) as lv:
                for g in range(4):
                    act.wait_ge(z["y"], 4 * lv + g + 1)
                    act.activation(y[:, 8 * g:8 * g + 8, :].rearrange("p a n -> p (a n)"), bank[g], ACT.Copy).then_inc(z["yout"], 1)
            act.wait_ge(z["gw"], NT)
            for t in range(NT):
                act.wait_ge(z["dl"], t + 1)
                act.activation(de[:, t, :, :].rearrange("p h n -> p (h n)"), bank[t], ACT.Copy).then_inc(z["de"], 1)
            for t in range(NT):
                act.wait_ge(z["o"], t + 1)
                act.activation(bv[:, t, :, :].rearrange("p h n -> p (h n)"), bank[t], ACT.Square).then_inc(z["osq"], 1)
            act.wait_ge(z["oss"], NT)
            act.activation(osd[:, :], oss[:, :], ACT.Sqrt, scale=1.0 / VD, bias=eps[:, 0:1]).then_inc(z["osd"], 1)
            for t in range(NT):
                act.wait_ge(z["ogt"], t + 1)
                act.activation(de[:, t, :, :].rearrange("p h n -> p (h n)"), bank[t], ACT.Copy).then_inc(z["ogs"], 1)
            ln_scalar(act, l2, w)
            xt_scalar(act, l2, bank, ht, c.cols[:, COLS["e_g2"][0]:COLS["e_g2"][0] + 2],
                      c.cols[:, COLS["e_b2"][0]:COLS["e_b2"][0] + 2])
            for t in range(NT):
                act.wait_ge(z["b2"], t + 1)
                act.activation(xn[:, t, :], h[:, t, :], ACT.Gelu).then_inc(z["gel"], 1)

        @block.vector
        def _(dve):
            ln_vector(dve, c, l0, c.x, xl, w)
            dve.wait_ge(l0.xn, NT)
            ln_vector(dve, c, ln, xl, xn, w)
            for t in range(NT):
                dve.wait_ge(ln.xn, t + 1)
                dve.tensor_tensor(h[:, t, :], xn[:, t, :], c.row("e_g1"), ALU.mult).then_inc(z["h0"], 1)
            for t in range(NT):
                dve.wait_ge(z["h0"], t + 1)
                dve.tensor_tensor(h[:, t, :], h[:, t, :], c.row("e_b1"), ALU.add).then_inc(z["h1"], 1)
            dve.wait_ge(z["hsq"], NT)
            dve.tensor_scalar(ms[:, :], ms[:, :], 1.0 / D, 1e-6, ALU.mult, ALU.add).then_inc(z["hms"], 1)
            dve.wait_ge(z["hroot"], 1)
            dve.reciprocal(mrs[:, :], mroot[:, :]).then_inc(z["hrs"], 1)
            dve.wait_ge(z["hrs"], 1)
            for t in range(NT):
                dve.scalar_tensor_tensor(h[:, t, :], h[:, t, :], mrs[:, t:t + 1], c.row("e_rms"), ALU.mult,
                                         ALU.mult).then_inc(z["h"], 1)
            for m in range(8):
                src = ps[:, 1024 * ((m + 2) % 4):1024 * ((m + 2) % 4) + 1024].rearrange("p (b s) -> p b s", s=S)
                o_ = cv[:, m % 2, :, :]
                dve.wait_ge(z["tap"], m + 1)
                for back in range(1, 4):
                    if back > 1:
                        dve.wait_ge(z["xx"], 2 * m + back - 1)
                    i = dve.scalar_tensor_tensor(o_[:, :, back:S], src[:, :, 0:S - back], c.col("e_cw", 4 * m + 3 - back),
                                                 o_[:, :, back:S], ALU.mult, ALU.add)
                    i.then_inc(z["xx"] if back < 3 else z["conv"], 1)
            dve.wait_ge(z["ab"], 1)
            dve.wait_ge(z["beta"], 1)
            dve.tensor_tensor(u[:, :, :], bank[4][:, 0:64].rearrange("p (t n) -> p t n", n=8)[:, :, 0:4],
                              c.row("e_dt").unsqueeze(1).to_broadcast([P, NT, HG]), ALU.add).then_inc(z["u"], 1)
            dve.wait_ge(z["u"], 1)
            dve.tensor_scalar(re[:, :, :], u[:, :, :], 0.0, None, ALU.max).then_inc(z["re"], 1)
            dve.wait_ge(z["re"], 1)
            dve.scalar_tensor_tensor(nabs[:, :, :], re[:, :, :], -2.0, u[:, :, :], ALU.mult, ALU.add).then_inc(z["nabs"], 1)
            dve.wait_ge(z["ex"], 1)
            dve.tensor_scalar(den[:, :, :], ex[:, :, :], 2.0, None, ALU.add).then_inc(z["den"], 1)
            dve.wait_ge(z["den"], 1)
            dve.reciprocal(rden[:, :, :], den[:, :, :]).then_inc(z["rden"], 1)
            dve.wait_ge(z["rden"], 1)
            dve.tensor_tensor(zz[:, :, :], ex[:, :, :], rden[:, :, :], ALU.mult).then_inc(z["zz"], 1)
            dve.wait_ge(z["zz"], 1)
            dve.tensor_tensor(z2[:, :, :], zz[:, :, :], zz[:, :, :], ALU.mult).then_inc(z["z2"], 1)
            dve.wait_ge(z["z2"], 1)
            dve.tensor_scalar(po[:, :, :], z2[:, :, :], 1 / 15, None, ALU.mult).then_inc(z["po"], 1)
            for i, k in enumerate(LOG1P):
                dve.wait_ge(z["po"], i + 1)
                dve.scalar_tensor_tensor(po[:, :, :], po[:, :, :], k, z2[:, :, :], ALU.add, ALU.mult).then_inc(z["po"], 1)
            dve.wait_ge(z["po"], len(LOG1P) + 1)
            dve.scalar_tensor_tensor(po[:, :, :], po[:, :, :], 1.0, zz[:, :, :], ALU.add, ALU.mult).then_inc(z["lp"], 1)
            dve.wait_ge(z["lp"], 1)
            dve.wait_ge(z["re"], 1)
            dve.scalar_tensor_tensor(sp[:, :, :], po[:, :, :], 2.0, re[:, :, :], ALU.mult, ALU.add).then_inc(z["sp"], 1)
            dve.wait_ge(z["sp"], 1)
            dve.wait_ge(z["ea"], 1)
            dve.scalar_tensor_tensor(sp[:, :, :], sp[:, :, :], -1.0, ea[:, :].unsqueeze(1).to_broadcast([P, NT, HG]),
                                     ALU.mult, ALU.mult).then_inc(z["g"], 1)

            def spread(dst, eye, val, s_):
                for r in range(2):
                    i = dve.tensor_tensor(
                        dst[:, 16 * r:16 * r + 16, :].rearrange("p (t c) n -> p t c n", c=2),
                        eye[:, :].unsqueeze(1).unsqueeze(1).to_broadcast([P, NT, 2, S]),
                        val[:, :, :].rearrange("p t (c r) -> p r t c", r=2)[:, r, :, :].unsqueeze(3)
                        .to_broadcast([P, NT, 2, S]), ALU.mult)
                i.then_inc(s_, 1)
            dve.wait_ge(z["consts"], 64)
            dve.wait_ge(z["dec"], 1)
            spread(da, i2z, dec, z["da"])
            dve.wait_ge(z["beta"], 1)
            spread(dts, i2, beta, z["db"])
            for m in range(4):
                dve.wait_ge(z["root"], m + 1)
                if m:
                    dve.wait_ge(z["qk"], m)
                pp = ps[:, 1024 * (m % 2):1024 * (m % 2) + 1024]
                dve.reciprocal(pp, cv[:, 1, :, :].rearrange("p b s -> p (b s)")).then_inc(z["rrec"], 1)
                dve.wait_ge(z["rrec"], m + 1)
                dve.tensor_tensor(qkv[:, m, :], qkv[:, m, :], pp, ALU.mult).then_inc(z["qk"], 1)
            dve.wait_ge(z["dabc"], 4)
            dve.wait_ge(z["i2rep"], 1)
            flat = lambda a: a[:, :, :].rearrange("p a n -> p (a n)")
            dve.tensor_tensor_scan(flat(dt), ps[:, 0:2048], flat(i2rep), 0.0, ALU.mult, ALU.add).then_inc(z["scan"], 1)
            dve.wait_ge(z["scan"], 1)
            dve.wait_ge(z["dbbc"], 4)
            dve.tensor_tensor(flat(da), flat(dt), flat(i2rep), ALU.subtract).then_inc(z["scan"], 1)
            dve.wait_ge(z["scan"], 2)
            dve.tensor_tensor(flat(dts), flat(da), ps[:, 2048:4096], ALU.mult).then_inc(z["dts"], 1)
            dve.wait_ge(z["dts"], 1)
            dve.wait_ge(z["kk"], 1)
            dve.tensor_tensor(flat(lT), flat(dts), ps[:, 0:2048], ALU.mult).then_inc(z["lT"], 1)
            dve.wait_ge(z["kk"], 2)
            dve.tensor_tensor(flat(aT), flat(dt), ps[:, 2048:4096], ALU.mult).then_inc(z["aT"], 1)
            dve.wait_ge(z["lT"], 1)
            dve.wait_ge(z["initx"], 2)

            def mask_level(lv):
                dve.tensor_tensor(lm[:, :, :], lT[:, :, :], mt[:, bass.ds(lv, 1), :].to_broadcast([P, NB, S]),
                                  ALU.mult).then_inc(z["lm"], 1)
            octet = lambda a, g: a[:, 8 * g:8 * g + 8, :].rearrange("p a n -> p (a n)")
            mask_level(0)
            dve.wait_ge(z["lm"], 1)
            dve.tensor_tensor(flat(xT), flat(xT), flat(lm), ALU.subtract).then_inc(z["xt0"], 1)
            for g in range(4):
                dve.wait_ge(z["y"], g + 1)
                dve.tensor_tensor(octet(x_, g), octet(x_, g), bank[g], ALU.subtract).then_inc(z["xt"], 2)
            dve.wait_ge(z["xt0"], 1)
            mask_level(1)
            with dve.Fori(1, LEVELS - 1) as lv:
                dve.wait_ge(z["y"], 4 * lv + 4)
                mask_level(lv + 1)
                for g in range(4):
                    dve.wait_ge(z["zx"], 8 * lv + 2 * g - 7)
                    dve.tensor_tensor(octet(x_, g), octet(x_, g), bank[4 + g], ALU.subtract).then_inc(z["xt"], 1)
                    dve.wait_ge(z["zx"], 8 * lv + 2 * g - 6)
                    dve.tensor_tensor(octet(xT, g), octet(xT, g), bank[g], ALU.subtract).then_inc(z["xt"], 1)
            for g in range(4):
                dve.wait_ge(z["zx"], 8 * (LEVELS - 2) + g + 1)
                if g == 0:
                    dve.wait_ge(z["bdz"], 4)
                for b2 in range(2):
                    rows = slice(64 * b2, 64 * b2 + 64)
                    i = dve.tensor_tensor(xbd[g // 2][rows, 8 * (g % 2):8 * (g % 2) + 8, rows], xT[rows, 8 * g:8 * g + 8, :],
                                          bank[g][rows, :].rearrange("p (a n) -> p a n", n=S), ALU.subtract)
                i.then_inc(z["xt"], 1)
            for t in range(NT):
                dve.wait_ge(z["vt"], t + 1)
                dve.tensor_tensor(bv[:, t, :, :], bank[t].rearrange("p (h n) -> p h n", n=VD),
                                  beta[:, t, :].unsqueeze(2).to_broadcast([P, HG, VD]), ALU.mult).then_inc(z["bv"], 1)
            for t in range(NT):
                dve.wait_ge(z["osq"], t + 1)
                dve.reduce_sum(oss[:, 4 * t:4 * t + 4], bv[:, t, :, :], AXX).then_inc(z["oss"], 1)
            dve.wait_ge(z["osd"], 1)
            dve.reciprocal(ors[:, :], osd[:, :]).then_inc(z["ors"], 1)
            dve.wait_ge(z["ors"], 1)
            for t in range(NT):
                dve.tensor_tensor(de[:, t, :, :], bank[t].rearrange("p (h n) -> p h n", n=VD),
                                  ors[:, 4 * t:4 * t + 4].unsqueeze(2).to_broadcast([P, HG, VD]), ALU.mult).then_inc(z["on"], 1)
            for t in range(NT):
                dve.wait_ge(z["on"], t + 1)
                dve.wait_ge(z["gw"], t + 1)
                dve.tensor_tensor(bv[:, t, :, :], de[:, t, :, :], gw[:, t, :, :], ALU.mult).then_inc(z["og"], 1)
            for t in range(NT):
                dve.wait_ge(z["enc"], 2 * (t // 2) + 2)
                dve.tensor_tensor(x1[:, t, :], xl[:, t, :], bank[t // 2][:, (t % 2) * D:(t % 2 + 1) * D],
                                  ALU.add).then_inc(z["x1"], 1)
            dve.wait_ge(z["x1"], NT)
            ln_vector(dve, c, l2, x1, xn, w)
            for t in range(NT):
                dve.wait_ge(z["f2"], t // 2 + 1)
                dve.tensor_tensor(h[:, t, :], bank[4 + t // 2][:, (t % 2) * D:(t % 2 + 1) * D], c.row("e_w2b"),
                                  ALU.add).then_inc(z["b2"], 1)
            for t in range(NT):
                dve.wait_ge(z["gel"], t + 1)
                dve.wait_ge(z["xs"], t + 1)
                dve.tensor_tensor(c.x[:, t, :], c.x[:, t, :], xn[:, t, :], ALU.add).then_inc(z["xout"], 1)

        @block.tensor
        def _(pe):
            xt_tensor(pe, c, ln, h, bank, z["h"])
            pe.wait_ge(z["weights"], 80)
            for m in range(8):
                pe.wait_ge(ln.xt, 4)
                if m > 3:
                    pe.wait_ge(z["conv"], m - 3)
                at = 1024 * ((m + 2) % 4)
                for g in range(2):
                    for kk in range(KC):
                        i = pe.matmul(ps[:, at + 512 * g:at + 512 * g + 512], wqkv[:, kk, m * P:(m + 1) * P],
                                      ht[:, kk, 512 * g:512 * g + 512], start=(kk == 0), stop=(kk == KC - 1))
                i.then_inc(z["proj"], 1)
            pe.wait_ge(z["conv"], 5)
            for t in range(NT):
                for kk in range(KC):
                    i = pe.matmul(bank[4][:, 8 * t:8 * t + 8], ht[:, kk, t * P:(t + 1) * P], wab[:, kk, :],
                                  start=(kk == 0), stop=(kk == KC - 1))
            i.then_inc(z["ab"], 1)
            for t in range(NT):
                if t == 0:
                    pe.wait_ge(z["conv"], 8)
                if t > 3:
                    pe.wait_ge(z["gate"], t - 3)
                for kk in range(KC):
                    i = pe.matmul(bank[t % 4], ht[:, kk, t * P:(t + 1) * P], wg[:, kk, :], start=(kk == 0), stop=(kk == KC - 1))
                i.then_inc(z["proj"], 1)
            pe.wait_ge(z["consts"], 64)
            pe.wait_ge(z["gate"], NT)
            for m in range(4):
                pe.wait_ge(z["sq"], m + 1)
                if m > 1:
                    pe.wait_ge(z["qk"], m - 1)
                for g in range(2):
                    i = pe.matmul(bank[2 * (m % 2) + g], ones[:, :],
                                  cv[:, 0, 8 * g:8 * g + 8, :].rearrange("p b s -> p (b s)"), start=True, stop=True)
                i.then_inc(z["ss"], 1)
            pe.wait_ge(z["qk"], 4)
            pe.wait_ge(z["da"], 1)
            for g in range(4):
                pe.matmul(bank[g], ones[:, :], da[:, 8 * g:8 * g + 8, :].rearrange("p a n -> p (a n)"),
                          start=True, stop=True).then_inc(z["dabc"], 1)
            pe.wait_ge(z["db"], 1)
            pe.wait_ge(z["beta"], 1)
            pe.wait_ge(z["u"], 1)
            for g in range(4):
                pe.matmul(bank[4 + g], ones[:, :], dts[:, 8 * g:8 * g + 8, :].rearrange("p a n -> p (a n)"),
                          start=True, stop=True).then_inc(z["dbbc"], 1)
            for which in range(2):
                if which == 0:
                    pe.wait_ge(z["scan"], 1)
                else:
                    pe.wait_ge(z["dts"], 1)
                for t in range(NT):
                    for b2 in range(2):
                        for cc in range(2):
                            for r in range(2):
                                at = 2048 * which + S * blk(t, 2 * cc + r)
                                tok = t * P + b2 * S
                                kx = qkv[64 * r:64 * r + 64, 2 + cc, tok:tok + S]
                                rx = kx if which == 0 else qkv[64 * r:64 * r + 64, cc, tok:tok + S]
                                i = pe.matmul(ps[64 * b2:64 * b2 + 64, at:at + S], kx, rx, start=True, stop=True,
                                              tile_position=(64 * r, 64 * b2))
                i.then_inc(z["kk"], 1)

            def product(dst, lhs, rhs, g):
                for a in range(8 * g, 8 * g + 8):
                    for b2 in range(2):
                        r = slice(64 * b2, 64 * b2 + 64)
                        i = pe.matmul(dst[r, (a % 8) * S:(a % 8 + 1) * S], lhs[r, a, :], rhs[r, a, :], start=True,
                                      stop=True, tile_position=(64 * b2, 64 * b2))
                return i
            pe.wait_ge(z["lT"], 1)
            pe.wait_ge(z["aT"], 1)
            pe.wait_ge(z["initx"], 2)

            pe.wait_ge(z["lm"], 1)
            for g in range(4):
                product(bank[g], lm, x_, g).then_inc(z["y"], 1)
            pe.wait_ge(z["xt0"], 1)

            def level(lv, last):
                pe.wait_ge(z["lm"], lv + 1)
                for g in range(4):
                    pe.wait_ge(z["xt"], 8 * lv - 6 + 2 * g)
                    pe.nop(nofuse=True)
                    product(bank[g], lm, x_, g).then_inc(z["y"], 1)
                for g in range(4):
                    pe.wait_ge(z["yout"], 4 * lv + g - 3)
                    pe.nop(nofuse=True)
                    if not last:
                        product(bank[4 + g], xT, y, g).then_inc(z["zx"], 1)
                    product(bank[g], y, xT, g).then_inc(z["zx"], 1)
            with pe.Fori(1, LEVELS - 1) as lv:
                level(lv, False)
            level(LEVELS - 1, True)
            pe.wait_ge(z["xt"], 8 * (LEVELS - 1) + 4)
            for t in range(NT):
                for hh in range(HG):
                    i = pe.transpose(bank[t][:, hh * P:(hh + 1) * P], qkv[:, 4 + hh, t * P:(t + 1) * P], c.ident[:, :])
                i.then_inc(z["vt"], 1)

            def apply(mats, vec, ready, done):
                for t in range(NT):
                    pe.wait_ge(ready, t + 1)
                    for hh in range(HG):
                        i = pe.matmul(bank[t][:, hh * VD:(hh + 1) * VD], mats[hh % 2][:, 2 * t + hh // 2, :], vec[:, t, hh, :],
                                      start=True, stop=True)
                    i.then_inc(done, 1)
            apply(xbd, bv, z["bv"], z["dl"])
            pe.wait_ge(z["abd"], 4)
            apply(abd, de, z["de"], z["o"])
            for t in range(NT):
                pe.wait_ge(z["og"], t + 1)
                for hh in range(HG):
                    i = pe.transpose(bank[t][:, hh * P:(hh + 1) * P], bv[:, t, hh, :], c.ident[:, :])
                i.then_inc(z["ogt"], 1)
            for t in range(NT):
                pe.wait_ge(z["ogs"], max(t + 1, min(NT, t // 2 + 1)))
                for hh in range(HG):
                    i = pe.matmul(bank[t // 2][:, (t % 2) * D:(t % 2 + 1) * D], de[:, t, hh, :], wo[:, hh, :],
                                  start=(hh == 0), stop=(hh == HG - 1))
                i.then_inc(z["enc"], 1)
            pe.wait_ge(z["x1"], NT)
            xt_tensor(pe, c, l2, xn, bank, l2.xn)
            for t in range(NT):
                pe.wait_ge(l2.xt, 4)
                for kk in range(KC):
                    i = pe.matmul(bank[4 + t // 2][:, (t % 2) * D:(t % 2 + 1) * D], ht[:, kk, t * P:(t + 1) * P], w2[:, kk, :],
                                  start=(kk == 0), stop=(kk == KC - 1))
                if t % 2:
                    i.then_inc(z["f2"], 1)


def stage_f(nc, c):
    with stage_semaphores(nc) as ctx:
        sb, sem, sems, bank = stage_kit(nc, ctx, "f")
        FC = F // P
        slots_x, slots_y = c.slots_x, c.slots_y
        zero = sb("zero", [P, D])
        xn = sb("xn", [P, NT, D])
        xt = sb("xt", [P, KC, N])
        w1 = sb("w1", [P, E, KC, F])
        w2 = sb("w2", [P, E, FC, D])
        wr = sb("wr", [P, KC, E])
        before = sb("before", [P, P])
        ones = sb("ones", [P, P])
        tab = sb("tab", [P, E + E * NT + E * E])
        iota = tab[:, 0:E]
        over = tab[:, E:E + E * NT].rearrange("p (e k) -> p e k", e=E)
        prior = tab[:, E + E * NT:].rearrange("p (e f) -> p e f", e=E)
        lg, sh, ex, eq, cand, hot, posm, posh = (sb(n, [P, NT, E]) for n in "lg sh ex eq cand hot posm posh".split())
        mx, se, rse, ix, pos = (sb(n, [P, NT]) for n in "mx se rse ix pos".split())
        run = sb("run", [P, NT + 1, E])
        cmp_ = sb("cmp", [P, E, NT])
        more, cnt, first = (sb(n, [P, E]) for n in "more cnt first".split())
        pri = sb("pri", [P, E, E])
        posi = sb("posi", [P, NT], U32)
        ends = sb("ends", [1, E + 1], mybir.dt.int32)
        xs = sb("xs", [P, D])
        xts = sb("xts", [P, 2, KC, P])
        hb = sb("hb", [P, FC, P])
        yb = sb("yb", [P, D])
        yg = sb("yg", [P, NT, D])
        s = ln_sems(sem, "ln")
        z = sems("small zero logits lg mx sh ex se rse eq cand ix hot rank tot run cmp more cnt pri first posa "
                 "posb posh pos posi ends scattered xs xst xts hid act ypr yb stored gathered xout")
        s_w = [sem(f"w{e}") for e in range(E)]
        block = ctx.enter_context(nc.Block())

        def tiles(eng, body):
            eng.wait_ge(z["ends"], 2)
            at = 0
            for e in range(E):
                end = eng.value_load(ends[0:1, e:e + 1], min_val=e + 1, max_val=MAXT)
                with eng.Fori(at, end) as i:
                    body(e, i)
                at = end
            return at

        @block.sync
        def _(sp):
            sp.dma_start(wr[:, :, :], c.d["f_wr"].rearrange("(k p) n -> p k n", p=P)).then_inc(z["small"], 16)
            sp.dma_start(before[:, :], c.d["before"]).then_inc(z["small"], 16)
            sp.dma_start(ones[:, :], c.d["ones"]).then_inc(z["small"], 16)
            sp.dma_start(tab[:, :], c.d["f_tab"]).then_inc(z["small"], 16)

            for e in range(E):
                if e > 1:
                    sp.wait_ge(s_w[e - 2], 32)
                if e == 3:
                    sp.wait_ge(z["scattered"], 16 * NT)
                sp.dma_start(w1[:, e, :, :], c.d["f_w1"][e, :, :].rearrange("(k p) n -> p k n", p=P)).then_inc(s_w[e], 16)
                sp.dma_start(w2[:, e, :, :], c.d["f_w2"][e, :, :].rearrange("(k p) n -> p k n", p=P)).then_inc(s_w[e], 16)

        @block.gpsimd
        def _(pool):
            pool.memset(zero[:, :], 0.0).then_inc(z["zero"], 1)
            pool.wait_ge(z["zero"], 1)
            pool.dma_start(slots_x[MAXT * P:(MAXT + 1) * P, :], zero[:, :]).then_inc(z["stored"], 16)
            pool.wait_ge(z["stored"], 16)
            pool.wait_ge(z["posi"], 1)
            for t in range(NT):
                pool.indirect_dma_start(slots_x, bass.IndirectOffsetOnAxis(ap=posi[:, t:t + 1], axis=0),
                                        xn[:, t, :], None).then_inc(z["scattered"], 16)

            def store(e, i):
                pool.wait_ge(z["yb"], i + 2)
                pool.nop(nofuse=True)
                pool.dma_start(slots_y[bass.ds(i * P, P), :], yb[:, :]).then_inc(z["stored"], 16)
            end = tiles(pool, store)
            pool.wait_ge(z["stored"], end * 16 + 16)
            pool.nop(nofuse=True)
            for t in range(NT):
                pool.indirect_dma_start(yg[:, t, :], None, slots_y,
                                        bass.IndirectOffsetOnAxis(ap=posi[:, t:t + 1], axis=0)).then_inc(z["gathered"], 16)

        @block.scalar
        def _(act):
            ln_scalar(act, s, c.w)
            xt_scalar(act, s, bank, xt)
            act.wait_ge(z["sh"], NT)
            act.activation(ex[:, :, :], sh[:, :, :], ACT.Exp).then_inc(z["ex"], 1)
            act.sem_inc(z["act"], 4)

            act.wait_ge(z["scattered"], 16 * NT)
            act.dma_start(xs[:, :], slots_x[0:P, :]).then_inc(z["xs"], 16)

            def hidden(e, i):
                act.wait_ge(z["xst"], i + 1)
                act.nop(nofuse=True)
                act.dma_start(xs[:, :], slots_x[bass.ds(i * P + P, P), :]).then_inc(z["xs"], 16)
                for m in range(FC):
                    act.wait_ge(z["hid"], i * FC + (m + 1))
                    act.activation(hb[:, m, :], bank[m % 4][:, 0:P], ACT.Gelu, bias=c.col("f_b1", e * FC + m)
                                   ).then_inc(z["act"], 1)
            end = tiles(act, hidden)
            act.wait_ge(z["xs"], end * 16 + 16)
            act.nop(nofuse=True)

        @block.vector
        def _(dve):
            ln_vector(dve, c, s, c.x, xn, c.w)
            dve.wait_ge(z["logits"], 1)
            dve.tensor_tensor(lg[:, :, :], bank[4][:, 0:64].rearrange("p (t n) -> p t n", n=E),
                              c.row("f_br").unsqueeze(1).to_broadcast([P, NT, E]), ALU.add).then_inc(z["lg"], 1)
            dve.wait_ge(z["lg"], 1)
            dve.reduce_max(mx[:, :], lg[:, :, :], AXX).then_inc(z["mx"], 1)
            dve.wait_ge(z["mx"], 1)
            for t in range(NT):
                dve.tensor_scalar(sh[:, t, :], lg[:, t, :], mx[:, t:t + 1], None, ALU.subtract).then_inc(z["sh"], 1)
            dve.wait_ge(z["sh"], NT)
            dve.tensor_scalar(eq[:, :, :], sh[:, :, :], 0.0, -float(E), ALU.is_ge, ALU.mult).then_inc(z["eq"], 1)
            dve.wait_ge(z["eq"], 1)
            dve.wait_ge(z["small"], 64)
            dve.tensor_tensor(cand[:, :, :], eq[:, :, :], iota.unsqueeze(1).to_broadcast([P, NT, E]), ALU.add
                              ).then_inc(z["cand"], 1)
            dve.wait_ge(z["cand"], 1)
            dve.tensor_reduce(ix[:, :], cand[:, :, :], AXX, ALU.min).then_inc(z["ix"], 1)
            dve.wait_ge(z["ix"], 1)
            dve.tensor_tensor(hot[:, :, :], cand[:, :, :], ix[:, :].unsqueeze(2).to_broadcast([P, NT, E]),
                              ALU.is_equal).then_inc(z["hot"], 1)
            dve.memset(run[:, 0, :], 0.0).then_inc(z["run"], 1)
            dve.wait_ge(z["tot"], 1)
            for t in range(NT):
                dve.wait_ge(z["run"], t + 1)
                dve.tensor_tensor(run[:, t + 1, :], run[:, t, :], bank[5][:, E * t:E * t + E], ALU.add).then_inc(z["run"], 1)
            dve.wait_ge(z["run"], NT + 1)
            dve.tensor_tensor(cmp_[:, :, :], run[:, NT, :].unsqueeze(2).to_broadcast([P, E, NT]), over,
                              ALU.is_gt).then_inc(z["cmp"], 1)
            dve.tensor_tensor(posm[:, :, :], run[:, 0:NT, :], bank[4][:, 64:128].rearrange("p (t n) -> p t n", n=E),
                              ALU.add).then_inc(z["posa"], 1)
            dve.wait_ge(z["cmp"], 1)
            dve.reduce_sum(more[:, :], cmp_[:, :, :], AXX).then_inc(z["more"], 1)
            dve.wait_ge(z["more"], 1)
            dve.tensor_scalar(cnt[:, :], more[:, :], 1.0, None, ALU.add).then_inc(z["cnt"], 1)
            dve.wait_ge(z["cnt"], 1)
            dve.tensor_tensor(pri[:, :, :], cnt[:, :].unsqueeze(1).to_broadcast([P, E, E]), prior, ALU.mult).then_inc(z["pri"], 1)
            dve.wait_ge(z["pri"], 1)
            dve.reduce_sum(first[:, :], pri[:, :, :], AXX).then_inc(z["first"], 1)
            dve.wait_ge(z["first"], 1)
            dve.wait_ge(z["posa"], 1)
            dve.scalar_tensor_tensor(posm[:, :, :], first[:, :].unsqueeze(1).to_broadcast([P, NT, E]), float(P),
                                     posm[:, :, :], ALU.mult, ALU.add).then_inc(z["posb"], 1)
            dve.wait_ge(z["posb"], 1)
            dve.tensor_tensor(posh[:, :, :], posm[:, :, :], hot[:, :, :], ALU.mult).then_inc(z["posh"], 1)
            dve.wait_ge(z["posh"], 1)
            dve.reduce_sum(pos[:, :], posh[:, :, :], AXX).then_inc(z["pos"], 1)
            dve.wait_ge(z["pos"], 1)
            dve.tensor_copy(posi[:, :], pos[:, :]).then_inc(z["posi"], 1)
            dve.tensor_tensor(ends[:, 0:E], first[0:1, :], cnt[0:1, :], ALU.add).then_inc(z["ends"], 1)
            dve.memset(ends[:, E:E + 1], 0).then_inc(z["ends"], 1)
            dve.wait_ge(z["ex"], 1)
            dve.reduce_sum(se[:, :], ex[:, :, :], AXX).then_inc(z["se"], 1)
            dve.wait_ge(z["se"], 1)
            dve.reciprocal(rse[:, :], se[:, :]).then_inc(z["rse"], 1)

            def turned(i, slot):
                dve.wait_ge(z["xst"], i + 1)
                dve.tensor_copy(xts[:, slot, :, :].rearrange("p k n -> p (k n)"), bank[4][:, 0:D]).then_inc(z["xts"], 1)
            dve.wait_ge(z["xst"], 1)
            dve.tensor_copy(xts[:, 0, :, :].rearrange("p k n -> p (k n)"), bank[4][:, 0:D]).then_inc(z["xts"], 1)
            dve.sem_inc(z["yb"], 1)

            def out_(e, i):
                dve.wait_ge(z["xst"], i + 2)
                dve.tensor_scalar(xts[:, bass.ds((i + 1) % 2, 1), :, :].rearrange("p b k n -> p (b k n)"), bank[4][:, 0:D],
                                  1.0, None, ALU.mult).then_inc(z["xts"], 1)
                dve.wait_ge(z["ypr"], i + 1)
                dve.wait_ge(z["stored"], i * 16 + 16)
                dve.tensor_tensor(yb[:, :], bank[5][:, 0:D], c.row("f_b2", e * D, D), ALU.add).then_inc(z["yb"], 1)
            tiles(dve, out_)
            dve.wait_ge(z["rse"], 1)
            dve.wait_ge(z["gathered"], 16 * NT)
            for t in range(NT):
                dve.scalar_tensor_tensor(c.x[:, t, :], yg[:, t, :], rse[:, t:t + 1], c.x[:, t, :], ALU.mult,
                                         ALU.add).then_inc(z["xout"], 1)

        @block.tensor
        def _(pe):
            xt_tensor(pe, c, s, xn, bank, s.xn)
            pe.wait_ge(z["small"], 64)
            for t in range(NT):
                pe.wait_ge(s.xt, 2 * (t // 4) + 2)
                for kk in range(KC):
                    m = pe.matmul(bank[4][:, E * t:E * t + E], xt[:, kk, t * P:(t + 1) * P], wr[:, kk, :],
                                  start=(kk == 0), stop=(kk == KC - 1))
            m.then_inc(z["logits"], 1)
            pe.wait_ge(z["lg"], 1)
            pe.wait_ge(z["hot"], 1)
            hv = hot[:, :, :].rearrange("p t e -> p (t e)")
            pe.matmul(bank[4][:, 64:128], before[:, :], hv, start=True, stop=True)
            pe.matmul(bank[5][:, 0:64], ones[:, :], hv, start=True, stop=True).then_inc(z["tot"], 1)
            pe.wait_ge(z["posa"], 1)

            def turn():
                for k in range(KC):
                    m = pe.transpose(bank[4][:, k * P:(k + 1) * P], xs[:, k * P:(k + 1) * P], c.ident[:, :])
                m.then_inc(z["xst"], 1)
            pe.wait_ge(z["xs"], 16)
            turn()
            seen = [0]

            def tile(e, i):
                pe.wait_ge(z["xts"], i + 1)
                for m in range(FC):
                    pe.wait_ge(z["act"], i * FC + (m + 1))
                    for kk in range(KC):
                        j = pe.matmul(bank[m % 4][:, 0:P], w1[:, e, kk, m * P:(m + 1) * P],
                                      xts[:, bass.ds(i % 2, 1), kk, :].rearrange("p b n -> p (b n)"),
                                      start=(kk == 0), stop=(kk == KC - 1))
                    j.then_inc(z["hid"], 1)
                    if m == 3:
                        pe.wait_ge(z["xs"], i * 16 + 32)
                        turn()
                pe.wait_ge(z["yb"], i + 1)
                for m in range(FC):
                    pe.wait_ge(z["act"], i * FC + (m + 5))
                    j = pe.matmul(bank[5][:, 0:D], hb[:, m, :], w2[:, e, m, :], start=(m == 0), stop=(m == FC - 1))
                j.then_inc(z["ypr"], 1)

            def body(e, i):
                pe.wait_ge(s_w[e], 32)
                tile(e, i)
            tiles(pe, body)


def build(nc, d, out):
    ctx = ExitStack()
    with ctx:
        c = Names()
        c.d = d
        c.slots_x = nc.dram_tensor("slots_x", ((MAXT + 1) * P, D), F32, kind="Internal").ap()
        c.slots_y = nc.dram_tensor("slots_y", (MAXT * P, D), F32, kind="Internal").ap()

        def sb(name, shape, dt=F32):
            return ctx.enter_context(nc.sbuf_tensor(name, shape, dt))
        c.x = sb("x", [P, NT, D])
        c.ident = sb("ident", [P, P])
        c.identb = sb("identb", [P, P], BF16)
        c.eo = sb("evenodd", [P, 2])
        c.cols = sb("cols", [P, NCOLS])
        c.rows = sb("rows", [P, NROWS])
        c.w = Names()
        c.w.st = sb("ln_st", [P, NT, 6])
        c.w.mv = sb("ln_mv", [P, NT, 2])
        c.w.ve = sb("ln_ve", [P, NT])
        c.w.sd = sb("ln_sd", [P, NT])
        c.w.rs = sb("ln_rs", [P, NT])
        c.col = lambda n, i: c.cols[:, COLS[n][0] + i:COLS[n][0] + i + 1]
        c.row = lambda n, i=0, m=None: c.rows[:, ROWS[n][0] + i:ROWS[n][0] + i + (m or ROWS[n][1])]
        with ExitStack() as held:
            c.b_weights = [held.enter_context(nc.sbuf_tensor(f"b_{n}", [P, k, m], F32)) for n, k, m in (
                ("wq", KC, QKV), ("wk", KC, QKV), ("wv", KC, QKV), ("wo", QKV // P, D))]
            stage_a(nc, c)
            stage_b(nc, c)
        stage_c(nc, c)
        stage_d(nc, c)
        stage_e(nc, c)
        stage_f(nc, c)
        finish(nc, c, out)


def finish(nc, c, out):
    with nc.semaphore("stored") as stored, nc.Block() as block:
        @block.sync
        def _(sp):
            sp.dma_start(out.rearrange("(t p) d -> p t d", p=P), c.x[:, :, :]).then_inc(stored, 16)
            sp.wait_ge(stored, 16)


def kernel(**inputs):
    import numpy as _np
    import concourse.bacc as _bacc
    import ml_dtypes as _ml
    from concourse import mybir as _mybir
    from concourse.bass_utils import run_bass_kernel_spmd as _run

    a = {k: _np.asarray(v) for k, v in inputs.items()}
    col = lambda v: v.reshape(-1, P).T
    mask = _np.ascontiguousarray(a["mask_1x1xSxS2_bk0"][0, 0]).view(_np.uint32)
    cw = _np.concatenate([a["L1_attn_conv_q_w"], a["L1_attn_conv_k_w"], a["L1_attn_conv_v_w"]])
    cols = _np.concatenate(
        [col(a["L0_xattn_bq"]), col(a["L0_xattn_bk"]), col(a["L0_xattn_bv"])]
        + [_np.concatenate([a[n]] * 2).reshape(P, 1) for n in ("L0_attn_q_gamma", "L0_attn_q_beta", "L0_attn_k_gamma",
                                                               "L0_attn_k_beta")]
        + [col(a["L1_xattn_bq"]), col(a["L1_xattn_bk"]), col(a["L1_xattn_bv"]), col(a["L1_attn_ln2_g"]),
           col(a["L1_attn_ln2_b"]), cw.reshape(8, P, 4).transpose(1, 0, 2).reshape(P, 32),
           a["L1_ffn_b1"].reshape(64, P).T], axis=1)
    rows = _np.concatenate([a[n].ravel() for n in (
        "L0_xattn_bo", "L0_ffn_scale", "L0_ffn_bias", "L1_xattn_bo", "L1_attn_ln1_g", "L1_attn_ln1_b",
        "L1_attn_rms_in_w", "L1_attn_b2", "L1_attn_o_norm_w", "L1_attn_dt_bias", "L1_attn_A_log", "L1_ffn_b2",
        "L1_ffn_br")])
    part = _np.arange(P)
    NR = SK // KR
    eye = _np.eye(P, dtype=_np.float32)
    even = (part // HD % 2 == 0)
    i2 = _np.tile(_np.eye(S, dtype=_np.float32), (2, 1))
    s_, t_ = _np.arange(S)[:, None], _np.arange(S)[None, :]
    levels = [(s_ // (2 * n) == t_ // (2 * n)) & (s_ // n % 2 == 0) & (t_ // n % 2 == 1) for n in (1, 2, 4, 8, 16, 32)]
    tab = _np.concatenate([_np.arange(E), _np.tile(P * _np.append(_np.arange(1, NT), N), E),
                           _np.tril(_np.ones((E, E)), -1).ravel()])
    arrays = {
        "x": a["x"].reshape(N, D),
        "ctxt": a["ctx_1024"].transpose(0, 2, 1),
        "mask2": _np.concatenate([mask, mask]),
        "cols": cols, "rows": rows,
        "ident": eye, "identb": eye.astype(_ml.bfloat16),
        "rounds": _np.concatenate([_np.arange(NR) + 2 * NR, _np.arange(NR)])[None].astype(_np.float32),
        "evenodd": _np.stack([even, ~even], 1).astype(_np.float32),
        "a_wq": a["L0_xattn_Wq"], "a_wk": a["L0_xattn_Wk"], "a_wv": a["L0_xattn_Wv"], "a_wo": a["L0_xattn_Wo"],
        "b_wq": a["L0_attn_Wq"].T, "b_wk": a["L0_attn_Wk"].T, "b_wv": a["L0_attn_Wv"].T, "b_wo": a["L0_attn_Wo"].T,
        "causal": _np.kron(_np.eye(2), _np.triu(_np.ones((S, S)))).astype(_np.float32),
        "c_w": a["L0_ffn_weights"].T,
        "d_wq": a["L1_xattn_Wq"].T, "d_wk": a["L1_xattn_Wk"].T, "d_wv": a["L1_xattn_Wv"].T, "d_wo": a["L1_xattn_Wo"].T,
        "d_masks": _np.concatenate([part[:, None] // HD == _np.arange(P // HD),
                                    part[:, None] // S == _np.arange(2)], axis=1).astype(_np.float32),
        "causalb": _np.tile(_np.triu(_np.full((S, S), -1e30), 1), (2, 1)).astype(_ml.bfloat16),
        "e_wqkv": _np.concatenate([a["L1_attn_Wq"], a["L1_attn_Wk"], a["L1_attn_Wv"]], axis=1),
        "e_wg": a["L1_attn_Wg"], "e_wab": _np.concatenate([a["L1_attn_Wa"], a["L1_attn_Wb"]], axis=1),
        "e_wo": a["L1_attn_Wo"], "e_w2": a["L1_attn_W2"],
        "i2": i2, "i2z": i2 * (_np.arange(S) > 0).astype(_np.float32),
        "ones64": _np.kron(_np.eye(2), _np.ones((S, S))).astype(_np.float32),
        "levels": _np.tile(_np.stack(levels, 1), (2, 1, 1)).astype(_np.float32),
        "f_w1": a["L1_ffn_W1"], "f_w2": a["L1_ffn_W2"], "f_wr": a["L1_ffn_Wr"],
        "before": _np.triu(_np.ones((P, P)), 1).astype(_np.float32), "ones": _np.ones((P, P), _np.float32),
        "f_tab": _np.tile(tab.astype(_np.float32), (P, 1)),
    }
    nc = _bacc.Bacc("TRN2", target_bir_lowering=False, num_devices=1)
    ins, d = {}, {}
    for name, v in arrays.items():
        v = _np.ascontiguousarray(v)
        ins["in_" + name] = v
        d[name] = nc.dram_tensor("in_" + name, v.shape, _mybir.dt.from_np(v.dtype), kind="ExternalInput").ap()
    out = nc.dram_tensor("out_0_dram", (N, D), _mybir.dt.float32, kind="ExternalOutput").ap()
    build(nc, d, out)
    r = _run(nc, [ins], core_ids=[0])
    return _np.asarray(r.results[0]["out_0_dram"]).reshape(B, S, D)
```
